# Optimizing a Trainium2 kernel written in Bass

```python
import numpy as np
import jax
import jax.numpy as jnp

def _softmax(x, axis=-1):
    return jax.nn.softmax(x, axis=axis)

def _gelu(x):
    return jax.nn.gelu(x, approximate=True)

def _silu(x):
    return jax.nn.silu(x)

def _sigmoid(x):
    return jax.nn.sigmoid(x)

def _layernorm(x, axis=-1, eps=1e-05):
    m = jnp.mean(x, axis=axis, keepdims=True)
    v = jnp.var(x, axis=axis, keepdims=True)
    return (x - m) / jnp.sqrt(v + eps)

def _scatter_add(tgt, idx, src, axis=0):
    return tgt.at[idx].add(src)

def _segment_sum(src, seg, n):
    return jax.ops.segment_sum(src, seg, n)
kernel_name = 'mk_flamingo_gated_d2_seqx_r4_9e2513'

def setup_inputs(seed: int=0):
    np.random.seed(seed)
    _w = jnp.asarray

    def _rec_inputs():
        import jax
        import jax.numpy as jnp
        _rk = jax.random.key(seed)
        x = -0.0002928 + 1 * jax.random.normal(jax.random.fold_in(_rk, 1), (8, 256, 256), jnp.float32)
        _lenS = 256 - jax.random.randint(jax.random.fold_in(_rk, 7), (8,), 0, max(1, 256 // 4) + 1, jnp.int32)
        _lenS2 = 120 - jax.random.randint(jax.random.fold_in(_rk, 8), (8,), 0, max(1, 120 // 4) + 1, jnp.int32)
        _ctx_1024P = jax.random.normal(jax.random.fold_in(_rk, 11), (8, 16, 256), jnp.float32)
        _ctx_1024c = jax.random.dirichlet(jax.random.fold_in(_rk, 511), 0.3 * jnp.ones((16,), jnp.float32), (8, 120))
        _ctx_1024t = jnp.einsum('bsk,bkd->bsd', _ctx_1024c, _ctx_1024P)
        _ctx_1024t = _ctx_1024t * jax.lax.rsqrt(jnp.mean(jnp.square(_ctx_1024t)) + 1e-12) * 0.953939
        ctx_1024 = -1.39393e-06 + 0.999914 * (_ctx_1024t + 0.3 * jax.random.normal(jax.random.fold_in(_rk, 611), (8, 120, 256), jnp.float32))
        _validS = jnp.arange(256)[None, :] < _lenS[:, None]
        _validS2 = jnp.arange(120)[None, :] < _lenS2[:, None]
        _causal = jnp.tril(jnp.ones((256, 256), dtype=bool))
        mask_SxS2_fk0 = jnp.where(jnp.broadcast_to(_validS2[0:1, :], (256, 120)), -1000000000.0, 0.0).astype(jnp.float32)
        _g = jax.random.normal(jax.random.fold_in(_rk, 9001), (2, 2), jnp.float32)
        _g = jnp.sign(_g) * jnp.maximum(jnp.abs(_g), 1.0) + (_g == 0) * 1.0
        g_xattn = _g[0]
        g_ffn = _g[1]
        return (x, ctx_1024, mask_SxS2_fk0, g_xattn, g_ffn)
    x, ctx_1024, mask_SxS2_fk0, g_xattn, g_ffn = _rec_inputs()

    def _L0_xattn_setup():
        import jax, jax.numpy as jnp
        import numpy as np
        B, S, D, H = (2, 512, 256, 16)
        A = D // H
        NEG = -1000000000.0
        key = jax.random.key(seed)
        ks = jax.random.split(key, 5)
        std = 1.0 / np.sqrt(D)
        query = jax.random.normal(ks[0], (B, S, D), dtype=jnp.float32)
        context = jax.random.normal(ks[1], (B, S, D), dtype=jnp.float32)
        Wq = jax.random.normal(ks[2], (D, D), dtype=jnp.float32) * std
        Wkv = jax.random.normal(ks[3], (2 * D, D), dtype=jnp.float32) * std
        Wout = jax.random.normal(ks[4], (D, D), dtype=jnp.float32) * std
        mask = jnp.where(jnp.tril(jnp.ones((S, S), dtype=bool)), 0.0, NEG).astype(jnp.float32)
        return {'query': query, 'context': context, 'Wq': Wq, 'Wkv': Wkv, 'Wout': Wout, 'mask': mask}
    _L0_xattn_all = _L0_xattn_setup()
    _L0_xattn_in = {k: v for k, v in _L0_xattn_all.items() if k in ('Wq', 'Wkv', 'Wout')}
    del _L0_xattn_all

    def _L0_ffn_setup():
        import jax, jax.numpy as jnp
        import numpy as np
        BITS = 8
        LORA_RANK = 16
        LORA_ALPHA = 32
        SCALING = LORA_ALPHA / LORA_RANK

        def fake_quant_weight(w, bits=BITS):
            qmax = 2.0 ** (bits - 1) - 1
            scale = jnp.max(jnp.abs(w)) / qmax
            wq = jnp.clip(jnp.round(w / scale), -qmax - 1, qmax) * scale
            return w + jax.lax.stop_gradient(wq - w)

        def qat_lora_linear(x, W, b, A, B):
            Wq = fake_quant_weight(W)
            base = jnp.einsum('bsi,oi->bso', x, Wq) + b
            lora = jnp.einsum('bsr,or->bso', jnp.einsum('bsi,ri->bsr', x, A), B)
            return base + SCALING * lora
        key = jax.random.key(seed)
        ks = jax.random.split(key, 9)
        d, f = (256, 1024)
        s_in = 1.0 / np.sqrt(d)
        s_ff = 1.0 / np.sqrt(f)
        return {'hidden_states': jax.random.normal(ks[0], (4, 512, d), jnp.float32), 'W_fc': jax.random.normal(ks[1], (f, d), jnp.float32) * s_in, 'b_fc': jnp.zeros((f,), jnp.float32), 'A_fc': jax.random.normal(ks[2], (LORA_RANK, d), jnp.float32) * s_in, 'B_fc': jnp.zeros((f, LORA_RANK), jnp.float32), 'W_proj': jax.random.normal(ks[3], (d, f), jnp.float32) * s_ff, 'b_proj': jnp.zeros((d,), jnp.float32), 'A_proj': jax.random.normal(ks[4], (LORA_RANK, f), jnp.float32) * s_ff, 'B_proj': jnp.zeros((d, LORA_RANK), jnp.float32)}
    _L0_ffn_all = _L0_ffn_setup()
    _L0_ffn_in = {k: v for k, v in _L0_ffn_all.items() if k in ('W_fc', 'b_fc', 'A_fc', 'B_fc', 'W_proj', 'b_proj', 'A_proj', 'B_proj')}
    del _L0_ffn_all

    def _L1_xattn_setup():
        import jax, jax.numpy as jnp
        import numpy as np
        EMBED_DIM = 256
        B, QL, KL = (4, 512, 512)
        key = jax.random.key(seed)
        k1, k2, k3, k4 = jax.random.split(key, 4)
        hidden_states = jax.random.normal(k1, (B, QL, EMBED_DIM), dtype=jnp.float32)
        decoder_hidden_states = jax.random.normal(k2, (B, KL, EMBED_DIM), dtype=jnp.float32)
        Wq = jax.random.normal(k3, (EMBED_DIM, EMBED_DIM), dtype=jnp.float32) * (1.0 / np.sqrt(EMBED_DIM))
        Wkv = jax.random.normal(k4, (EMBED_DIM, 2 * EMBED_DIM), dtype=jnp.float32) * (1.0 / np.sqrt(EMBED_DIM))
        return {'hidden_states': hidden_states, 'decoder_hidden_states': decoder_hidden_states, 'Wq': Wq, 'Wkv': Wkv}
    _L1_xattn_all = _L1_xattn_setup()
    _L1_xattn_in = {k: v for k, v in _L1_xattn_all.items() if k in ('Wq', 'Wkv')}
    del _L1_xattn_all

    def _L1_ffn_setup():
        import jax, jax.numpy as jnp
        import numpy as np
        B, N, D, E, DFF = (4, 512, 256, 16, 1024)
        CAPACITY_FACTOR = 2.0
        CAP = int(N * CAPACITY_FACTOR / E)
        SINKHORN_ITERS = 6

        def _sinkhorn(logits, n_iters=SINKHORN_ITERS, tau=1.0):
            t = logits / tau
            for _ in range(n_iters):
                t = t - jax.scipy.special.logsumexp(t, axis=-2, keepdims=True)
                t = t - jax.scipy.special.logsumexp(t, axis=-1, keepdims=True)
            return jnp.exp(t)
        key = jax.random.key(seed)
        ks = jax.random.split(key, 6)
        scaled = lambda k, sh, fan: (jax.random.normal(k, sh, jnp.float32) / np.sqrt(fan)).astype(jnp.float32)
        return {'x': jax.random.normal(ks[0], (B, N, D), jnp.float32), 'gate_query': scaled(ks[1], (E, D), D), 'log_temp': jnp.asarray(np.log(0.5), jnp.float32), 'w1': scaled(ks[2], (E, D, DFF), D), 'b1': jnp.zeros((E, DFF), jnp.float32), 'w2': scaled(ks[3], (E, DFF, D), DFF), 'b2': jnp.zeros((E, D), jnp.float32)}
    _L1_ffn_all = _L1_ffn_setup()
    _L1_ffn_in = {k: v for k, v in _L1_ffn_all.items() if k in ('gate_query', 'log_temp', 'w1', 'b1', 'w2', 'b2')}
    del _L1_ffn_all
    return {'x': x, 'ctx_1024': ctx_1024, 'mask_SxS2_fk0': mask_SxS2_fk0, 'g_xattn': g_xattn, 'g_ffn': g_ffn, 'L0_xattn_Wq': _L0_xattn_in['Wq'], 'L0_xattn_Wkv': _L0_xattn_in['Wkv'], 'L0_xattn_Wout': _L0_xattn_in['Wout'], 'L0_ffn_W_fc': _L0_ffn_in['W_fc'], 'L0_ffn_b_fc': _L0_ffn_in['b_fc'], 'L0_ffn_A_fc': _L0_ffn_in['A_fc'], 'L0_ffn_B_fc': _L0_ffn_in['B_fc'], 'L0_ffn_W_proj': _L0_ffn_in['W_proj'], 'L0_ffn_b_proj': _L0_ffn_in['b_proj'], 'L0_ffn_A_proj': _L0_ffn_in['A_proj'], 'L0_ffn_B_proj': _L0_ffn_in['B_proj'], 'L1_xattn_Wq': _L1_xattn_in['Wq'], 'L1_xattn_Wkv': _L1_xattn_in['Wkv'], 'L1_ffn_gate_query': _L1_ffn_in['gate_query'], 'L1_ffn_log_temp': _L1_ffn_in['log_temp'], 'L1_ffn_w1': _L1_ffn_in['w1'], 'L1_ffn_b1': _L1_ffn_in['b1'], 'L1_ffn_w2': _L1_ffn_in['w2'], 'L1_ffn_b2': _L1_ffn_in['b2']}

def reference(x, ctx_1024, mask_SxS2_fk0, g_xattn, g_ffn, L0_xattn_Wq, L0_xattn_Wkv, L0_xattn_Wout, L0_ffn_W_fc, L0_ffn_b_fc, L0_ffn_A_fc, L0_ffn_B_fc, L0_ffn_W_proj, L0_ffn_b_proj, L0_ffn_A_proj, L0_ffn_B_proj, L1_xattn_Wq, L1_xattn_Wkv, L1_ffn_gate_query, L1_ffn_log_temp, L1_ffn_w1, L1_ffn_b1, L1_ffn_w2, L1_ffn_b2):
    import jax
    import jax.numpy as jnp

    def _L0_xattn_ref(query, context, Wq, Wkv, Wout, mask):
        import jax, jax.numpy as jnp
        import numpy as np
        B, S, D, H = (2, 512, 256, 16)
        A = D // H
        NEG = -1000000000.0
        b, q_len, d = query.shape
        c_len = context.shape[1]
        h, a = (H, A)
        scale = 1.0 / np.sqrt(d)
        q = query @ Wq.T
        kv = context @ Wkv.T
        k, v = jnp.split(kv, 2, axis=-1)
        q = q.reshape(b, q_len, h, a)
        k = k.reshape(b, c_len, h, a)
        v = v.reshape(b, c_len, h, a)
        scores = jnp.einsum('bqha,bkha->bqkh', q, k)
        scores = scores + mask[None, :, :, None]
        attn = jax.nn.softmax(scores * scale, axis=2)
        out = jnp.einsum('bqkh,bkha->bqha', attn, v).reshape(b, q_len, d)
        return out @ Wout.T

    def _L0_ffn_ref(hidden_states, W_fc, b_fc, A_fc, B_fc, W_proj, b_proj, A_proj, B_proj):
        import jax, jax.numpy as jnp
        import numpy as np
        BITS = 8
        LORA_RANK = 16
        LORA_ALPHA = 32
        SCALING = LORA_ALPHA / LORA_RANK

        def fake_quant_weight(w, bits=BITS):
            qmax = 2.0 ** (bits - 1) - 1
            scale = jnp.max(jnp.abs(w)) / qmax
            wq = jnp.clip(jnp.round(w / scale), -qmax - 1, qmax) * scale
            return w + jax.lax.stop_gradient(wq - w)

        def qat_lora_linear(x, W, b, A, B):
            Wq = fake_quant_weight(W)
            base = jnp.einsum('bsi,oi->bso', x, Wq) + b
            lora = jnp.einsum('bsr,or->bso', jnp.einsum('bsi,ri->bsr', x, A), B)
            return base + SCALING * lora
        h = qat_lora_linear(hidden_states, W_fc, b_fc, A_fc, B_fc)
        h = jax.nn.gelu(h, approximate=False)
        h = qat_lora_linear(h, W_proj, b_proj, A_proj, B_proj)
        return h

    def _L1_xattn_ref(hidden_states, decoder_hidden_states, Wq, Wkv):
        import jax, jax.numpy as jnp
        import numpy as np
        EMBED_DIM = 256
        B, QL, KL = (4, 512, 512)
        d = Wq.shape[0]
        scale = 1.0 / np.sqrt(d)
        query = hidden_states @ Wq
        kv = decoder_hidden_states @ Wkv
        key, value = jnp.split(kv, 2, axis=-1)
        scores = jnp.einsum('bqd,bkd->bqk', query, key) * scale
        w = jax.nn.softmax(scores, axis=-1)
        return jnp.einsum('bqk,bkd->bqd', w, value)

    def _L1_ffn_ref(x, gate_query, log_temp, w1, b1, w2, b2):
        import jax, jax.numpy as jnp
        import numpy as np
        B, N, D, E, DFF = (4, 512, 256, 16, 1024)
        CAPACITY_FACTOR = 2.0
        CAP = int(N * CAPACITY_FACTOR / E)
        SINKHORN_ITERS = 6

        def _sinkhorn(logits, n_iters=SINKHORN_ITERS, tau=1.0):
            t = logits / tau
            for _ in range(n_iters):
                t = t - jax.scipy.special.logsumexp(t, axis=-2, keepdims=True)
                t = t - jax.scipy.special.logsumexp(t, axis=-1, keepdims=True)
            return jnp.exp(t)
        b, n, d = x.shape
        gate_logits = jnp.einsum('bnd,ed->ben', x, gate_query)
        affinity_logits = gate_logits / jnp.exp(log_temp)
        affinity = _sinkhorn(affinity_logits)
        gates, idx = jax.lax.top_k(affinity, CAP)
        expert_in = jnp.take_along_axis(x[:, None, :, :], idx[..., None], axis=2)
        h = jax.nn.gelu(jnp.einsum('becd,edf->becf', expert_in, w1) + b1[None, :, None, :])
        expert_out = jnp.einsum('becf,efd->becd', h, w2) + b2[None, :, None, :]
        out = jnp.zeros_like(x)
        out = out.at[jnp.arange(b)[:, None, None], idx].add(gates[..., None] * expert_out)
        return out
    x = x + jnp.tanh(g_xattn[0]) * _L0_xattn_ref(_layernorm(x, axis=-1), ctx_1024, L0_xattn_Wq, L0_xattn_Wkv, L0_xattn_Wout, mask_SxS2_fk0)
    x = x + jnp.tanh(g_ffn[0]) * _L0_ffn_ref(_layernorm(x, axis=-1), L0_ffn_W_fc, L0_ffn_b_fc, L0_ffn_A_fc, L0_ffn_B_fc, L0_ffn_W_proj, L0_ffn_b_proj, L0_ffn_A_proj, L0_ffn_B_proj)
    x = x + jnp.tanh(g_xattn[1]) * _L1_xattn_ref(_layernorm(x, axis=-1), ctx_1024, L1_xattn_Wq, L1_xattn_Wkv)
    x = x + jnp.tanh(g_ffn[1]) * _L1_ffn_ref(_layernorm(x, axis=-1), L1_ffn_gate_query, L1_ffn_log_temp, L1_ffn_w1, L1_ffn_b1, L1_ffn_w2, L1_ffn_b2)
    return x

_drawn_inputs = setup_inputs


def setup_inputs(seed=0):
    import zlib

    import numpy as np

    out = dict(_drawn_inputs(seed))
    spreads = {'g_ffn': (-1.0, 0.6),
     'L0_ffn_b_fc': (0.0, 0.1),
     'L0_ffn_B_fc': (0.0, 0.1),
     'L0_ffn_b_proj': (0.0, 0.1),
     'L0_ffn_B_proj': (0.0, 0.1),
     'L1_ffn_b1': (0.0, 0.8),
     'L1_ffn_b2': (0.0, 2.0)}
    factors = {'L1_ffn_gate_query': 5.892, 'L1_ffn_w1': 6.011, 'L1_ffn_w2': 5.377}
    for name, (base, spread) in spreads.items():
        noise = np.random.default_rng([zlib.crc32(name.encode()), seed]).standard_normal(out[name].shape)
        drawn = base * np.exp(spread * noise) if base else spread * noise
        out[name] = jnp.asarray(drawn.astype(out[name].dtype))
    for name, factor in factors.items():
        out[name] = (out[name] * factor).astype(out[name].dtype)
    return out
```

```python
from contextlib import ExitStack

import concourse.bass as bass
from concourse import mybir

F32 = mybir.dt.float32
BF16 = mybir.dt.bfloat16
I32 = mybir.dt.int32
ALU = mybir.AluOpType
ACT = mybir.ActivationFunctionType
AX = mybir.AxisListType

P = 128
EPS = 1e-5
ROUND = 12582912.0


class Sig:

    def __init__(self, sem, per=0):
        self.sem, self.per, self.n = sem, per, 0

    def up(self, ins):
        self.n += 1
        ins.then_inc(self.sem, 1)

    def wait(self, eng, b, k):
        eng.wait_ge(self.sem, b * self.per + k)


def build(nc, x, ctx_1024, mask, g_xattn, g_ffn, wq0, wkv0, wout0, w_fc, b_fc, a_fc, bb_fc, w_proj, b_proj,
          a_proj, bb_proj, wq1, wkv1, gate_query, log_temp, w1, b1, w2, b2, out):
    B, S, D = x.shape
    C = ctx_1024.shape[1]
    H, A = 16, D // 16
    FF = w_fc.shape[0]
    E, _, DFF = w1.shape
    R = a_fc.shape[0]
    CAP = 64
    NT, KT, FT = S // P, D // P, FF // P
    T = B * NT
    EF = DFF // P
    ISQ = 1.0 / 16.0
    SINK = 6
    assert B * E == P and D == 256 and FF == DFF == 1024

    with ExitStack() as cx:
        def sb(name, shape, dt=F32):
            return cx.enter_context(nc.sbuf_tensor(name, shape, dt))

        def sem(name):
            return cx.enter_context(nc.semaphore(name))

        ident = sb("ident", [P, P])
        blk8 = sb("blk8", [P, B])
        blk = sb("blk", [P, P])
        iota_c = sb("iota_c", [P, CAP])
        iota_i = sb("iota_i", [P, CAP], I32)
        identb = sb("identb", [P, P], BF16)
        posB = sb("posB", [P, NT, B, E])
        affp = sb("affp", [P, NT, 3, B, E], BF16)
        G = sb("G", [P, 2, NT * B, CAP], BF16)
        gt = sb("gt", [P, 2, 4])
        rm = sb("rm", [P, 8])
        scratch = sb("scratch", [P, 1])
        Bd = sb("Bd", [P, B])
        ra = sb("ra", [P, NT * B])
        vt = sb("vt", [P, B])
        m8 = sb("m8", [P, 8])
        xs = sb("xs", [P, T, D])
        gates4 = sb("gates4", [P, 4])
        xh = sb("xh", [P, T, D], BF16)
        xl = sb("xl", [P, T, D], BF16)
        tlog = sb("tlog", [P, NT, B, E])
        b1T = sb("b1T", [P, EF, E])

        ARENA = 41984
        arena = sb("arena", [P, ARENA])
        at = [0]

        def carve(shape, dt=F32):
            n = 1
            for s in shape:
                n *= s
            words = n if dt != BF16 else (n + 1) // 2
            v = arena[:, at[0]:at[0] + words]
            at[0] += words
            assert at[0] <= ARENA, at[0]
            if dt != F32:
                v = v.bitcast(dt)
            names = "abcdef"[:len(shape)]
            if len(shape) == 1:
                return v
            return v.rearrange(f"p ({' '.join(names)}) -> p {' '.join(names)}",
                               **{c: s for c, s in zip(names, shape)})

        ctxn = carve([B, D])
        maskr = carve([NT, C])
        wnat = carve([2 + 4 + 2, D])
        wfn = carve([FT, D])
        wpn = carve([KT, FF])
        wq1s = carve([KT, D])
        wkv1s = carve([KT, 2 * D])
        afc = carve([D])
        apj = carve([FF])
        bfn = carve([FT, R])
        bpn = carve([KT, R])
        gqn = carve([D])
        bfT = carve([FF])
        bpT = carve([D])
        w0T = carve([KT, 8 * P])
        W1T = carve([KT, FF])
        W2T = carve([FT, D])
        ctxT = carve([KT, B * C])
        k0T = carve([KT, B * C])
        k1T = carve([KT, B * C])
        V0 = carve([B, H, A + 1])
        V1 = carve([B, D])
        gqT = carve([KT, E])
        bfcT = carve([FT])
        b8n = carve([P])
        b1n = carve([DFF])
        bpb = carve([D])
        ltb = carve([1])
        wmx = carve([2])
        wsc = carve([4, 2])
        dense_end = at[0]

        LNS = ("attn0", "ffn0", "attn1", "ffn1")
        xn = carve([NT, D])
        xT = carve([KT, S])
        st = carve([NT, 6])
        mv = carve([NT, 2])
        vpe = carve([NT])
        lnv = carve([NT])
        y0 = carve([NT])
        nt1 = carve([NT])
        qT = carve([KT, S])
        kbd = wnat.rearrange("p j d -> p (j d)")[:, 0:KT * 8 * C].rearrange("p (k h c) -> p k h c", k=KT, h=8)
        Tb = carve([2, 4, C])
        Eb = carve([2, 4, C])
        mx = carve([2, 4])
        PT = carve([2, 4, P])
        rden = carve([H])
        att = carve([NT, D])
        hT = wfn
        nm1 = carve([NT])
        sm1 = carve([NT])
        ri1 = carve([NT])
        assert at[0] <= ARENA, at[0]

        ps = cx.enter_context(nc.psum_tensor("ps", [P, 8, 512], F32))


        def bank(n, words=512):
            return ps[:, n, 0:words]

        ld_misc, ld_w, ld_ffn, ld_x = sem("ld_misc"), sem("ld_w"), sem("ld_ffn"), sem("ld_x")
        const_ready = sem("const_ready")
        consts_made = sem("consts_made")
        absmax_ready, allmax_ready, quant_step = sem("absmax_ready"), sem("allmax_ready"), sem("quant_step")
        prep_mm, prep_ev = sem("prep_mm"), sem("prep_ev")
        gate_act = sem("gate_act")

        def sig(name, per):
            return Sig(sem(name), per)

        ln_dve = [sig(f"ln_dve_{n}", 11) for n in LNS]
        ln_act = [sig(f"ln_act_{n}", 2) for n in LNS]
        xT_mm = [sig(f"xT_mm_{n}", 1) for n in LNS]
        xT_ready = [sig(f"xT_ready_{n}", 1) for n in LNS]
        kbd_ready = sig("kbd_ready", 2)
        q_mm, q_ready = sig("q_mm", 1), sig("q_ready", 1)
        s_mm, s_masked, s_max, s_sub, s_exp = (sig(n, 8) for n in ("s_mm", "s_masked", "s_max", "s_sub", "s_exp"))
        pT_mm, pT_ready, av_mm = sig("pT_mm", 8), sig("pT_ready", 8), sig("av_mm", 8)
        att_ready = sig("att_ready", 4)
        attT_mm, attT_ready, wo_mm, x_attn0 = sig("attT_mm", 1), sig("attT_ready", 1), sig("wo_mm", 1), sig("x_attn0", 1)
        h_mm, h_ready, f_mm, x_ffn0 = sig("h_mm", 4), sig("h_ready", 8), sig("f_mm", 1), sig("x_ffn0", 2)
        q1_mm, q1_ready, s1_mm, m1_ready, e1_ready = (sig(n, p) for n, p in (
            ("q1_mm", 1), ("q1_ready", 1), ("s1_mm", 1), ("m1_ready", 2), ("e1_ready", 2)))
        p1T_mm, p1T_ready, av1_mm, r1_ready, x_attn1 = (sig(n, p) for n, p in (
            ("p1T_mm", 1), ("p1T_ready", 1), ("av1_mm", 1), ("r1_ready", 2), ("x_attn1", 2)))
        xh_ready, xl_ready, g_mm, t_ready = (sig(n, 1) for n in ("xh_ready", "xl_ready", "g_mm", "t_ready"))

        N_MISC, N_W, N_FFN, N_X = 8, 6, 6, 4
        CONSTS = 11
        EV_K0 = 13

        route_dve, route_act, route_pe = Sig(sem("route_dve")), sem("route_act"), sem("route_pe")
        ROUTED = 53
        stored = sem("stored")
        ld_w1, ld_w2, ld_b2 = sig("ld_w1", 16), sig("ld_w2", 16), sig("ld_b2", 16)
        w1h_ready, w1l_ready, w2h_ready, w2l_ready = (sig(n, 2) for n in ("w1h_ready", "w1l_ready", "w2h_ready", "w2l_ready"))
        g_ready, g_mm2, xgh_ready, xgl_ready, gt_ready = (sig(n, p) for n, p in (
            ("g_ready", 1), ("g_mm2", 5), ("xgh_ready", 2), ("xgl_ready", 2), ("gt_ready", 2)))
        m1_mm, gelu_ready, hh_ready, hl_ready = (sig(n, EF) for n in ("m1_mm", "gelu_ready", "hh_ready", "hl_ready"))
        m2_mm, y_t, yh_ready, yl_ready = sig("m2_mm", 2), sig("y_t", 2), sig("yh_ready", 2), sig("yl_ready", 2)
        yg_ready = sig("yg_ready", 8)
        gs_ready, gst_mm = (sig(n, NT) for n in ("gs_ready", "gst_mm"))
        gt2_act, gt2_dve = (sig(n, 1) for n in ("gt2_act", "gt2_dve"))
        c_mm, out_ready = sig("c_mm", 1), sig("out_ready", 1)

        def psb(n):
            return ps[:, n, :].bitcast(BF16)

        at[0] = 0
        YH, YL = [carve([E // 2, B, D], BF16) for _ in range(2)]
        w1h_at = at[0]
        w1h, w1l = [carve([2, KT, DFF], BF16) for _ in range(2)]
        w2h, w2l = [carve([2, EF, D], BF16) for _ in range(2)]
        xgh, xgl = [carve([2, KT, B * CAP], BF16) for _ in range(2)]
        hh, hl = [carve([EF, B * CAP], BF16) for _ in range(2)]
        hf = carve([2, B * CAP])
        yt = carve([2, 2, D])
        yg = carve([2, 4, D])
        experts_end = at[0]
        at[0] = w1h_at
        GT = carve([2, NT, E // 2, P], BF16)
        Gs = carve([2, NT, E, CAP], BF16)
        assert at[0] <= w1h_at + 8192
        at[0] = 0
        ls = carve([NT * B])
        mxe = carve([NT * B])
        tn = carve([NT, B * E])
        ex = carve([NT, B * E])
        KA = carve([S])
        KB = carve([NT, P])
        lnU = carve([S])
        t6 = carve([S])
        aff = carve([S])
        wk = carve([S])
        posn = carve([S])
        blkB = carve([P])
        assert at[0] <= w1h_at and experts_end <= ARENA - 4096 - 512, (at[0], experts_end)
        w1r, w2r, b2b = (arena[:, ARENA - o:ARENA - o + w] for o, w in ((4608, 2048), (2560, 2048), (512, 512)))
        w1r = w1r.rearrange("p (k f) -> p k f", k=KT)
        w2r = w2r.rearrange("p (f d) -> p f d", f=EF)
        b2b = b2b.rearrange("p (a d) -> p a d", a=2)

        block = cx.enter_context(nc.Block())

        @block.sync
        def _(sp):
            def ld(dst, src, s):
                sp.dma_start(dst, src).then_inc(s, 16)

            xv = x.rearrange("b (n p) d -> p (b n) d", p=P)
            ld(ctxn[0:C], ctx_1024.rearrange("b c d -> c b d"), ld_w)
            ld(wnat[:, 0:2], wq0.rearrange("(j p) d -> p j d", p=P), ld_w)
            ld(wnat[:, 2:6], wkv0.rearrange("(j p) d -> p j d", p=P), ld_w)
            ld(wnat[:, 6:8], wout0.rearrange("(j p) d -> p j d", p=P), ld_w)
            ld(wq1s, wq1.rearrange("(k p) n -> p k n", p=P), ld_w)
            ld(wkv1s, wkv1.rearrange("(k p) n -> p k n", p=P), ld_w)
            ld(wfn, w_fc.rearrange("(j p) d -> p j d", p=P), ld_ffn)
            ld(wpn, w_proj.rearrange("(j p) d -> p j d", p=P), ld_ffn)
            ld(bfn, bb_fc.rearrange("(j p) r -> p j r", p=P), ld_ffn)
            ld(bpn, bb_proj.rearrange("(j p) r -> p j r", p=P), ld_ffn)
            ld(afc[0:R], a_fc, ld_ffn)
            ld(apj[0:R], a_proj, ld_ffn)
            for q in range(4):
                ld(xs[:, 4 * q:4 * q + 4, :], xv[:, 4 * q:4 * q + 4, :], ld_x)
            ld(maskr, mask.rearrange("(n p) c -> p n c", p=P), ld_misc)
            ld(gqn[0:E], gate_query, ld_misc)
            ld(b8n[0:FT], b_fc.rearrange("(j p) -> j p", p=P), ld_misc)
            ld(b1n[0:E], b1, ld_misc)
            ld(bpb, b_proj.rearrange("(a d) -> a d", a=1).broadcast_to([P, D]), ld_misc)
            ld(ltb, log_temp.rearrange("(a d) -> a d", a=1).broadcast_to([P, 1]), ld_misc)
            ld(gates4[:, 0:2], g_xattn.rearrange("(a d) -> a d", a=1).broadcast_to([P, 2]), ld_misc)
            ld(gates4[:, 2:4], g_ffn.rearrange("(a d) -> a d", a=1).broadcast_to([P, 2]), ld_misc)

        def pool_batch(pool, b):
            for m in range(KT):
                kb = k0T[:, m, bass.ds(b * C, C)] if not isinstance(b, int) else k0T[:, m, b * C:b * C + C]
                kbd_ready.up(pool.tensor_tensor(kbd[:, m], kb.unsqueeze(1).broadcast_to([P, 8, C]),
                                                blk8[:, :].unsqueeze(2).broadcast_to([P, 8, C]), ALU.mult))
            for s in range(8):
                s_max.wait(pool, b, s + 1)
                s_sub.up(pool.tensor_tensor(Tb[:, s % 2], Tb[:, s % 2],
                                            mx[:, s % 2].unsqueeze(2).broadcast_to([P, 4, C]), ALU.subtract))
            ln_dve[3].wait(pool, b, 11)
            xh_ready.up(pool.tensor_copy(tiles(xh, b), xn))

        def tiles(t, b):
            return t[:, bass.ds(b * NT, NT), :] if not isinstance(b, int) else t[:, b * NT:b * NT + NT, :]

        @block.gpsimd
        def _(pool):
            pool.memset(ident[:, :], 0.0).then_inc(consts_made, 1)
            pool.memset(blk8[:, :], 1.0).then_inc(consts_made, 1)
            pool.memset(blk[:, :], 1.0).then_inc(consts_made, 1)
            pool.iota(iota_i[:, :], [[1, CAP]], base=0, channel_multiplier=0).then_inc(consts_made, 1)
            pool.wait_ge(consts_made, 4)
            pool.affine_select(out=ident[:, :], in_=ident[:, :], compare_op=ALU.not_equal, fill=1.0,
                               base=0, pattern=[[-1, P]], channel_multiplier=1).then_inc(consts_made, 1)
            pool.affine_select(out=blk8[:, :], in_=blk8[:, :], compare_op=ALU.is_ge, fill=0.0,
                               base=0, pattern=[[-E, B]], channel_multiplier=1).then_inc(consts_made, 1)
            pool.affine_select(out=blk[:, :], in_=blk[:, :], compare_op=ALU.is_ge, fill=0.0,
                               base=0, pattern=[[-E, B], [0, E]], channel_multiplier=1).then_inc(consts_made, 1)
            pool.tensor_copy(iota_c[:, :], iota_i[:, :]).then_inc(consts_made, 1)
            pool.wait_ge(consts_made, 5)
            pool.tensor_copy(identb[:, :], ident[:, :]).then_inc(consts_made, 1)
            pool.wait_ge(consts_made, 9)
            pool.affine_select(out=blk8[:, :], in_=blk8[:, :], compare_op=ALU.is_ge, fill=0.0,
                               base=E - 1, pattern=[[E, B]], channel_multiplier=-1).then_inc(consts_made, 1)
            pool.affine_select(out=blk[:, :], in_=blk[:, :], compare_op=ALU.is_ge, fill=0.0,
                               base=E - 1, pattern=[[E, B], [0, E]], channel_multiplier=-1).then_inc(consts_made, 1)
            pool.wait_ge(consts_made, CONSTS)
            pool.wait_ge(absmax_ready, 2)
            pool.partition_all_reduce(wsc[:, 0], wmx[:, :], P, bass.bass_isa.ReduceOp.max).then_inc(allmax_ready, 1)
            pool.wait_ge(prep_ev, EV_K0)
            with pool.Fori(0, B) as b:
                pool_batch(pool, b)

        def transpose(pe, dst, src, parts=P):
            return pe.transpose(dst, src, ident[0:parts, 0:parts])

        def pe_transposed(pe, L, b):
            ln_dve[L].wait(pe, b, 11)
            for k in range(KT):
                for n in range(NT):
                    last = transpose(pe, bank(0)[:, k * S + n * P:k * S + n * P + P], xn[:, n, k * P:k * P + P])
            xT_mm[L].up(last)

        def project(pe, w, wcol):
            for m in range(KT):
                for k in range(KT):
                    last = pe.matmul(bank(1)[:, m * S:m * S + S], w[:, k, wcol + m * P:wcol + m * P + P], xT[:, k, :],
                                     start=(k == 0), stop=(k == KT - 1))
            return last

        def col(t, k, b):
            return t[:, k, bass.ds(b * C, C)] if not isinstance(b, int) else t[:, k, b * C:b * C + C]

        def at_batch(t, b):
            return t[:, bass.ds(b, 1)] if not isinstance(b, int) else t[:, b:b + 1]

        def pe_batch(pe, b):
            pe_transposed(pe, 0, b)
            xT_ready[0].wait(pe, b, 1)
            q_mm.up(project(pe, w0T, 0))
            q_ready.wait(pe, b, 1)
            kbd_ready.wait(pe, b, 2)

            def scores(s):
                n, g = s // 4, s % 4
                if s >= 2:
                    s_masked.wait(pe, b, s - 1)
                s_mm.up(pe.matmul(bank(1 + s % 2, 4 * C), qT[:, g // 2, n * P:n * P + P],
                                  kbd[:, g // 2, 4 * (g % 2):4 * (g % 2) + 4, :], start=True, stop=True))

            def weighted(s):
                n, g = s // 4, s % 4
                pT_ready.wait(pe, b, s + 1)
                for h in range(4):
                    hh = 4 * g + h
                    last = pe.matmul(bank(4 + n)[:, hh * (A + 1):(hh + 1) * (A + 1)], PT[0:C, s % 2, h, :],
                                     at_batch(V0, b)[0:C, :, hh, :].rearrange("p a c -> p (a c)"),
                                     start=True, stop=True)
                av_mm.up(last)

            scores(0)
            scores(1)
            for s in range(8):
                s_exp.wait(pe, b, s + 1)
                if s >= 1:
                    pT_ready.wait(pe, b, s)
                for h in range(4):
                    last = transpose(pe, bank(3)[0:C, h * P:h * P + P], Eb[:, s % 2, h, :])
                pT_mm.up(last)
                if s + 2 < 8:
                    scores(s + 2)
                if s >= 1:
                    weighted(s - 1)
            weighted(7)
            att_ready.wait(pe, b, 4)
            for k in range(KT):
                for n in range(NT):
                    last = transpose(pe, bank(0)[:, k * S + n * P:k * S + n * P + P], att[:, n, k * P:k * P + P])
            attT_mm.up(last)
            attT_ready.wait(pe, b, 1)
            for n in range(NT):
                for k in range(KT):
                    last = pe.matmul(bank(6)[:, n * D:n * D + D], xT[:, k, n * P:n * P + P], w0T[:, k, 6 * P:8 * P],
                                     start=(k == 0), stop=(k == KT - 1))
            wo_mm.up(last)
            pe_transposed(pe, 1, b)
            xT_ready[1].wait(pe, b, 1)
            for j in range(4):
                if j >= 2:
                    h_ready.wait(pe, b, 2 * j - 2)
                for f in (2 * j, 2 * j + 1):
                    for k in range(KT):
                        last = pe.matmul(bank(6 + j % 2)[:, (f % 2) * S:(f % 2) * S + S],
                                         W1T[:, k, f * P:f * P + P], xT[:, k, :], start=(k == 0), stop=(k == KT - 1))
                h_mm.up(last)
            for f in range(FT):
                h_ready.wait(pe, b, f + 1)
                for n in range(NT):
                    last = pe.matmul(bank(4 + n)[:, 0:D], hT[:, f, n * P:n * P + P], W2T[:, f, :],
                                     start=(f == 0), stop=(f == FT - 1))
            f_mm.up(last)
            pe_transposed(pe, 2, b)
            xT_ready[2].wait(pe, b, 1)
            q1_mm.up(project(pe, wq1s, 0))
            q1_ready.wait(pe, b, 1)
            for n in range(NT):
                for k in range(KT):
                    last = pe.matmul(bank(2)[:, n * C:n * C + C], qT[:, k, n * P:n * P + P], col(k1T, k, b),
                                     start=(k == 0), stop=(k == KT - 1))
            s1_mm.up(last)
            e1_ready.wait(pe, b, 2)
            for n in range(NT):
                last = transpose(pe, bank(3)[0:C, n * P:n * P + P], Eb[:, 0, n, :])
            p1T_mm.up(last)
            p1T_ready.wait(pe, b, 1)
            for n in range(NT):
                last = pe.matmul(bank(6)[:, n * D:n * D + D], PT[0:C, 0, n, :],
                                 at_batch(V1, b)[0:C].rearrange("p a d -> p (a d)"), start=True, stop=True)
            av1_mm.up(last)
            pe_transposed(pe, 3, b)
            xT_ready[3].wait(pe, b, 1)
            for n in range(NT):
                for k in range(KT):
                    last = pe.matmul(bank(1)[:, n * E:n * E + E], xT[:, k, n * P:n * P + P], gqT[:, k, :],
                                     start=(k == 0), stop=(k == KT - 1))
            g_mm.up(last)

        def pe_prep(pe):
            n = [0]

            def group():
                if n[0] >= 8:
                    pe.wait_ge(prep_ev, n[0] - 7)
                n[0] += 1
                return (n[0] - 1) % 8

            def done(last):
                last.then_inc(prep_mm, 1)

            def put(g, c0, src, parts):
                w = src.shape[-1]
                return transpose(pe, bank(g)[0:w, c0:c0 + parts], src, parts)

            pe.wait_ge(consts_made, CONSTS)
            pe.wait_ge(ld_w, 16 * N_W)
            for k in range(KT):
                for jh in range(2):
                    g = group()
                    for j in range(4):
                        last = put(g, j * P, wnat[:, 4 * jh + j, k * P:k * P + P], P)
                    done(last)
            for k in range(KT):
                for bh in range(2):
                    g = group()
                    for j in range(4):
                        last = put(g, j * C, ctxn[0:C, 4 * bh + j, k * P:k * P + P], C)
                    done(last)
            pe.wait_ge(ld_misc, 16 * N_MISC)
            g = group()
            put(g, 0, b8n[0:FT, :], FT)
            for k in range(KT):
                put(g, 16 + k * E, gqn[0:E, k * P:k * P + P], E)
            for j in range(EF):
                last = put(g, 64 + j * E, b1n[0:E, j * P:j * P + P], E)
            done(last)
            pe.wait_ge(prep_ev, 8)
            for m in range(KT):
                for half in range(2):
                    g = group()
                    for k in range(KT):
                        last = pe.matmul(bank(g, 4 * C), w0T[:, k, D + m * P:D + m * P + P],
                                         ctxT[:, k, half * 4 * C:(half + 1) * 4 * C], start=(k == 0), stop=(k == 1))
                    done(last)
            for m in range(KT):
                for half in range(2):
                    g = group()
                    for k in range(KT):
                        last = pe.matmul(bank(g, 4 * C), wkv1s[:, k, m * P:m * P + P],
                                         ctxT[:, k, half * 4 * C:(half + 1) * 4 * C], start=(k == 0), stop=(k == 1))
                    done(last)
            for b in range(B):
                g = group()
                for c0, w in ((0, w0T[:, :, 2 * D:3 * D]), (D, wkv1s[:, :, D:2 * D])):
                    for k in range(KT):
                        last = pe.matmul(bank(g)[0:C, c0:c0 + D], ctxT[:, k, b * C:b * C + C], w[:, k, :],
                                         start=(k == 0), stop=(k == 1))
                done(last)
            pe.wait_ge(ld_ffn, 16 * N_FFN)
            for half in range(2):
                g = group()
                for j in range(4):
                    last = put(g, j * P, bfn[:, 4 * half + j, :], P)
                done(last)
            g = group()
            for j in range(KT):
                last = put(g, j * P, bpn[:, j, :], P)
            done(last)
            pe.wait_ge(quant_step, 8)
            for k in range(KT):
                for half in range(2):
                    g = group()
                    for j in range(4):
                        last = put(g, j * P, wfn[:, 4 * half + j, k * P:k * P + P], P)
                    done(last)
            pe.wait_ge(prep_ev, 28)
            for k in range(KT):
                for half in range(2):
                    g = group()
                    done(pe.matmul(bank(g), afc[0:R, k * P:k * P + P], bfT[0:R, half * 512:half * 512 + 512],
                                   start=True, stop=True))
            for q in range(4):
                g = group()
                for f in range(2):
                    for j in range(KT):
                        last = put(g, f * D + j * P, wpn[:, j, (2 * q + f) * P:(2 * q + f + 1) * P], P)
                done(last)
            for q in range(4):
                g = group()
                for f in range(2):
                    last = pe.matmul(bank(g)[:, f * D:f * D + D], apj[0:R, (2 * q + f) * P:(2 * q + f + 1) * P],
                                     bpT[0:R, :], start=True, stop=True)
                done(last)

        @block.tensor
        def _(pe):
            pe_prep(pe)
            pe.wait_ge(prep_ev, 44)
            with pe.Fori(0, B) as b:
                pe_batch(pe, b)

        def dve_prep(dve):
            n = [0]

            def evac(ins_of, *args):
                dve.wait_ge(prep_mm, n[0] + 1)
                last = ins_of(n[0] % 8)
                last.then_inc(prep_ev, 1)
                n[0] += 1

            dve.memset(V0[:, :, :, A:A + 1], 1.0)
            for k in range(KT):
                for jh in range(2):
                    evac(lambda g: dve.tensor_copy(w0T[:, k, jh * 512:jh * 512 + 512], bank(g)))
            for k in range(KT):
                for bh in range(2):
                    evac(lambda g: dve.tensor_copy(ctxT[:, k, bh * 480:bh * 480 + 480], bank(g, 480)))

            def small(g):
                dve.tensor_copy(bfcT[:, :], bank(g)[:, 0:FT])
                dve.tensor_copy(gqT[:, :, :], bank(g)[:, 16:16 + KT * E].rearrange("p (k e) -> p k e", k=KT))
                return dve.tensor_copy(b1T[:, :, :], bank(g)[:, 64:64 + EF * E].rearrange("p (k e) -> p k e", k=EF))

            evac(small)
            for dst in (k0T, k1T):
                for m in range(KT):
                    for half in range(2):
                        evac(lambda g: dve.tensor_copy(dst[:, m, half * 480:half * 480 + 480], bank(g, 480)))

            def values(g, b):
                dve.tensor_copy(V0[0:C, b, :, 0:A], bank(g)[0:C, 0:D].rearrange("p (h a) -> p h a", h=H))
                return dve.tensor_copy(V1[0:C, b, :], bank(g)[0:C, D:2 * D])

            for b in range(B):
                evac(lambda g: values(g, b))
            dve.wait_ge(ld_ffn, 16 * N_FFN)
            dve.tensor_reduce(wmx[:, 0:1], wfn, AX.XY, ALU.max, apply_absolute_value=True).then_inc(absmax_ready, 1)
            dve.tensor_reduce(wmx[:, 1:2], wpn, AX.XY, ALU.max, apply_absolute_value=True).then_inc(absmax_ready, 1)
            dve.wait_ge(allmax_ready, 1)
            dve.tensor_scalar(wsc[:, 1], wsc[:, 0], 1.0 / 127.0, None, ALU.mult).then_inc(quant_step, 1)
            dve.wait_ge(quant_step, 1)
            dve.reciprocal(wsc[:, 2], wsc[:, 1]).then_inc(quant_step, 1)
            dve.wait_ge(quant_step, 2)
            for i, w in ((0, wfn), (1, wpn)):
                dve.tensor_scalar(w, w, wsc[:, 2, i:i + 1], ROUND, ALU.mult, ALU.add).then_inc(quant_step, 1)
            dve.wait_ge(quant_step, 4)
            for w in (wfn, wpn):
                dve.tensor_scalar(w, w, ROUND, 127.0, ALU.subtract, ALU.min).then_inc(quant_step, 1)
            dve.wait_ge(quant_step, 6)
            for i, w in ((0, wfn), (1, wpn)):
                dve.tensor_scalar(w, w, -128.0, wsc[:, 1, i:i + 1], ALU.max, ALU.mult).then_inc(quant_step, 1)
            dve.wait_ge(gate_act, 2)
            dve.tensor_scalar(bpb[:, :], bpb[:, :], gates4[:, 2:3], None, ALU.mult).then_inc(quant_step, 1)
            for half in range(2):
                evac(lambda g: dve.tensor_scalar(bfT[0:R, half * 512:half * 512 + 512], bank(g)[0:R, :], 2.0, None, ALU.mult))
            evac(lambda g: dve.tensor_scalar(bpT[0:R, :], bank(g)[0:R, 0:D], 2.0, None, ALU.mult))
            for k in range(KT):
                for half in range(2):
                    evac(lambda g: dve.tensor_copy(W1T[:, k, half * 512:half * 512 + 512], bank(g)))
            dve.wait_ge(prep_ev, 32)
            for k in range(KT):
                for half in range(2):
                    evac(lambda g: dve.tensor_tensor(W1T[:, k, half * 512:half * 512 + 512],
                                                     W1T[:, k, half * 512:half * 512 + 512], bank(g), ALU.add))
            for q in range(4):
                evac(lambda g: dve.tensor_copy(W2T[:, 2 * q:2 * q + 2, :].rearrange("p f d -> p (f d)"), bank(g)))
            dve.wait_ge(prep_ev, 40)
            for q in range(4):
                v = W2T[:, 2 * q:2 * q + 2, :].rearrange("p f d -> p (f d)")
                evac(lambda g: dve.tensor_tensor(v, v, bank(g), ALU.add))

        def dve_norm(dve, L, b):
            s = ln_dve[L]
            dve.memset(scratch[:, :], 0.0)
            for n in range(NT):
                s.up(dve.bn_stats(st[:, n, :], tiles(xs, b)[:, n, :]))
            s.wait(dve, b, 2)
            dve.memset(scratch[:, :], 0.0)
            for n in range(NT):
                s.up(dve.bn_aggr(mv[:, n, :], st[:, n, :]))
            s.wait(dve, b, 4)
            s.up(dve.tensor_scalar(vpe[:, :], mv[:, :, 1], EPS, None, ALU.add))
            ln_act[L].wait(dve, b, 2)
            s.up(dve.tensor_tensor(nt1[:, :], y0[:, :], y0[:, :], ALU.mult))
            s.wait(dve, b, 6)
            s.up(dve.tensor_tensor(nt1[:, :], nt1[:, :], vpe[:, :], ALU.mult))
            s.wait(dve, b, 7)
            s.up(dve.tensor_scalar(nt1[:, :], nt1[:, :], -0.5, 1.5, ALU.mult, ALU.add))
            s.wait(dve, b, 8)
            s.up(dve.tensor_tensor(y0[:, :], y0[:, :], nt1[:, :], ALU.mult))
            s.wait(dve, b, 9)
            for n in range(NT):
                s.up(dve.tensor_scalar(xn[:, n, :], tiles(xs, b)[:, n, :], mv[:, n, 0:1], y0[:, n:n + 1],
                                       ALU.subtract, ALU.mult))

        def dve_batch(dve, b):
            dve_norm(dve, 0, b)

            def maximum(s):
                s_masked.wait(dve, b, s + 1)
                s_max.up(dve.tensor_reduce(mx[:, s % 2], Tb[:, s % 2], AX.X, ALU.max))

            def normalise(n):
                av_mm.wait(dve, b, 4 * n + 4)
                o = bank(4 + n)[:, 0:H * (A + 1)].rearrange("p (h a) -> p h a", h=H)
                att_ready.up(dve.reciprocal(rden[:, :], o[:, :, A]))
                att_ready.wait(dve, b, 2 * n + 1)
                att_ready.up(dve.tensor_tensor(att[:, n, :].rearrange("p (h a) -> p h a", h=H), o[:, :, 0:A],
                                               rden[:, :].unsqueeze(2).broadcast_to([P, H, A]), ALU.mult))

            for s in range(8):
                n = s // 4
                s_mm.wait(dve, b, s + 1)
                if s >= 2:
                    s_exp.wait(dve, b, s - 1)
                s_masked.up(dve.tensor_tensor(
                    Tb[:, s % 2], bank(1 + s % 2, 4 * C).rearrange("p (h c) -> p h c", h=4),
                    maskr[:, n, :].unsqueeze(1).broadcast_to([P, 4, C]), ALU.add))
                maximum(s)
                if s == 6:
                    normalise(0)
            normalise(1)
            wo_mm.wait(dve, b, 1)
            xb = tiles(xs, b)
            x_attn0.up(dve.scalar_tensor_tensor(out=xb, in0=bank(6).rearrange("p (n d) -> p n d", n=NT),
                                                scalar=gates4[:, 0:1], in1=xb, op0=ALU.mult, op1=ALU.add))
            x_attn0.wait(dve, b, 1)
            dve_norm(dve, 1, b)
            f_mm.wait(dve, b, 1)
            x_ffn0.up(dve.scalar_tensor_tensor(out=xb, in0=ps[:, 4:6, 0:D], scalar=gates4[:, 2:3], in1=xb,
                                               op0=ALU.mult, op1=ALU.add))
            x_ffn0.wait(dve, b, 1)
            x_ffn0.up(dve.tensor_tensor(xb, xb, bpb[:, :].unsqueeze(1).broadcast_to([P, NT, D]), ALU.add))
            x_ffn0.wait(dve, b, 2)
            dve_norm(dve, 2, b)
            s1_mm.wait(dve, b, 1)
            m1_ready.up(dve.tensor_reduce(nm1[:, :], bank(2)[:, 0:NT * C].rearrange("p (n c) -> p n c", n=NT),
                                          AX.X, ALU.max))
            m1_ready.wait(dve, b, 1)
            m1_ready.up(dve.tensor_scalar(nm1[:, :], nm1[:, :], -ISQ, None, ALU.mult))
            e1_ready.wait(dve, b, 2)
            r1_ready.up(dve.reciprocal(ri1[:, :], sm1[:, :]))
            r1_ready.wait(dve, b, 1)
            r1_ready.up(dve.tensor_scalar(ri1[:, :], ri1[:, :], gates4[:, 1:2], None, ALU.mult))
            r1_ready.wait(dve, b, 2)
            av1_mm.wait(dve, b, 1)
            for n in range(NT):
                x_attn1.up(dve.scalar_tensor_tensor(out=xb[:, n, :], in0=bank(6)[:, n * D:n * D + D],
                                                    scalar=ri1[:, n:n + 1], in1=xb[:, n, :], op0=ALU.mult, op1=ALU.add))
            x_attn1.wait(dve, b, 2)
            dve_norm(dve, 3, b)
            xh_ready.wait(dve, b, 1)
            xl_ready.up(dve.tensor_tensor(tiles(xl, b), xn, tiles(xh, b), ALU.subtract))
            g_mm.wait(dve, b, 1)
            tl = tlog[:, :, bass.ds(b, 1), :] if not isinstance(b, int) else tlog[:, :, b:b + 1, :]
            t_ready.up(dve.tensor_scalar(tl.rearrange("p n a e -> p n (a e)"),
                                         bank(1)[:, 0:NT * E].rearrange("p (n e) -> p n e", n=NT),
                                         ltb[:, 0:1], None, ALU.mult))
            xl_ready.wait(dve, b, 1)

        @block.vector
        def _(dve):
            dve_prep(dve)
            dve.wait_ge(ld_x, 64)
            with dve.Fori(0, B) as b:
                dve_batch(dve, b)

        def act_norm(act, L, b):
            ln_dve[L].wait(act, b, 5)
            ln_act[L].up(act.activation(lnv[:, :], vpe[:, :], ACT.Ln))
            ln_act[L].wait(act, b, 1)
            ln_act[L].up(act.activation(y0[:, :], lnv[:, :], ACT.Exp, scale=-0.5))
            xT_mm[L].wait(act, b, 1)
            xT_ready[L].up(act.activation(xT.rearrange("p k s -> p (k s)"), bank(0), ACT.Copy))

        def act_batch(act, b):
            act_norm(act, 0, b)
            q_mm.wait(act, b, 1)
            q_ready.up(act.activation(qT.rearrange("p k s -> p (k s)"), bank(1), ACT.Copy))

            def transposed(s):
                pT_mm.wait(act, b, s + 1)
                if s >= 2:
                    av_mm.wait(act, b, s - 1)
                pT_ready.up(act.activation(PT[0:C, s % 2], bank(3)[0:C].rearrange("p (h q) -> p h q", h=4), ACT.Copy))

            for s in range(8):
                s_sub.wait(act, b, s + 1)
                if s >= 2:
                    pT_mm.wait(act, b, s - 1)
                s_exp.up(act.activation(Eb[:, s % 2], Tb[:, s % 2], ACT.Exp, scale=ISQ))
                if s >= 1:
                    transposed(s - 1)
            transposed(7)
            attT_mm.wait(act, b, 1)
            attT_ready.up(act.activation(xT.rearrange("p k s -> p (k s)"), bank(0), ACT.Copy))
            act_norm(act, 1, b)
            for f in range(FT):
                j = f // 2
                h_mm.wait(act, b, j + 1)
                h_ready.up(act.activation(hT[:, f, :], bank(6 + j % 2)[:, (f % 2) * S:(f % 2) * S + S],
                                          ACT.Gelu, bias=bfcT[:, f:f + 1]))
            act_norm(act, 2, b)
            q1_mm.wait(act, b, 1)
            q1_ready.up(act.activation(qT.rearrange("p k s -> p (k s)"), bank(1), ACT.Copy))
            m1_ready.wait(act, b, 2)
            for n in range(NT):
                e1_ready.up(act.activation(Eb[:, 0, n, :], bank(2)[:, n * C:n * C + C], ACT.Exp,
                                           bias=nm1[:, n:n + 1], scale=ISQ, accum_out=sm1[:, n:n + 1]))
            p1T_mm.wait(act, b, 1)
            p1T_ready.up(act.activation(PT[0:C, 0, 0:NT, :],
                                        bank(3)[0:C, 0:NT * P].rearrange("p (n q) -> p n q", n=NT), ACT.Copy))
            act_norm(act, 3, b)

        @block.scalar
        def _(act):
            act.wait_ge(ld_misc, 16 * N_MISC)
            act.activation(gates4[:, :], gates4[:, :], ACT.Tanh).then_inc(gate_act, 1)
            act.activation(ltb[:, :], ltb[:, :], ACT.Exp, scale=-1.0).then_inc(gate_act, 1)
            act.wait_ge(prep_ev, 44)
            with act.Fori(0, B) as b:
                act_batch(act, b)

        def nb(t):
            return t.rearrange("p (g e) -> p g e", e=E)

        @block.vector
        def _(dve):
            T0 = tlog[:, :, :, :].rearrange("p n b e -> p (n b) e")
            TN = tn.rearrange("p n (b e) -> p (n b) e", e=E)
            EX = ex.rearrange("p n (b e) -> p (n b) e", e=E)

            def step(ins):
                route_dve.n += 1
                ins.then_inc(route_dve.sem, 1)
                dve.wait_ge(route_dve.sem, route_dve.n)

            def bc(v, k=E):
                return v.unsqueeze(2).broadcast_to([P, NT * B, k])

            dve.wait_ge(t_ready.sem, B)
            step(dve.tensor_reduce(mxe[:, :], T0, AX.X, ALU.max))
            step(dve.tensor_tensor(TN, T0, bc(mxe), ALU.subtract))
            dve.wait_ge(route_act, 1)
            step(dve.tensor_reduce(ls[:, :], EX, AX.X, ALU.add))
            dve.wait_ge(route_act, 2)
            step(dve.tensor_tensor(TN, TN, bc(ls), ALU.subtract))
            dve.wait_ge(route_pe, 1)
            step(dve.tensor_reduce(rm[:, 0:1], bank(0)[:, 0:S], AX.X, ALU.max))
            step(dve.tensor_scalar(rm[:, 1:2], rm[:, 0:1], -1.0, None, ALU.mult))
            dve.wait_ge(route_act, 3)
            step(dve.reciprocal(rm[:, 3:4], rm[:, 2:3]))
            step(dve.tensor_scalar(Bd[:, :], blk8[:, :], rm[:, 3:4], None, ALU.mult))
            for it in range(SINK - 2):
                dve.wait_ge(route_pe, 3 + 2 * it)
                step(dve.reciprocal(ra[:, :], bank(1)[:, 0:NT * B]))
                dve.wait_ge(route_pe, 4 + 2 * it)
                step(dve.tensor_tensor_reduce(out=vt[:, :], in0=bank(2)[:, 0:B], in1=blk8[:, :], scale=1.0,
                                              scalar=0.0, op0=ALU.mult, op1=ALU.add, accum_out=rm[:, 2:3]))
                step(dve.reciprocal(rm[:, 3:4], rm[:, 2:3]))
                step(dve.tensor_scalar(Bd[:, :], blk8[:, :], rm[:, 3:4], None, ALU.mult))
            step(dve.tensor_scalar(blkB[:, :], blk[:, :], rm[:, 3:4], None, ALU.mult))
            dve.wait_ge(route_act, 5)
            step(dve.tensor_tensor(t6[:, :], bank(0)[:, 0:S], lnU[:, :], ALU.subtract))
            dve.wait_ge(route_act, 6)
            step(dve.reciprocal(rm[:, 5:6], rm[:, 4:5]))
            step(dve.tensor_scalar(aff[:, :], aff[:, :], rm[:, 5:6], None, ALU.mult))
            src = aff
            for _ in range(CAP // 8):
                step(dve.max(m8[:, :], src[:, :]))
                step(dve.match_replace(out=wk[:, :], in_to_replace=m8[:, :], in_values=src[:, :], imm_value=-1.0))
                src = wk
            step(dve.tensor_scalar(wk[:, :], wk[:, :], 0.0, None, ALU.is_lt))
            step(dve.memset(lnU[:, :], 1.0))
            step(dve.tensor_tensor_scan(posn[:, :], lnU[:, :], wk[:, :], 0.0, ALU.mult, ALU.add))
            step(dve.tensor_tensor(posn[:, :], posn[:, :], wk[:, :], ALU.mult))
            dve.wait_ge(route_pe, 3 + 2 * (SINK - 2) + 1)
            pv = posB[:, :, :, :].rearrange("p n b e -> p n (b e)")
            step(dve.tensor_scalar(pv, bank(1)[:, 0:S].rearrange("p (n j) -> p n j", n=NT), 1.0, None, ALU.subtract))
            A3 = [affp[:, :, i].rearrange("p n b e -> p n (b e)") for i in range(3)]
            AB = bank(2)[:, 0:S].rearrange("p (n j) -> p n j", n=NT)
            step(dve.tensor_copy(A3[0], AB))
            step(dve.tensor_tensor(tn, AB, A3[0], ALU.subtract))
            step(dve.tensor_copy(A3[1], tn))
            step(dve.tensor_tensor(A3[2], tn, A3[1], ALU.subtract))
            assert route_dve.n == ROUTED

        @block.scalar
        def _(act):
            act.wait_ge(route_dve.sem, 2)
            act.activation(ex.rearrange("p n j -> p (n j)"), tn.rearrange("p n j -> p (n j)"), ACT.Exp).then_inc(route_act, 1)
            act.wait_ge(route_dve.sem, 3)
            act.activation(ls[:, :], ls[:, :], ACT.Ln).then_inc(route_act, 1)
            act.wait_ge(route_dve.sem, 6)
            act.activation(KA[:, :], bank(0)[:, 0:S], ACT.Exp, bias=rm[:, 1:2], accum_out=rm[:, 2:3]).then_inc(route_act, 1)
            act.wait_ge(route_pe, 2)
            act.activation(KB.rearrange("p n j -> p (n j)"), bank(3)[:, 0:S], ACT.Copy).then_inc(route_act, 1)
            act.wait_ge(route_pe, 3 + 2 * (SINK - 2))
            act.activation(lnU[:, :], bank(4)[:, 0:S], ACT.Ln).then_inc(route_act, 1)
            act.wait_ge(route_dve.sem, 26)
            act.activation(aff[:, :], t6[:, :], ACT.Exp, bias=rm[:, 1:2], accum_out=rm[:, 4:5]).then_inc(route_act, 1)

        @block.tensor
        def _(pe):
            pe.wait_ge(route_dve.sem, 4)
            for n in range(NT):
                last = transpose(pe, bank(0)[:, n * P:n * P + P], tn[:, n, :])
            last.then_inc(route_pe, 1)
            pe.wait_ge(route_act, 3)
            for n in range(NT):
                last = transpose(pe, bank(3)[:, n * P:n * P + P], KA[:, n * P:n * P + P])
            last.then_inc(route_pe, 1)
            for it in range(SINK - 2):
                pe.wait_ge(route_dve.sem, 8 + 4 * it)
                for n in range(NT):
                    last = pe.matmul(bank(1)[:, n * B:n * B + B], KA[:, n * P:n * P + P], Bd[:, :], start=True, stop=True)
                last.then_inc(route_pe, 1)
                if it == 0:
                    pe.wait_ge(route_act, 4)
                pe.wait_ge(route_dve.sem, 9 + 4 * it)
                for n in range(NT):
                    last = pe.matmul(bank(2)[:, 0:B], KB[:, n, :], ra[:, n * B:n * B + B], start=(n == 0), stop=(n == NT - 1))
                last.then_inc(route_pe, 1)
            pe.wait_ge(route_dve.sem, 25)
            pe.matmul(bank(4)[:, 0:S], blkB[:, :], KA[:, :], start=True, stop=True).then_inc(route_pe, 1)
            pe.wait_ge(route_dve.sem, 48)
            for k, t in ((1, posn), (2, aff)):
                for n in range(NT):
                    last = transpose(pe, bank(k)[:, n * P:n * P + P], t[:, n * P:n * P + P])
            last.then_inc(route_pe, 1)

        def one(t, i, n=1):
            return bass.ds(i, n) if not isinstance(i, int) else slice(i, i + n)

        w1_dram = w1.rearrange("e (k p) f -> p e k f", p=P)
        w2_dram = w2.rearrange("e (f p) d -> p e f d", p=P)

        @block.sync
        def _(sp):
            def load(e, par):
                if not (isinstance(e, int) and e == 0):
                    w1h_ready.wait(sp, e - 1, 2)
                    w1l_ready.wait(sp, e - 1, 2)
                sp.dma_start(w1r, w1_dram[:, one(w1, e)].rearrange("p a k f -> p (a k) f")).then_inc(ld_w1.sem, 16)
                if not (isinstance(e, int) and e == 0):
                    w2h_ready.wait(sp, e - 1, 2)
                    w2l_ready.wait(sp, e - 1, 2)
                sp.dma_start(w2r, w2_dram[:, one(w2, e)].rearrange("p a f d -> p (a f) d")).then_inc(ld_w2.sem, 16)
                if not (isinstance(e, int) and e < 2):
                    y_t.wait(sp, e - 2, 2)
                sp.dma_start(b2b[:, par], b2[one(b2, e)].broadcast_to([P, D])).then_inc(ld_b2.sem, 16)

            load(0, 0)
            load(1, 1)
            with sp.Fori(1, E // 2) as j:
                load(2 * j, 0)
                load(2 * j + 1, 1)
            with sp.Fori(0, B) as b:
                out_ready.wait(sp, b, 1)
                sp.dma_start(out.rearrange("b (n p) d -> p b n d", p=P)[:, one(out, b)].rearrange("p a n d -> p (a n) d"),
                             tiles(xs, b)).then_inc(stored, 16)
            sp.wait_ge(stored, 16 * B)

        @block.gpsimd
        def _(pool):
            def parts(e):
                for f in range(EF):
                    hh_ready.wait(pool, e, f + 1)
                    hl_ready.up(pool.tensor_tensor(hl[:, f, :], hf[:, f % 2, :], hh[:, f, :], ALU.subtract))

            def prepare(e, par):
                for p in range(2):
                    w2h_ready.wait(pool, e, p + 1)
                    w2l_ready.up(pool.tensor_tensor(w2l[:, par, 4 * p:4 * p + 4], w2r[:, 4 * p:4 * p + 4],
                                                    w2h[:, par, 4 * p:4 * p + 4], ALU.subtract))

            def outputs(e, par, pair):
                q = slice(64 * par, 64 * par + 64)
                if isinstance(e, int) and e == E - 1:
                    hl_ready.wait(pool, e, EF)
                else:
                    w2l_ready.wait(pool, e + 1, 2)
                for pr in range(2):
                    yh_ready.wait(pool, e, pr + 1)
                    yl_ready.up(pool.tensor_tensor(
                        YL[q, one(YL, pair), 4 * pr:4 * pr + 4, :].rearrange("p a b d -> p (a b) d"), yg[q, pr],
                        YH[q, one(YH, pair), 4 * pr:4 * pr + 4, :].rearrange("p a b d -> p (a b) d"), ALU.subtract))
                yl_ready.wait(pool, e, 2)

            prepare(0, 0)
            parts(0)
            with pool.Fori(0, E // 2 - 1) as j:
                prepare(2 * j + 1, 1)
                outputs(2 * j, 0, j)
                parts(2 * j + 1)
                prepare(2 * j + 2, 0)
                outputs(2 * j + 1, 1, j)
                parts(2 * j + 2)
            prepare(E - 1, 1)
            outputs(E - 2, 0, E // 2 - 1)
            parts(E - 1)
            outputs(E - 1, 1, E // 2 - 1)

        @block.tensor
        def _(pe):
            def gather(e, par):
                g_ready.wait(pe, e, 1)
                idx = 0
                for k in range(KT):
                    for part, src in ((0, xh), (1, xl)):
                        if idx >= 2:
                            (xgh_ready if part == 0 else xgl_ready).wait(pe, e, 1)
                        for b in range(B):
                            for n in range(NT):
                                last = pe.matmul(bank(2 + idx % 2)[:, b * CAP:(b + 1) * CAP],
                                                 src[:, b * NT + n, k * P:k * P + P], G[:, par, n * B + b, :],
                                                 start=(n == 0), stop=(n == NT - 1))
                        g_mm2.up(last)
                        idx += 1
                if not (isinstance(e, int) and e == 0):
                    gt_ready.wait(pe, e - 1, 2)
                for t in range(4):
                    for n in range(NT):
                        last = pe.matmul(bank(6)[:, t * 8:t * 8 + 6],
                                         G[:, par, n * B + 2 * t:n * B + 2 * t + 2, :].rearrange("p b c -> p (b c)"),
                                         affp[:, n, :, 2 * t:2 * t + 2, one(affp, e)].rearrange("p i b a -> p i (b a)"),
                                         start=(n == 0), stop=(n == NT - 1))
                g_mm2.up(last)

            def expert(e, par, ahead, pair=0):
                xgh_ready.wait(pe, e, 2)
                xgl_ready.wait(pe, e, 2)
                w1h_ready.wait(pe, e, 2)
                w1l_ready.wait(pe, e, 2)
                for f in range(EF):
                    if f >= 2:
                        gelu_ready.wait(pe, e, f - 1)
                    first = True
                    for wp, xp in ((w1h, xgh), (w1h, xgl), (w1l, xgh)):
                        for k in range(KT):
                            last = pe.matmul(bank(f % 2), wp[:, par, k, f * P:f * P + P], xp[:, par, k, :],
                                             start=first, stop=(wp is w1l and k == KT - 1))
                            first = False
                    m1_mm.up(last)
                if ahead:
                    gather(e + 1, 1 - par)
                hl_ready.wait(pe, e, EF)
                w2h_ready.wait(pe, e, 2)
                w2l_ready.wait(pe, e, 2)
                for t in range(4):
                    if t % 2 == 0 and not (isinstance(e, int) and e == 0):
                        y_t.wait(pe, e - 1, t // 2 + 1)
                    for f in range(EF):
                        for hp, wp in ((hh, w2h), (hh, w2l), (hl, w2h)):
                            last = pe.matmul(bank(4 + t // 2)[:, (t % 2) * D:(t % 2) * D + D],
                                             hp[:, f, t * P:t * P + P], wp[:, par, f, :],
                                             start=(f == 0 and wp is w2h and hp is hh),
                                             stop=(f == EF - 1 and hp is hl))
                    if t % 2:
                        m2_mm.up(last)

            gather(0, 0)
            expert(0, 0, True)
            with pe.Fori(0, E // 2 - 1) as j:
                expert(2 * j + 1, 1, True, j)
                expert(2 * j + 2, 0, True, j + 1)
            expert(E - 1, 1, False, E // 2 - 1)

            def places(b, par):
                for n in range(NT):
                    gs_ready.wait(pe, b, n + 1)
                    for r in range(E // 2):
                        last = pe.transpose(psb(2 * par + n)[:, r * P:r * P + P],
                                            Gs[:, par, n, 2 * r:2 * r + 2, :].rearrange("p e c -> p (e c)"), identb[:, :])
                    gst_mm.up(last)

            def combine(b, par):
                for n in range(NT):
                    (gt2_act, gt2_dve)[n].wait(pe, b, 1)
                    for r in range(E // 2):
                        for Y in (YH, YL):
                            last = pe.matmul(bank(4 + par)[:, n * D:n * D + D], GT[:, par, n, r, :],
                                             Y[:, r, one(Y, b), :].rearrange("p a d -> p (a d)"),
                                             start=(r == 0 and Y is YH), stop=(r == E // 2 - 1 and Y is YL))
                c_mm.up(last)

            places(0, 0)
            yl_ready.wait(pe, E - 1, 2)
            with pe.Fori(0, B // 2 - 1) as j:
                places(2 * j + 1, 1)
                combine(2 * j, 0)
                places(2 * j + 2, 0)
                combine(2 * j + 1, 1)
            places(B - 1, 1)
            combine(B - 2, 0)
            combine(B - 1, 1)

        @block.vector
        def _(dve):
            def onehot(e, par):
                if not (isinstance(e, int) and e < 2):
                    g_mm2.wait(dve, e - 2, 5)
                g_ready.up(dve.tensor_tensor(
                    G[:, par], posB[:, :, :, one(posB, e)].rearrange("p n b a -> p (n b) a").broadcast_to([P, NT * B, CAP]),
                    iota_c[:, :].unsqueeze(1).broadcast_to([P, NT * B, CAP]), ALU.is_equal))

            def onehots_of_batch(b, par):
                for n in range(NT):
                    gs_ready.up(dve.tensor_tensor(
                        Gs[:, par, n], posB[:, n, one(posB, b)].rearrange("p a e -> p (a e)").unsqueeze(2).broadcast_to([P, E, CAP]),
                        iota_c[:, :].unsqueeze(1).broadcast_to([P, E, CAP]), ALU.is_equal))

            def prepare(e, par, piece):
                if piece == 0:
                    ld_w1.wait(dve, e, 16)
                if piece < 2:
                    w1h_ready.wait(dve, e, piece + 1)
                    w1l_ready.up(dve.tensor_tensor(w1l[:, par, piece], w1r[:, piece], w1h[:, par, piece], ALU.subtract))
                elif piece == 2:
                    onehot(e, par)

            def gathered(e, par):
                for k in range(KT):
                    g_mm2.wait(dve, e, 2 * k + 2)
                    xgl_ready.up(dve.tensor_copy(xgl[:, par, k, :], bank(3)))
                g_mm2.wait(dve, e, 5)
                gv = bank(6)[:, 0:32].rearrange("p (t i b) -> p t i b", t=4, b=2)
                for half in range(2):
                    q = slice(64 * half, 64 * half + 64)
                    gt_ready.up(dve.tensor_reduce(gt[q, par, :], gv[q, :, 0:3, half], AX.X, ALU.add))

            def expert(e, par, ahead, pair=0):
                for f in range(EF):
                    gelu_ready.wait(dve, e, f + 1)
                    hh_ready.up(dve.tensor_copy(hh[:, f, :], hf[:, f % 2, :]))
                    if ahead and f % 2 == 1:
                        prepare(e + 1, 1 - par, f // 2)
                if ahead:
                    gathered(e + 1, 1 - par)
                ld_b2.wait(dve, e, 16)
                for pr in range(2):
                    m2_mm.wait(dve, e, pr + 1)
                    y_t.up(dve.tensor_tensor(yt[:, pr], bank(4 + pr).rearrange("p (t d) -> p t d", t=2),
                                             b2b[:, par].unsqueeze(1).broadcast_to([P, 2, D]), ALU.add))
                    yg_ready.wait(dve, e, 4 * pr + 4)
                    q = slice(64 * par, 64 * par + 64)
                    yh_ready.up(dve.tensor_scalar(
                        YH[q, one(YH, pair), 4 * pr:4 * pr + 4, :].rearrange("p a b d -> p (a b) d"), yg[q, pr],
                        1.0, None, ALU.mult))

            for piece in range(4):
                prepare(0, 0, piece)
            gathered(0, 0)
            expert(0, 0, True)
            with dve.Fori(0, E // 2 - 1) as j:
                expert(2 * j + 1, 1, True, j)
                expert(2 * j + 2, 0, True, j + 1)
            expert(E - 1, 1, False, E // 2 - 1)
            def places(b, par):
                onehots_of_batch(b, par)
                gst_mm.wait(dve, b, 2)
                gt2_dve.up(dve.tensor_copy(GT[:, par, 1].rearrange("p r q -> p (r q)"), psb(2 * par + 1)))

            def finish(b, par):
                c_mm.wait(dve, b, 1)
                xb = tiles(xs, b)
                out_ready.up(dve.scalar_tensor_tensor(
                    out=xb, in0=bank(4 + par).rearrange("p (n d) -> p n d", n=NT), scalar=gates4[:, 3:4], in1=xb,
                    op0=ALU.mult, op1=ALU.add))

            places(0, 0)
            with dve.Fori(0, B // 2 - 1) as j:
                places(2 * j + 1, 1)
                finish(2 * j, 0)
                places(2 * j + 2, 0)
                finish(2 * j + 1, 1)
            places(B - 1, 1)
            finish(B - 2, 0)
            finish(B - 1, 1)

        @block.scalar
        def _(act):
            def prepare(e, par, piece):
                if piece == 0:
                    ld_w1.wait(act, e, 16)
                if piece == 2:
                    ld_w2.wait(act, e, 16)
                if piece < 2:
                    w1h_ready.up(act.activation(w1h[:, par, piece], w1r[:, piece], ACT.Copy))
                else:
                    p = piece - 2
                    w2h_ready.up(act.activation(w2h[:, par, 4 * p:4 * p + 4], w2r[:, 4 * p:4 * p + 4], ACT.Copy))

            def gathered(e, par):
                for k in range(KT):
                    g_mm2.wait(act, e, 2 * k + 1)
                    xgh_ready.up(act.activation(xgh[:, par, k, :], bank(2), ACT.Copy))

            def expert(e, par, ahead, pair=0):
                for f in range(EF):
                    m1_mm.wait(act, e, f + 1)
                    if f >= 2:
                        hl_ready.wait(act, e, f - 1)
                    gelu_ready.up(act.activation(hf[:, f % 2, :], bank(f % 2), ACT.Gelu_apprx_tanh,
                                                 bias=b1T[:, f, one(b1T, e)]))
                    if ahead and f % 2 == 0:
                        prepare(e + 1, 1 - par, f // 2)
                if ahead:
                    gathered(e + 1, 1 - par)
                for pr in range(2):
                    y_t.wait(act, e, pr + 1)
                    if not (isinstance(e, int) and e == 0):
                        yl_ready.wait(act, e - 1, pr + 1)
                    for i in range(4):
                        t, half = 2 * pr + i // 2, i % 2
                        q, o = slice(64 * half, 64 * half + 64), slice(64 * par, 64 * par + 64)
                        yg_ready.up(act.activation(yg[o, pr, i, :], yt[q, pr, i // 2, :], ACT.Copy,
                                                   scale=gt[q, par, t:t + 1]))

            for piece in range(4):
                prepare(0, 0, piece)
            gathered(0, 0)
            expert(0, 0, True)
            with act.Fori(0, E // 2 - 1) as j:
                expert(2 * j + 1, 1, True, j)
                expert(2 * j + 2, 0, True, j + 1)
            expert(E - 1, 1, False, E // 2 - 1)
            def places(b, par):
                gst_mm.wait(act, b, 1)
                gt2_act.up(act.activation(GT[:, par, 0].rearrange("p r q -> p (r q)"), psb(2 * par), ACT.Copy))

            places(0, 0)
            with act.Fori(0, B // 2 - 1) as j:
                places(2 * j + 1, 1)
                places(2 * j + 2, 0)
            places(B - 1, 1)


_INS = ["x", "ctx_1024", "mask_SxS2_fk0", "g_xattn", "g_ffn", "L0_xattn_Wq", "L0_xattn_Wkv", "L0_xattn_Wout",
        "L0_ffn_W_fc", "L0_ffn_b_fc", "L0_ffn_A_fc", "L0_ffn_B_fc", "L0_ffn_W_proj", "L0_ffn_b_proj",
        "L0_ffn_A_proj", "L0_ffn_B_proj", "L1_xattn_Wq", "L1_xattn_Wkv", "L1_ffn_gate_query", "L1_ffn_log_temp",
        "L1_ffn_w1", "L1_ffn_b1", "L1_ffn_w2", "L1_ffn_b2"]


def kernel(**inputs):
    import numpy as np
    import concourse.bacc as bacc
    from concourse.bass_utils import run_bass_kernel_spmd

    nc = bacc.Bacc("TRN2", target_bir_lowering=False, num_devices=1)
    arrays, args = {}, []
    for name in _INS:
        a = np.ascontiguousarray(inputs[name])
        a = a.reshape(a.shape or (1,))
        arrays[f"in_{name}"] = a
        args.append(nc.dram_tensor(f"in_{name}", a.shape, mybir.dt.from_np(a.dtype), kind="ExternalInput").ap())
    shape = inputs["x"].shape
    args.append(nc.dram_tensor("out_0", shape, F32, kind="ExternalOutput").ap())
    build(nc, *args)
    r = run_bass_kernel_spmd(nc, [arrays], core_ids=[0])
    return r.results[0]["out_0"]
```

```python
from contextlib import ExitStack

import concourse.bass as bass
from concourse import mybir

F32 = mybir.dt.float32
BF16 = mybir.dt.bfloat16
I32 = mybir.dt.int32
ALU = mybir.AluOpType
ACT = mybir.ActivationFunctionType
AX = mybir.AxisListType

P = 128
EPS = 1e-5
ROUND = 12582912.0


class Sig:

    def __init__(self, sem, per=0):
        self.sem, self.per, self.n = sem, per, 0

    def up(self, ins):
        self.n += 1
        ins.then_inc(self.sem, 1)

    def wait(self, eng, b, k):
        eng.wait_ge(self.sem, b * self.per + k)


def build(nc, x, ctx_1024, mask, g_xattn, g_ffn, wq0, wkv0, wout0, w_fc, b_fc, a_fc, bb_fc, w_proj, b_proj,
          a_proj, bb_proj, wq1, wkv1, gate_query, log_temp, w1, b1, w2, b2, out):
    B, S, D = x.shape
    C = ctx_1024.shape[1]
    H, A = 16, D // 16
    FF = w_fc.shape[0]
    E, _, DFF = w1.shape
    R = a_fc.shape[0]
    CAP = 64
    NT, KT, FT = S // P, D // P, FF // P
    T = B * NT
    EF = DFF // P
    ISQ = 1.0 / 16.0
    SINK = 6
    assert B * E == P and D == 256 and FF == DFF == 1024

    with ExitStack() as cx:
        def sb(name, shape, dt=F32):
            return cx.enter_context(nc.sbuf_tensor(name, shape, dt))

        def sem(name):
            return cx.enter_context(nc.semaphore(name))

        ident = sb("ident", [P, P])
        blk8 = sb("blk8", [P, B])
        blk = sb("blk", [P, P])
        iota_c = sb("iota_c", [P, CAP])
        iota_i = sb("iota_i", [P, CAP], I32)
        identb = sb("identb", [P, P], BF16)
        posB = sb("posB", [P, NT, B, E])
        affp = sb("affp", [P, NT, 3, B, E], BF16)
        G = sb("G", [P, 2, NT * B, CAP], BF16)
        gt = sb("gt", [P, 2, 4])
        rm = sb("rm", [P, 8])
        scratch = sb("scratch", [P, 1])
        mhalf = sb("mhalf", [P, NT])
        Bd = sb("Bd", [P, B])
        ra = sb("ra", [P, NT * B])
        vt = sb("vt", [P, B])
        m8 = sb("m8", [P, 8])
        xs = sb("xs", [P, T, D])
        gates4 = sb("gates4", [P, 4])
        xh = sb("xh", [P, T, D], BF16)
        xl = sb("xl", [P, T, D], BF16)
        tlog = sb("tlog", [P, NT, B, E])
        b1T = sb("b1T", [P, EF, E])

        ARENA = 41984
        arena = sb("arena", [P, ARENA])
        at = [0]

        def carve(shape, dt=F32):
            n = 1
            for s in shape:
                n *= s
            words = n if dt != BF16 else (n + 1) // 2
            v = arena[:, at[0]:at[0] + words]
            at[0] += words
            assert at[0] <= ARENA, at[0]
            if dt != F32:
                v = v.bitcast(dt)
            names = "abcdef"[:len(shape)]
            if len(shape) == 1:
                return v
            return v.rearrange(f"p ({' '.join(names)}) -> p {' '.join(names)}",
                               **{c: s for c, s in zip(names, shape)})

        ctxn = carve([B, D])
        maskr = carve([NT, C])
        wnat = carve([2 + 4 + 2, D])
        wfn = carve([FT, D])
        wpn_at = at[0]
        wpn = carve([KT, FF])
        wq1s = carve([KT, D])
        wkv1s = carve([KT, 2 * D])
        afc = carve([D])
        apj = carve([FF])
        bfn = carve([FT, R])
        bpn = carve([KT, R])
        gqn = carve([D])
        bfT = carve([FF])
        bpT = carve([D])
        w0T = carve([KT, 8 * P])
        W1T = carve([KT, FF])
        W2T = carve([FT, D])
        ctxT = carve([KT, B * C])
        k0T = carve([KT, B * C])
        k1T = carve([KT, B * C])
        V0 = carve([B, H, A + 1])
        V1 = carve([B, D])
        gqT = carve([KT, E])
        bfcT = carve([FT])
        b8n = carve([P])
        b1n = carve([DFF])
        bpb = carve([D])
        ltb = carve([1])
        wmx = carve([2])
        wsc = carve([4, 2])
        dense_end = at[0]

        LNS = ("attn0", "ffn0", "attn1", "ffn1")

        def norm_buffers():
            return carve([NT, D]), carve([KT, S]), carve([NT, 6]), carve([NT, 2]), carve([NT]), carve([NT])

        buf_a = norm_buffers()
        qT = carve([KT, S])
        kbd = wnat.rearrange("p j d -> p (j d)")[:, 0:KT * 8 * C].rearrange("p (k h c) -> p k h c", k=KT, h=8)
        Tb = carve([2, 4, C])
        Eb = carve([2, 4, C])
        mx = carve([2, 4])
        PT = carve([2, 4, P])
        rden = carve([H])
        att = carve([NT, D])
        hT = wfn
        nm1 = carve([NT])
        sm1 = carve([NT])
        ri1 = carve([NT])
        here, at[0] = at[0], wpn_at
        buf_b = norm_buffers()
        qTb = carve([KT, S])
        assert at[0] <= wpn_at + KT * FF
        at[0] = 0
        E1 = carve([NT, C])
        PT1 = carve([NT, P])
        assert at[0] <= B * D
        at[0] = here
        assert at[0] <= ARENA, at[0]

        ps = cx.enter_context(nc.psum_tensor("ps", [P, 8, 512], F32))


        def bank(n, words=512):
            return ps[:, n, 0:words]

        ld_misc, ld_w, ld_ffn, ld_x = sem("ld_misc"), sem("ld_w"), sem("ld_ffn"), sem("ld_x")
        const_ready = sem("const_ready")
        consts_made = sem("consts_made")
        absmax_ready, allmax_ready, quant_step = sem("absmax_ready"), sem("allmax_ready"), sem("quant_step")
        prep_mm, prep_ev = sem("prep_mm"), sem("prep_ev")
        gate_act = sem("gate_act")

        def sig(name, per):
            return Sig(sem(name), per)

        ln_dve = [sig(f"ln_dve_{n}", 7) for n in LNS]
        rstd_ready = [sig(f"rstd_{n}", 1) for n in LNS]
        xT_mm = [sig(f"xT_mm_{n}", 1) for n in LNS]
        xT_ready = [sig(f"xT_ready_{n}", 1) for n in LNS]
        kbd_ready = sig("kbd_ready", 2)
        q_mm, q_ready = sig("q_mm", 1), sig("q_ready", 1)
        s_mm, s_masked, s_max, s_sub, s_exp = (sig(n, 8) for n in ("s_mm", "s_masked", "s_max", "s_sub", "s_exp"))
        pT_mm, pT_ready, av_mm = sig("pT_mm", 8), sig("pT_ready", 8), sig("av_mm", 8)
        att_ready = sig("att_ready", 4)
        attT_mm, attT_ready, wo_mm, x_attn0 = sig("attT_mm", 1), sig("attT_ready", 1), sig("wo_mm", 1), sig("x_attn0", 1)
        h_mm, h_ready, f_mm, x_ffn0 = sig("h_mm", 4), sig("h_ready", 8), sig("f_mm", 1), sig("x_ffn0", 2)
        q1_mm, q1_ready, s1_mm, m1_ready, e1_ready = (sig(n, p) for n, p in (
            ("q1_mm", 1), ("q1_ready", 1), ("s1_mm", 1), ("m1_ready", 2), ("e1_ready", 2)))
        p1T_mm, p1T_ready, av1_mm, r1_ready, x_attn1 = (sig(n, p) for n, p in (
            ("p1T_mm", 1), ("p1T_ready", 1), ("av1_mm", 1), ("r1_ready", 2), ("x_attn1", 2)))
        xh_ready, xl_ready, g_mm, t_ready = (sig(n, 1) for n in ("xh_ready", "xl_ready", "g_mm", "t_ready"))

        N_MISC, N_W, N_FFN, N_X = 8, 6, 6, 4
        CONSTS = 12
        EV_K0 = 13

        route_dve, route_act, route_pe = Sig(sem("route_dve")), sem("route_act"), sem("route_pe")
        ROUTED = 53
        stored = sem("stored")
        ld_w1, ld_w2, ld_b2 = sig("ld_w1", 16), sig("ld_w2", 16), sig("ld_b2", 16)
        w1h_ready, w1l_ready, w2h_ready, w2l_ready = (sig(n, 2) for n in ("w1h_ready", "w1l_ready", "w2h_ready", "w2l_ready"))
        g_ready, g_mm2, xgh_ready, xgl_ready, gt_ready = (sig(n, p) for n, p in (
            ("g_ready", 1), ("g_mm2", 5), ("xgh_ready", 2), ("xgl_ready", 2), ("gt_ready", 2)))
        m1_mm, gelu_ready, hh_ready, hl_ready = (sig(n, EF) for n in ("m1_mm", "gelu_ready", "hh_ready", "hl_ready"))
        m2_mm, y_t, yh_ready, yl_ready = sig("m2_mm", 2), sig("y_t", 2), sig("yh_ready", 2), sig("yl_ready", 2)
        yg_ready = sig("yg_ready", 8)
        gs_ready, gst_mm = (sig(n, NT) for n in ("gs_ready", "gst_mm"))
        gt2_act, gt2_dve = (sig(n, 1) for n in ("gt2_act", "gt2_dve"))
        c_mm, out_ready = sig("c_mm", 1), sig("out_ready", 1)

        def psb(n):
            return ps[:, n, :].bitcast(BF16)

        at[0] = 0
        YH, YL = [carve([E // 2, B, D], BF16) for _ in range(2)]
        w1h_at = at[0]
        w1h, w1l = [carve([2, KT, DFF], BF16) for _ in range(2)]
        w2h, w2l = [carve([2, EF, D], BF16) for _ in range(2)]
        xgh, xgl = [carve([2, KT, B * CAP], BF16) for _ in range(2)]
        hh, hl = [carve([EF, B * CAP], BF16) for _ in range(2)]
        hf = carve([2, B * CAP])
        yt = carve([2, 2, D])
        yg = carve([2, 4, D])
        experts_end = at[0]
        at[0] = w1h_at
        GT = carve([2, NT, E // 2, P], BF16)
        Gs = carve([2, NT, E, CAP], BF16)
        assert at[0] <= w1h_at + 8192
        at[0] = 0
        ls = carve([NT * B])
        mxe = carve([NT * B])
        tn = carve([NT, B * E])
        ex = carve([NT, B * E])
        KA = carve([S])
        KB = carve([NT, P])
        lnU = carve([S])
        t6 = carve([S])
        aff = carve([S])
        wk = carve([S])
        posn = carve([S])
        blkB = carve([P])
        assert at[0] <= w1h_at and experts_end <= ARENA - 4096 - 512, (at[0], experts_end)
        w1r, w2r, b2b = (arena[:, ARENA - o:ARENA - o + w] for o, w in ((4608, 2048), (2560, 2048), (512, 512)))
        w1r = w1r.rearrange("p (k f) -> p k f", k=KT)
        w2r = w2r.rearrange("p (f d) -> p f d", f=EF)
        b2b = b2b.rearrange("p (a d) -> p a d", a=2)

        block = cx.enter_context(nc.Block())

        @block.sync
        def _(sp):
            def ld(dst, src, s):
                sp.dma_start(dst, src).then_inc(s, 16)

            xv = x.rearrange("b (n p) d -> p (b n) d", p=P)
            ld(ctxn[0:C], ctx_1024.rearrange("b c d -> c b d"), ld_w)
            ld(wnat[:, 0:2], wq0.rearrange("(j p) d -> p j d", p=P), ld_w)
            ld(wnat[:, 2:6], wkv0.rearrange("(j p) d -> p j d", p=P), ld_w)
            ld(wnat[:, 6:8], wout0.rearrange("(j p) d -> p j d", p=P), ld_w)
            ld(wq1s, wq1.rearrange("(k p) n -> p k n", p=P), ld_w)
            ld(wkv1s, wkv1.rearrange("(k p) n -> p k n", p=P), ld_w)
            ld(wfn, w_fc.rearrange("(j p) d -> p j d", p=P), ld_ffn)
            ld(wpn, w_proj.rearrange("(j p) d -> p j d", p=P), ld_ffn)
            ld(bfn, bb_fc.rearrange("(j p) r -> p j r", p=P), ld_ffn)
            ld(bpn, bb_proj.rearrange("(j p) r -> p j r", p=P), ld_ffn)
            ld(afc[0:R], a_fc, ld_ffn)
            ld(apj[0:R], a_proj, ld_ffn)
            for q in range(4):
                ld(xs[:, 4 * q:4 * q + 4, :], xv[:, 4 * q:4 * q + 4, :], ld_x)
            ld(maskr, mask.rearrange("(n p) c -> p n c", p=P), ld_misc)
            ld(gqn[0:E], gate_query, ld_misc)
            ld(b8n[0:FT], b_fc.rearrange("(j p) -> j p", p=P), ld_misc)
            ld(b1n[0:E], b1, ld_misc)
            ld(bpb, b_proj.rearrange("(a d) -> a d", a=1).broadcast_to([P, D]), ld_misc)
            ld(ltb, log_temp.rearrange("(a d) -> a d", a=1).broadcast_to([P, 1]), ld_misc)
            ld(gates4[:, 0:2], g_xattn.rearrange("(a d) -> a d", a=1).broadcast_to([P, 2]), ld_misc)
            ld(gates4[:, 2:4], g_ffn.rearrange("(a d) -> a d", a=1).broadcast_to([P, 2]), ld_misc)

        def run(eng, iteration, prologue=None):
            iteration(eng, 0, first=True, rest=False, ahead=True)
            with eng.Fori(1, B - 1) as i:
                iteration(eng, i, first=True, rest=True, ahead=True)
            iteration(eng, B - 1, first=True, rest=True, ahead=False)
            iteration(eng, B, first=False, rest=True, ahead=False)

        def pool_rstd(pool, L, b):
            _, _, _, _, vpe, y0 = buf_a if L == 0 else buf_b
            ln_dve[L].wait(pool, b, 5)
            rstd_ready[L].up(pool.tensor_tensor(y0, vpe, mhalf[:, :], ALU.pow))

        def pool_keys(pool, b):
            for m in range(KT):
                kb = k0T[:, m, bass.ds(b * C, C)] if not isinstance(b, int) else k0T[:, m, b * C:b * C + C]
                kbd_ready.up(pool.tensor_tensor(kbd[:, m], kb.unsqueeze(1).broadcast_to([P, 8, C]),
                                                blk8[:, :].unsqueeze(2).broadcast_to([P, 8, C]), ALU.mult))

        def pool_iteration(pool, i, first, rest, ahead):
            def sub(s):
                if first:
                    s_max.wait(pool, i, s + 1)
                    s_sub.up(pool.tensor_tensor(Tb[:, s % 2], Tb[:, s % 2],
                                                mx[:, s % 2].unsqueeze(2).broadcast_to([P, 4, C]), ALU.subtract))

            if rest:
                pool_rstd(pool, 1, i - 1)
            for s in range(6):
                sub(s)
            if rest:
                pool_rstd(pool, 2, i - 1)
            sub(6)
            sub(7)
            if ahead:
                pool_rstd(pool, 0, i + 1)
                pool_keys(pool, i + 1)
            if rest:
                pool_rstd(pool, 3, i - 1)
                ln_dve[3].wait(pool, i - 1, 7)
                xh_ready.up(pool.tensor_copy(tiles(xh, i - 1), buf_b[0]))

        def tiles(t, b):
            return t[:, bass.ds(b * NT, NT), :] if not isinstance(b, int) else t[:, b * NT:b * NT + NT, :]

        @block.gpsimd
        def _(pool):
            pool.memset(ident[:, :], 0.0).then_inc(consts_made, 1)
            pool.memset(blk8[:, :], 1.0).then_inc(consts_made, 1)
            pool.memset(blk[:, :], 1.0).then_inc(consts_made, 1)
            pool.iota(iota_i[:, :], [[1, CAP]], base=0, channel_multiplier=0).then_inc(consts_made, 1)
            pool.memset(mhalf[:, :], -0.5).then_inc(consts_made, 1)
            pool.wait_ge(consts_made, 5)
            pool.affine_select(out=ident[:, :], in_=ident[:, :], compare_op=ALU.not_equal, fill=1.0,
                               base=0, pattern=[[-1, P]], channel_multiplier=1).then_inc(consts_made, 1)
            pool.affine_select(out=blk8[:, :], in_=blk8[:, :], compare_op=ALU.is_ge, fill=0.0,
                               base=0, pattern=[[-E, B]], channel_multiplier=1).then_inc(consts_made, 1)
            pool.affine_select(out=blk[:, :], in_=blk[:, :], compare_op=ALU.is_ge, fill=0.0,
                               base=0, pattern=[[-E, B], [0, E]], channel_multiplier=1).then_inc(consts_made, 1)
            pool.tensor_copy(iota_c[:, :], iota_i[:, :]).then_inc(consts_made, 1)
            pool.wait_ge(consts_made, 6)
            pool.tensor_copy(identb[:, :], ident[:, :]).then_inc(consts_made, 1)
            pool.wait_ge(consts_made, 10)
            pool.affine_select(out=blk8[:, :], in_=blk8[:, :], compare_op=ALU.is_ge, fill=0.0,
                               base=E - 1, pattern=[[E, B]], channel_multiplier=-1).then_inc(consts_made, 1)
            pool.affine_select(out=blk[:, :], in_=blk[:, :], compare_op=ALU.is_ge, fill=0.0,
                               base=E - 1, pattern=[[E, B], [0, E]], channel_multiplier=-1).then_inc(consts_made, 1)
            pool.wait_ge(consts_made, CONSTS)
            pool.wait_ge(absmax_ready, 2)
            pool.partition_all_reduce(wsc[:, 0], wmx[:, :], P, bass.bass_isa.ReduceOp.max).then_inc(allmax_ready, 1)
            pool.wait_ge(prep_ev, EV_K0)
            pool_rstd(pool, 0, 0)
            pool_keys(pool, 0)
            run(pool, pool_iteration)

        def transpose(pe, dst, src, parts=P):
            return pe.transpose(dst, src, ident[0:parts, 0:parts])

        def pe_transposed(pe, L, b):
            xn = (buf_a if L == 0 else buf_b)[0]
            ln_dve[L].wait(pe, b, 7)
            for k in range(KT):
                for n in range(NT):
                    last = transpose(pe, bank(0 if L == 0 else 5)[:, k * S + n * P:k * S + n * P + P],
                                     xn[:, n, k * P:k * P + P])
            xT_mm[L].up(last)

        def project(pe, to, w, wcol, xT):
            for m in range(KT):
                for k in range(KT):
                    last = pe.matmul(bank(to)[:, m * S:m * S + S], w[:, k, wcol + m * P:wcol + m * P + P], xT[:, k, :],
                                     start=(k == 0), stop=(k == KT - 1))
            return last

        def col(t, k, b):
            return t[:, k, bass.ds(b * C, C)] if not isinstance(b, int) else t[:, k, b * C:b * C + C]

        def at_batch(t, b):
            return t[:, bass.ds(b, 1)] if not isinstance(b, int) else t[:, b:b + 1]

        def pe_queries(pe, b):
            xT_ready[0].wait(pe, b, 1)
            q_mm.up(project(pe, 0, w0T, 0, buf_a[1]))

        def pe_iteration(pe, i, first, rest, ahead):
            b, p = i, i - 1
            xT, xTb = buf_a[1], buf_b[1]

            def scores(s):
                n, g = s // 4, s % 4
                if s >= 2:
                    s_masked.wait(pe, b, s - 1)
                s_mm.up(pe.matmul(bank(1 + s % 2, 4 * C), qT[:, g // 2, n * P:n * P + P],
                                  kbd[:, g // 2, 4 * (g % 2):4 * (g % 2) + 4, :], start=True, stop=True))

            def weighted(s):
                n, g = s // 4, s % 4
                pT_ready.wait(pe, b, s + 1)
                if s == 4:
                    att_ready.wait(pe, b, 2)
                for h in range(4):
                    hh = 4 * g + h
                    last = pe.matmul(bank(4)[:, hh * (A + 1):(hh + 1) * (A + 1)], PT[0:C, s % 2, h, :],
                                     at_batch(V0, b)[0:C, :, hh, :].rearrange("p a c -> p (a c)"),
                                     start=True, stop=True)
                av_mm.up(last)

            def step(s):
                if not first:
                    return
                s_exp.wait(pe, b, s + 1)
                if s >= 1:
                    pT_ready.wait(pe, b, s)
                for h in range(4):
                    last = transpose(pe, bank(3)[0:C, h * P:h * P + P], Eb[:, s % 2, h, :])
                pT_mm.up(last)
                if s + 2 < 8:
                    scores(s + 2)
                if s >= 1:
                    weighted(s - 1)

            def ffn_out(n, fs):
                h_ready.wait(pe, p, FT)
                for f in fs:
                    last = pe.matmul(bank(5)[:, n * D:n * D + D], hT[:, f, n * P:n * P + P], W2T[:, f, :],
                                     start=(f == 0), stop=(f == FT - 1))
                return last

            if first:
                q_ready.wait(pe, b, 1)
                kbd_ready.wait(pe, b, 2)
                scores(0)
                scores(1)
            if rest:
                pe_transposed(pe, 1, p)
                xT_ready[1].wait(pe, p, 1)
                for j in range(4):
                    if j >= 2:
                        h_ready.wait(pe, p, 2 * j - 2)
                    for f in (2 * j, 2 * j + 1):
                        for k in range(KT):
                            last = pe.matmul(bank(6 + j % 2)[:, (f % 2) * S:(f % 2) * S + S],
                                             W1T[:, k, f * P:f * P + P], xTb[:, k, :],
                                             start=(k == 0), stop=(k == KT - 1))
                    h_mm.up(last)
            for s in range(4):
                step(s)
                if rest:
                    last = ffn_out(s // 2, range(4 * (s % 2), 4 * (s % 2) + 4))
            if rest:
                f_mm.up(last)
            step(4)
            step(5)
            if rest:
                pe_transposed(pe, 2, p)
            step(6)
            if rest:
                xT_ready[2].wait(pe, p, 1)
                q1_mm.up(project(pe, 6, wq1s, 0, xTb))
            if ahead:
                pe_transposed(pe, 0, i + 1)
            step(7)
            if rest:
                q1_ready.wait(pe, p, 1)
                for n in range(NT):
                    for k in range(KT):
                        last = pe.matmul(bank(7)[:, n * C:n * C + C], qTb[:, k, n * P:n * P + P], col(k1T, k, p),
                                         start=(k == 0), stop=(k == KT - 1))
                s1_mm.up(last)
            if ahead:
                pe_queries(pe, i + 1)
            if first:
                weighted(7)
            if rest:
                e1_ready.wait(pe, p, 2)
                for n in range(NT):
                    last = transpose(pe, bank(5)[0:C, n * P:n * P + P], E1[:, n, :])
                p1T_mm.up(last)
            if first:
                att_ready.wait(pe, b, 4)
                if ahead:
                    q_ready.wait(pe, i + 1, 1)
                for k in range(KT):
                    for n in range(NT):
                        last = transpose(pe, bank(0)[:, k * S + n * P:k * S + n * P + P], att[:, n, k * P:k * P + P])
                attT_mm.up(last)
            if rest:
                p1T_ready.wait(pe, p, 1)
                for n in range(NT):
                    last = pe.matmul(bank(6)[:, n * D:n * D + D], PT1[0:C, n, :],
                                     at_batch(V1, p)[0:C].rearrange("p a d -> p (a d)"), start=True, stop=True)
                av1_mm.up(last)
            if first:
                attT_ready.wait(pe, b, 1)
                for n in range(NT):
                    for k in range(KT):
                        last = pe.matmul(bank(0)[:, n * D:n * D + D], xT[:, k, n * P:n * P + P], w0T[:, k, 6 * P:8 * P],
                                         start=(k == 0), stop=(k == KT - 1))
                wo_mm.up(last)
            if rest:
                pe_transposed(pe, 3, p)
                xT_ready[3].wait(pe, p, 1)
                for n in range(NT):
                    for k in range(KT):
                        last = pe.matmul(bank(7)[:, n * E:n * E + E], xTb[:, k, n * P:n * P + P], gqT[:, k, :],
                                         start=(k == 0), stop=(k == KT - 1))
                g_mm.up(last)

        def pe_prep(pe):
            n = [0]

            def group():
                if n[0] >= 8:
                    pe.wait_ge(prep_ev, n[0] - 7)
                n[0] += 1
                return (n[0] - 1) % 8

            def done(last):
                last.then_inc(prep_mm, 1)

            def put(g, c0, src, parts):
                w = src.shape[-1]
                return transpose(pe, bank(g)[0:w, c0:c0 + parts], src, parts)

            pe.wait_ge(consts_made, CONSTS)
            pe.wait_ge(ld_w, 16 * N_W)
            for k in range(KT):
                for jh in range(2):
                    g = group()
                    for j in range(4):
                        last = put(g, j * P, wnat[:, 4 * jh + j, k * P:k * P + P], P)
                    done(last)
            for k in range(KT):
                for bh in range(2):
                    g = group()
                    for j in range(4):
                        last = put(g, j * C, ctxn[0:C, 4 * bh + j, k * P:k * P + P], C)
                    done(last)
            pe.wait_ge(ld_misc, 16 * N_MISC)
            g = group()
            put(g, 0, b8n[0:FT, :], FT)
            for k in range(KT):
                put(g, 16 + k * E, gqn[0:E, k * P:k * P + P], E)
            for j in range(EF):
                last = put(g, 64 + j * E, b1n[0:E, j * P:j * P + P], E)
            done(last)
            pe.wait_ge(prep_ev, 8)
            for m in range(KT):
                for half in range(2):
                    g = group()
                    for k in range(KT):
                        last = pe.matmul(bank(g, 4 * C), w0T[:, k, D + m * P:D + m * P + P],
                                         ctxT[:, k, half * 4 * C:(half + 1) * 4 * C], start=(k == 0), stop=(k == 1))
                    done(last)
            for m in range(KT):
                for half in range(2):
                    g = group()
                    for k in range(KT):
                        last = pe.matmul(bank(g, 4 * C), wkv1s[:, k, m * P:m * P + P],
                                         ctxT[:, k, half * 4 * C:(half + 1) * 4 * C], start=(k == 0), stop=(k == 1))
                    done(last)
            for b in range(B):
                g = group()
                for c0, w in ((0, w0T[:, :, 2 * D:3 * D]), (D, wkv1s[:, :, D:2 * D])):
                    for k in range(KT):
                        last = pe.matmul(bank(g)[0:C, c0:c0 + D], ctxT[:, k, b * C:b * C + C], w[:, k, :],
                                         start=(k == 0), stop=(k == 1))
                done(last)
            pe.wait_ge(ld_ffn, 16 * N_FFN)
            for half in range(2):
                g = group()
                for j in range(4):
                    last = put(g, j * P, bfn[:, 4 * half + j, :], P)
                done(last)
            g = group()
            for j in range(KT):
                last = put(g, j * P, bpn[:, j, :], P)
            done(last)
            pe.wait_ge(quant_step, 8)
            for k in range(KT):
                for half in range(2):
                    g = group()
                    for j in range(4):
                        last = put(g, j * P, wfn[:, 4 * half + j, k * P:k * P + P], P)
                    done(last)
            pe.wait_ge(prep_ev, 28)
            for k in range(KT):
                for half in range(2):
                    g = group()
                    done(pe.matmul(bank(g), afc[0:R, k * P:k * P + P], bfT[0:R, half * 512:half * 512 + 512],
                                   start=True, stop=True))
            for q in range(4):
                g = group()
                for f in range(2):
                    for j in range(KT):
                        last = put(g, f * D + j * P, wpn[:, j, (2 * q + f) * P:(2 * q + f + 1) * P], P)
                done(last)
            for q in range(4):
                g = group()
                for f in range(2):
                    last = pe.matmul(bank(g)[:, f * D:f * D + D], apj[0:R, (2 * q + f) * P:(2 * q + f + 1) * P],
                                     bpT[0:R, :], start=True, stop=True)
                done(last)

        @block.tensor
        def _(pe):
            pe_prep(pe)
            pe.wait_ge(prep_ev, 44)
            pe_transposed(pe, 0, 0)
            pe_queries(pe, 0)
            run(pe, pe_iteration)

        def dve_prep(dve):
            n = [0]

            def evac(ins_of, *args):
                dve.wait_ge(prep_mm, n[0] + 1)
                last = ins_of(n[0] % 8)
                last.then_inc(prep_ev, 1)
                n[0] += 1

            dve.memset(V0[:, :, :, A:A + 1], 1.0)
            for k in range(KT):
                for jh in range(2):
                    evac(lambda g: dve.tensor_copy(w0T[:, k, jh * 512:jh * 512 + 512], bank(g)))
            for k in range(KT):
                for bh in range(2):
                    evac(lambda g: dve.tensor_copy(ctxT[:, k, bh * 480:bh * 480 + 480], bank(g, 480)))

            def small(g):
                dve.tensor_copy(bfcT[:, :], bank(g)[:, 0:FT])
                dve.tensor_copy(gqT[:, :, :], bank(g)[:, 16:16 + KT * E].rearrange("p (k e) -> p k e", k=KT))
                return dve.tensor_copy(b1T[:, :, :], bank(g)[:, 64:64 + EF * E].rearrange("p (k e) -> p k e", k=EF))

            evac(small)
            for dst in (k0T, k1T):
                for m in range(KT):
                    for half in range(2):
                        evac(lambda g: dve.tensor_copy(dst[:, m, half * 480:half * 480 + 480], bank(g, 480)))

            def values(g, b):
                dve.tensor_copy(V0[0:C, b, :, 0:A], bank(g)[0:C, 0:D].rearrange("p (h a) -> p h a", h=H))
                return dve.tensor_copy(V1[0:C, b, :], bank(g)[0:C, D:2 * D])

            for b in range(B):
                evac(lambda g: values(g, b))
            dve.wait_ge(ld_ffn, 16 * N_FFN)
            dve.tensor_reduce(wmx[:, 0:1], wfn, AX.XY, ALU.max, apply_absolute_value=True).then_inc(absmax_ready, 1)
            dve.tensor_reduce(wmx[:, 1:2], wpn, AX.XY, ALU.max, apply_absolute_value=True).then_inc(absmax_ready, 1)
            dve.wait_ge(allmax_ready, 1)
            dve.tensor_scalar(wsc[:, 1], wsc[:, 0], 1.0 / 127.0, None, ALU.mult).then_inc(quant_step, 1)
            dve.wait_ge(quant_step, 1)
            dve.reciprocal(wsc[:, 2], wsc[:, 1]).then_inc(quant_step, 1)
            dve.wait_ge(quant_step, 2)
            for i, w in ((0, wfn), (1, wpn)):
                dve.tensor_scalar(w, w, wsc[:, 2, i:i + 1], ROUND, ALU.mult, ALU.add).then_inc(quant_step, 1)
            dve.wait_ge(quant_step, 4)
            for w in (wfn, wpn):
                dve.tensor_scalar(w, w, ROUND, 127.0, ALU.subtract, ALU.min).then_inc(quant_step, 1)
            dve.wait_ge(quant_step, 6)
            for i, w in ((0, wfn), (1, wpn)):
                dve.tensor_scalar(w, w, -128.0, wsc[:, 1, i:i + 1], ALU.max, ALU.mult).then_inc(quant_step, 1)
            dve.wait_ge(gate_act, 2)
            dve.tensor_scalar(bpb[:, :], bpb[:, :], gates4[:, 2:3], None, ALU.mult).then_inc(quant_step, 1)
            for half in range(2):
                evac(lambda g: dve.tensor_scalar(bfT[0:R, half * 512:half * 512 + 512], bank(g)[0:R, :], 2.0, None, ALU.mult))
            evac(lambda g: dve.tensor_scalar(bpT[0:R, :], bank(g)[0:R, 0:D], 2.0, None, ALU.mult))
            for k in range(KT):
                for half in range(2):
                    evac(lambda g: dve.tensor_copy(W1T[:, k, half * 512:half * 512 + 512], bank(g)))
            dve.wait_ge(prep_ev, 32)
            for k in range(KT):
                for half in range(2):
                    evac(lambda g: dve.tensor_tensor(W1T[:, k, half * 512:half * 512 + 512],
                                                     W1T[:, k, half * 512:half * 512 + 512], bank(g), ALU.add))
            for q in range(4):
                evac(lambda g: dve.tensor_copy(W2T[:, 2 * q:2 * q + 2, :].rearrange("p f d -> p (f d)"), bank(g)))
            dve.wait_ge(prep_ev, 40)
            for q in range(4):
                v = W2T[:, 2 * q:2 * q + 2, :].rearrange("p f d -> p (f d)")
                evac(lambda g: dve.tensor_tensor(v, v, bank(g), ALU.add))

        def dve_norm(dve, L, b):
            xn, _, st, mv, vpe, y0 = buf_a if L == 0 else buf_b
            s = ln_dve[L]
            dve.memset(scratch[:, :], 0.0)
            for n in range(NT):
                s.up(dve.bn_stats(st[:, n, :], tiles(xs, b)[:, n, :]))
            s.wait(dve, b, 2)
            dve.memset(scratch[:, :], 0.0)
            for n in range(NT):
                s.up(dve.bn_aggr(mv[:, n, :], st[:, n, :]))
            s.wait(dve, b, 4)
            s.up(dve.tensor_scalar(vpe, mv[:, :, 1], EPS, None, ALU.add))
            rstd_ready[L].wait(dve, b, 1)
            for n in range(NT):
                s.up(dve.tensor_scalar(xn[:, n, :], tiles(xs, b)[:, n, :], mv[:, n, 0:1], y0[:, n:n + 1],
                                       ALU.subtract, ALU.mult))

        def dve_iteration(dve, i, first, rest, ahead):
            b, p = i, i - 1
            xb, xp = tiles(xs, b) if first else None, tiles(xs, p) if rest else None

            def mask_max(s):
                if not first:
                    return
                s_mm.wait(dve, b, s + 1)
                if s >= 2:
                    s_exp.wait(dve, b, s - 1)
                s_masked.up(dve.tensor_tensor(
                    Tb[:, s % 2], bank(1 + s % 2, 4 * C).rearrange("p (h c) -> p h c", h=4),
                    maskr[:, s // 4, :].unsqueeze(1).broadcast_to([P, 4, C]), ALU.add))
                s_masked.wait(dve, b, s + 1)
                s_max.up(dve.tensor_reduce(mx[:, s % 2], Tb[:, s % 2], AX.X, ALU.max))

            def normalise(n):
                if not first:
                    return
                av_mm.wait(dve, b, 4 * n + 4)
                o = bank(4)[:, 0:H * (A + 1)].rearrange("p (h a) -> p h a", h=H)
                att_ready.up(dve.reciprocal(rden[:, :], o[:, :, A]))
                att_ready.wait(dve, b, 2 * n + 1)
                att_ready.up(dve.tensor_tensor(att[:, n, :].rearrange("p (h a) -> p h a", h=H), o[:, :, 0:A],
                                               rden[:, :].unsqueeze(2).broadcast_to([P, H, A]), ALU.mult))

            if rest:
                dve_norm(dve, 1, p)
            for s in range(6):
                mask_max(s)
            if rest:
                f_mm.wait(dve, p, 1)
                x_ffn0.up(dve.scalar_tensor_tensor(out=xp, in0=bank(5).rearrange("p (n d) -> p n d", n=NT),
                                                   scalar=gates4[:, 2:3], in1=xp, op0=ALU.mult, op1=ALU.add))
                x_ffn0.wait(dve, p, 1)
                x_ffn0.up(dve.tensor_tensor(xp, xp, bpb[:, :].unsqueeze(1).broadcast_to([P, NT, D]), ALU.add))
                x_ffn0.wait(dve, p, 2)
                dve_norm(dve, 2, p)
            mask_max(6)
            normalise(0)
            mask_max(7)
            if ahead:
                dve_norm(dve, 0, i + 1)
            if rest:
                s1_mm.wait(dve, p, 1)
                m1_ready.up(dve.tensor_reduce(nm1[:, :], bank(7)[:, 0:NT * C].rearrange("p (n c) -> p n c", n=NT),
                                              AX.X, ALU.max))
                m1_ready.wait(dve, p, 1)
                m1_ready.up(dve.tensor_scalar(nm1[:, :], nm1[:, :], -ISQ, None, ALU.mult))
            normalise(1)
            if rest:
                e1_ready.wait(dve, p, 2)
                r1_ready.up(dve.reciprocal(ri1[:, :], sm1[:, :]))
                r1_ready.wait(dve, p, 1)
                r1_ready.up(dve.tensor_scalar(ri1[:, :], ri1[:, :], gates4[:, 1:2], None, ALU.mult))
                r1_ready.wait(dve, p, 2)
                av1_mm.wait(dve, p, 1)
                for n in range(NT):
                    x_attn1.up(dve.scalar_tensor_tensor(
                        out=xp[:, n, :], in0=bank(6)[:, n * D:n * D + D], scalar=ri1[:, n:n + 1], in1=xp[:, n, :],
                        op0=ALU.mult, op1=ALU.add))
                x_attn1.wait(dve, p, 2)
                dve_norm(dve, 3, p)
            if first:
                wo_mm.wait(dve, b, 1)
                x_attn0.up(dve.scalar_tensor_tensor(out=xb, in0=bank(0).rearrange("p (n d) -> p n d", n=NT),
                                                    scalar=gates4[:, 0:1], in1=xb, op0=ALU.mult, op1=ALU.add))
            if rest:
                xh_ready.wait(dve, p, 1)
                xl_ready.up(dve.tensor_tensor(tiles(xl, p), buf_b[0], tiles(xh, p), ALU.subtract))
                g_mm.wait(dve, p, 1)
                tl = tlog[:, :, bass.ds(p, 1), :] if not isinstance(p, int) else tlog[:, :, p:p + 1, :]
                t_ready.up(dve.tensor_scalar(tl.rearrange("p n a e -> p n (a e)"),
                                             bank(7)[:, 0:NT * E].rearrange("p (n e) -> p n e", n=NT),
                                             ltb[:, 0:1], None, ALU.mult))
                xl_ready.wait(dve, p, 1)
            if first:
                x_attn0.wait(dve, b, 1)

        @block.vector
        def _(dve):
            dve_prep(dve)
            dve.wait_ge(ld_x, 64)
            dve_norm(dve, 0, 0)
            run(dve, dve_iteration)

        def copy_512(act, dst, src):
            return act.activation(dst.rearrange("p k s -> p (k s)"), bank(src), ACT.Copy)

        def act_xT(act, L, b):
            xT_mm[L].wait(act, b, 1)
            xT_ready[L].up(copy_512(act, (buf_a if L == 0 else buf_b)[1], 0 if L == 0 else 5))

        def act_queries(act, b):
            q_mm.wait(act, b, 1)
            q_ready.up(copy_512(act, qT, 0))

        def act_iteration(act, i, first, rest, ahead):
            b, p = i, i - 1

            def transposed(s):
                if not first:
                    return
                pT_mm.wait(act, b, s + 1)
                if s >= 2:
                    av_mm.wait(act, b, s - 1)
                pT_ready.up(act.activation(PT[0:C, s % 2], bank(3)[0:C].rearrange("p (h q) -> p h q", h=4), ACT.Copy))

            def exps(s):
                if not first:
                    return
                s_sub.wait(act, b, s + 1)
                if s >= 2:
                    pT_mm.wait(act, b, s - 1)
                s_exp.up(act.activation(Eb[:, s % 2], Tb[:, s % 2], ACT.Exp, scale=ISQ))

            if rest:
                act_xT(act, 1, p)
                for f in range(FT):
                    j = f // 2
                    h_mm.wait(act, p, j + 1)
                    h_ready.up(act.activation(hT[:, f, :], bank(6 + j % 2)[:, (f % 2) * S:(f % 2) * S + S],
                                              ACT.Gelu, bias=bfcT[:, f:f + 1]))
            exps(0)
            for s in range(1, 6):
                exps(s)
                transposed(s - 1)
            if rest:
                act_xT(act, 2, p)
            exps(6)
            transposed(5)
            exps(7)
            transposed(6)
            if rest:
                q1_mm.wait(act, p, 1)
                q1_ready.up(copy_512(act, qTb, 6))
            if ahead:
                act_xT(act, 0, i + 1)
            transposed(7)
            if rest:
                m1_ready.wait(act, p, 2)
                for n in range(NT):
                    e1_ready.up(act.activation(E1[:, n, :], bank(7)[:, n * C:n * C + C], ACT.Exp,
                                               bias=nm1[:, n:n + 1], scale=ISQ, accum_out=sm1[:, n:n + 1]))
            if ahead:
                act_queries(act, i + 1)
            if rest:
                p1T_mm.wait(act, p, 1)
                p1T_ready.up(act.activation(PT1[0:C, :, :],
                                            bank(5)[0:C, 0:NT * P].rearrange("p (n q) -> p n q", n=NT), ACT.Copy))
            if first:
                attT_mm.wait(act, b, 1)
                attT_ready.up(copy_512(act, buf_a[1], 0))
            if rest:
                act_xT(act, 3, p)

        @block.scalar
        def _(act):
            act.wait_ge(ld_misc, 16 * N_MISC)
            act.activation(gates4[:, :], gates4[:, :], ACT.Tanh).then_inc(gate_act, 1)
            act.activation(ltb[:, :], ltb[:, :], ACT.Exp, scale=-1.0).then_inc(gate_act, 1)
            act.wait_ge(prep_ev, 44)
            act_xT(act, 0, 0)
            act_queries(act, 0)
            run(act, act_iteration)

        def nb(t):
            return t.rearrange("p (g e) -> p g e", e=E)

        @block.vector
        def _(dve):
            T0 = tlog[:, :, :, :].rearrange("p n b e -> p (n b) e")
            TN = tn.rearrange("p n (b e) -> p (n b) e", e=E)
            EX = ex.rearrange("p n (b e) -> p (n b) e", e=E)

            def step(ins):
                route_dve.n += 1
                ins.then_inc(route_dve.sem, 1)
                dve.wait_ge(route_dve.sem, route_dve.n)

            def bc(v, k=E):
                return v.unsqueeze(2).broadcast_to([P, NT * B, k])

            dve.wait_ge(t_ready.sem, B)
            step(dve.tensor_reduce(mxe[:, :], T0, AX.X, ALU.max))
            step(dve.tensor_tensor(TN, T0, bc(mxe), ALU.subtract))
            dve.wait_ge(route_act, 1)
            step(dve.tensor_reduce(ls[:, :], EX, AX.X, ALU.add))
            dve.wait_ge(route_act, 2)
            step(dve.tensor_tensor(TN, TN, bc(ls), ALU.subtract))
            dve.wait_ge(route_pe, 1)
            step(dve.tensor_reduce(rm[:, 0:1], bank(0)[:, 0:S], AX.X, ALU.max))
            step(dve.tensor_scalar(rm[:, 1:2], rm[:, 0:1], -1.0, None, ALU.mult))
            dve.wait_ge(route_act, 3)
            step(dve.reciprocal(rm[:, 3:4], rm[:, 2:3]))
            step(dve.tensor_scalar(Bd[:, :], blk8[:, :], rm[:, 3:4], None, ALU.mult))
            for it in range(SINK - 2):
                dve.wait_ge(route_pe, 3 + 2 * it)
                step(dve.reciprocal(ra[:, :], bank(1)[:, 0:NT * B]))
                dve.wait_ge(route_pe, 4 + 2 * it)
                step(dve.tensor_tensor_reduce(out=vt[:, :], in0=bank(2)[:, 0:B], in1=blk8[:, :], scale=1.0,
                                              scalar=0.0, op0=ALU.mult, op1=ALU.add, accum_out=rm[:, 2:3]))
                step(dve.reciprocal(rm[:, 3:4], rm[:, 2:3]))
                step(dve.tensor_scalar(Bd[:, :], blk8[:, :], rm[:, 3:4], None, ALU.mult))
            step(dve.tensor_scalar(blkB[:, :], blk[:, :], rm[:, 3:4], None, ALU.mult))
            dve.wait_ge(route_act, 5)
            step(dve.tensor_tensor(t6[:, :], bank(0)[:, 0:S], lnU[:, :], ALU.subtract))
            dve.wait_ge(route_act, 6)
            step(dve.reciprocal(rm[:, 5:6], rm[:, 4:5]))
            step(dve.tensor_scalar(aff[:, :], aff[:, :], rm[:, 5:6], None, ALU.mult))
            src = aff
            for _ in range(CAP // 8):
                step(dve.max(m8[:, :], src[:, :]))
                step(dve.match_replace(out=wk[:, :], in_to_replace=m8[:, :], in_values=src[:, :], imm_value=-1.0))
                src = wk
            step(dve.tensor_scalar(wk[:, :], wk[:, :], 0.0, None, ALU.is_lt))
            step(dve.memset(lnU[:, :], 1.0))
            step(dve.tensor_tensor_scan(posn[:, :], lnU[:, :], wk[:, :], 0.0, ALU.mult, ALU.add))
            step(dve.tensor_tensor(posn[:, :], posn[:, :], wk[:, :], ALU.mult))
            dve.wait_ge(route_pe, 3 + 2 * (SINK - 2) + 1)
            pv = posB[:, :, :, :].rearrange("p n b e -> p n (b e)")
            step(dve.tensor_scalar(pv, bank(1)[:, 0:S].rearrange("p (n j) -> p n j", n=NT), 1.0, None, ALU.subtract))
            A3 = [affp[:, :, i].rearrange("p n b e -> p n (b e)") for i in range(3)]
            AB = bank(2)[:, 0:S].rearrange("p (n j) -> p n j", n=NT)
            step(dve.tensor_copy(A3[0], AB))
            step(dve.tensor_tensor(tn, AB, A3[0], ALU.subtract))
            step(dve.tensor_copy(A3[1], tn))
            step(dve.tensor_tensor(A3[2], tn, A3[1], ALU.subtract))
            assert route_dve.n == ROUTED

        @block.scalar
        def _(act):
            act.wait_ge(route_dve.sem, 2)
            act.activation(ex.rearrange("p n j -> p (n j)"), tn.rearrange("p n j -> p (n j)"), ACT.Exp).then_inc(route_act, 1)
            act.wait_ge(route_dve.sem, 3)
            act.activation(ls[:, :], ls[:, :], ACT.Ln).then_inc(route_act, 1)
            act.wait_ge(route_dve.sem, 6)
            act.activation(KA[:, :], bank(0)[:, 0:S], ACT.Exp, bias=rm[:, 1:2], accum_out=rm[:, 2:3]).then_inc(route_act, 1)
            act.wait_ge(route_pe, 2)
            act.activation(KB.rearrange("p n j -> p (n j)"), bank(3)[:, 0:S], ACT.Copy).then_inc(route_act, 1)
            act.wait_ge(route_pe, 3 + 2 * (SINK - 2))
            act.activation(lnU[:, :], bank(4)[:, 0:S], ACT.Ln).then_inc(route_act, 1)
            act.wait_ge(route_dve.sem, 26)
            act.activation(aff[:, :], t6[:, :], ACT.Exp, bias=rm[:, 1:2], accum_out=rm[:, 4:5]).then_inc(route_act, 1)

        @block.tensor
        def _(pe):
            pe.wait_ge(route_dve.sem, 4)
            for n in range(NT):
                last = transpose(pe, bank(0)[:, n * P:n * P + P], tn[:, n, :])
            last.then_inc(route_pe, 1)
            pe.wait_ge(route_act, 3)
            for n in range(NT):
                last = transpose(pe, bank(3)[:, n * P:n * P + P], KA[:, n * P:n * P + P])
            last.then_inc(route_pe, 1)
            for it in range(SINK - 2):
                pe.wait_ge(route_dve.sem, 8 + 4 * it)
                for n in range(NT):
                    last = pe.matmul(bank(1)[:, n * B:n * B + B], KA[:, n * P:n * P + P], Bd[:, :], start=True, stop=True)
                last.then_inc(route_pe, 1)
                if it == 0:
                    pe.wait_ge(route_act, 4)
                pe.wait_ge(route_dve.sem, 9 + 4 * it)
                for n in range(NT):
                    last = pe.matmul(bank(2)[:, 0:B], KB[:, n, :], ra[:, n * B:n * B + B], start=(n == 0), stop=(n == NT - 1))
                last.then_inc(route_pe, 1)
            pe.wait_ge(route_dve.sem, 25)
            pe.matmul(bank(4)[:, 0:S], blkB[:, :], KA[:, :], start=True, stop=True).then_inc(route_pe, 1)
            pe.wait_ge(route_dve.sem, 48)
            for k, t in ((1, posn), (2, aff)):
                for n in range(NT):
                    last = transpose(pe, bank(k)[:, n * P:n * P + P], t[:, n * P:n * P + P])
            last.then_inc(route_pe, 1)

        def one(t, i, n=1):
            return bass.ds(i, n) if not isinstance(i, int) else slice(i, i + n)

        w1_dram = w1.rearrange("e (k p) f -> p e k f", p=P)
        w2_dram = w2.rearrange("e (f p) d -> p e f d", p=P)

        @block.sync
        def _(sp):
            def load(e, par):
                if not (isinstance(e, int) and e == 0):
                    w1h_ready.wait(sp, e - 1, 2)
                    w1l_ready.wait(sp, e - 1, 2)
                sp.dma_start(w1r, w1_dram[:, one(w1, e)].rearrange("p a k f -> p (a k) f")).then_inc(ld_w1.sem, 16)
                if not (isinstance(e, int) and e == 0):
                    w2h_ready.wait(sp, e - 1, 2)
                    w2l_ready.wait(sp, e - 1, 2)
                sp.dma_start(w2r, w2_dram[:, one(w2, e)].rearrange("p a f d -> p (a f) d")).then_inc(ld_w2.sem, 16)
                if not (isinstance(e, int) and e < 2):
                    y_t.wait(sp, e - 2, 2)
                sp.dma_start(b2b[:, par], b2[one(b2, e)].broadcast_to([P, D])).then_inc(ld_b2.sem, 16)

            load(0, 0)
            load(1, 1)
            with sp.Fori(1, E // 2) as j:
                load(2 * j, 0)
                load(2 * j + 1, 1)
            with sp.Fori(0, B) as b:
                out_ready.wait(sp, b, 1)
                sp.dma_start(out.rearrange("b (n p) d -> p b n d", p=P)[:, one(out, b)].rearrange("p a n d -> p (a n) d"),
                             tiles(xs, b)).then_inc(stored, 16)
            sp.wait_ge(stored, 16 * B)

        @block.gpsimd
        def _(pool):
            def parts(e):
                for f in range(EF):
                    hh_ready.wait(pool, e, f + 1)
                    hl_ready.up(pool.tensor_tensor(hl[:, f, :], hf[:, f % 2, :], hh[:, f, :], ALU.subtract))

            def prepare(e, par):
                for p in range(2):
                    w2h_ready.wait(pool, e, p + 1)
                    w2l_ready.up(pool.tensor_tensor(w2l[:, par, 4 * p:4 * p + 4], w2r[:, 4 * p:4 * p + 4],
                                                    w2h[:, par, 4 * p:4 * p + 4], ALU.subtract))

            def outputs(e, par, pair):
                q = slice(64 * par, 64 * par + 64)
                if isinstance(e, int) and e == E - 1:
                    hl_ready.wait(pool, e, EF)
                else:
                    w2l_ready.wait(pool, e + 1, 2)
                for pr in range(2):
                    yh_ready.wait(pool, e, pr + 1)
                    yl_ready.up(pool.tensor_tensor(
                        YL[q, one(YL, pair), 4 * pr:4 * pr + 4, :].rearrange("p a b d -> p (a b) d"), yg[q, pr],
                        YH[q, one(YH, pair), 4 * pr:4 * pr + 4, :].rearrange("p a b d -> p (a b) d"), ALU.subtract))
                yl_ready.wait(pool, e, 2)

            prepare(0, 0)
            parts(0)
            with pool.Fori(0, E // 2 - 1) as j:
                prepare(2 * j + 1, 1)
                outputs(2 * j, 0, j)
                parts(2 * j + 1)
                prepare(2 * j + 2, 0)
                outputs(2 * j + 1, 1, j)
                parts(2 * j + 2)
            prepare(E - 1, 1)
            outputs(E - 2, 0, E // 2 - 1)
            parts(E - 1)
            outputs(E - 1, 1, E // 2 - 1)

        @block.tensor
        def _(pe):
            def gather(e, par):
                g_ready.wait(pe, e, 1)
                idx = 0
                for k in range(KT):
                    for part, src in ((0, xh), (1, xl)):
                        if idx >= 2:
                            (xgh_ready if part == 0 else xgl_ready).wait(pe, e, 1)
                        for b in range(B):
                            for n in range(NT):
                                last = pe.matmul(bank(2 + idx % 2)[:, b * CAP:(b + 1) * CAP],
                                                 src[:, b * NT + n, k * P:k * P + P], G[:, par, n * B + b, :],
                                                 start=(n == 0), stop=(n == NT - 1))
                        g_mm2.up(last)
                        idx += 1
                if not (isinstance(e, int) and e == 0):
                    gt_ready.wait(pe, e - 1, 2)
                for t in range(4):
                    for n in range(NT):
                        last = pe.matmul(bank(6)[:, t * 8:t * 8 + 6],
                                         G[:, par, n * B + 2 * t:n * B + 2 * t + 2, :].rearrange("p b c -> p (b c)"),
                                         affp[:, n, :, 2 * t:2 * t + 2, one(affp, e)].rearrange("p i b a -> p i (b a)"),
                                         start=(n == 0), stop=(n == NT - 1))
                g_mm2.up(last)

            def expert(e, par, ahead, pair=0):
                xgh_ready.wait(pe, e, 2)
                xgl_ready.wait(pe, e, 2)
                w1h_ready.wait(pe, e, 2)
                w1l_ready.wait(pe, e, 2)
                for f in range(EF):
                    if f >= 2:
                        gelu_ready.wait(pe, e, f - 1)
                    first = True
                    for wp, xp in ((w1h, xgh), (w1h, xgl), (w1l, xgh)):
                        for k in range(KT):
                            last = pe.matmul(bank(f % 2), wp[:, par, k, f * P:f * P + P], xp[:, par, k, :],
                                             start=first, stop=(wp is w1l and k == KT - 1))
                            first = False
                    m1_mm.up(last)
                if ahead:
                    gather(e + 1, 1 - par)
                hl_ready.wait(pe, e, EF)
                w2h_ready.wait(pe, e, 2)
                w2l_ready.wait(pe, e, 2)
                for t in range(4):
                    if t % 2 == 0 and not (isinstance(e, int) and e == 0):
                        y_t.wait(pe, e - 1, t // 2 + 1)
                    for f in range(EF):
                        for hp, wp in ((hh, w2h), (hh, w2l), (hl, w2h)):
                            last = pe.matmul(bank(4 + t // 2)[:, (t % 2) * D:(t % 2) * D + D],
                                             hp[:, f, t * P:t * P + P], wp[:, par, f, :],
                                             start=(f == 0 and wp is w2h and hp is hh),
                                             stop=(f == EF - 1 and hp is hl))
                    if t % 2:
                        m2_mm.up(last)

            gather(0, 0)
            expert(0, 0, True)
            with pe.Fori(0, E // 2 - 1) as j:
                expert(2 * j + 1, 1, True, j)
                expert(2 * j + 2, 0, True, j + 1)
            expert(E - 1, 1, False, E // 2 - 1)

            def places(b, par):
                for n in range(NT):
                    gs_ready.wait(pe, b, n + 1)
                    for r in range(E // 2):
                        last = pe.transpose(psb(2 * par + n)[:, r * P:r * P + P],
                                            Gs[:, par, n, 2 * r:2 * r + 2, :].rearrange("p e c -> p (e c)"), identb[:, :])
                    gst_mm.up(last)

            def combine(b, par):
                for n in range(NT):
                    (gt2_act, gt2_dve)[n].wait(pe, b, 1)
                    for r in range(E // 2):
                        for Y in (YH, YL):
                            last = pe.matmul(bank(4 + par)[:, n * D:n * D + D], GT[:, par, n, r, :],
                                             Y[:, r, one(Y, b), :].rearrange("p a d -> p (a d)"),
                                             start=(r == 0 and Y is YH), stop=(r == E // 2 - 1 and Y is YL))
                c_mm.up(last)

            places(0, 0)
            yl_ready.wait(pe, E - 1, 2)
            with pe.Fori(0, B // 2 - 1) as j:
                places(2 * j + 1, 1)
                combine(2 * j, 0)
                places(2 * j + 2, 0)
                combine(2 * j + 1, 1)
            places(B - 1, 1)
            combine(B - 2, 0)
            combine(B - 1, 1)

        @block.vector
        def _(dve):
            def onehot(e, par):
                if not (isinstance(e, int) and e < 2):
                    g_mm2.wait(dve, e - 2, 5)
                g_ready.up(dve.tensor_tensor(
                    G[:, par], posB[:, :, :, one(posB, e)].rearrange("p n b a -> p (n b) a").broadcast_to([P, NT * B, CAP]),
                    iota_c[:, :].unsqueeze(1).broadcast_to([P, NT * B, CAP]), ALU.is_equal))

            def onehots_of_batch(b, par):
                for n in range(NT):
                    gs_ready.up(dve.tensor_tensor(
                        Gs[:, par, n], posB[:, n, one(posB, b)].rearrange("p a e -> p (a e)").unsqueeze(2).broadcast_to([P, E, CAP]),
                        iota_c[:, :].unsqueeze(1).broadcast_to([P, E, CAP]), ALU.is_equal))

            def prepare(e, par, piece):
                if piece == 0:
                    ld_w1.wait(dve, e, 16)
                if piece < 2:
                    w1h_ready.wait(dve, e, piece + 1)
                    w1l_ready.up(dve.tensor_tensor(w1l[:, par, piece], w1r[:, piece], w1h[:, par, piece], ALU.subtract))
                elif piece == 2:
                    onehot(e, par)

            def gathered(e, par):
                for k in range(KT):
                    g_mm2.wait(dve, e, 2 * k + 2)
                    xgl_ready.up(dve.tensor_copy(xgl[:, par, k, :], bank(3)))
                g_mm2.wait(dve, e, 5)
                gv = bank(6)[:, 0:32].rearrange("p (t i b) -> p t i b", t=4, b=2)
                for half in range(2):
                    q = slice(64 * half, 64 * half + 64)
                    gt_ready.up(dve.tensor_reduce(gt[q, par, :], gv[q, :, 0:3, half], AX.X, ALU.add))

            def expert(e, par, ahead, pair=0):
                for f in range(EF):
                    gelu_ready.wait(dve, e, f + 1)
                    hh_ready.up(dve.tensor_copy(hh[:, f, :], hf[:, f % 2, :]))
                    if ahead and f % 2 == 1:
                        prepare(e + 1, 1 - par, f // 2)
                if ahead:
                    gathered(e + 1, 1 - par)
                ld_b2.wait(dve, e, 16)
                for pr in range(2):
                    m2_mm.wait(dve, e, pr + 1)
                    y_t.up(dve.tensor_tensor(yt[:, pr], bank(4 + pr).rearrange("p (t d) -> p t d", t=2),
                                             b2b[:, par].unsqueeze(1).broadcast_to([P, 2, D]), ALU.add))
                    yg_ready.wait(dve, e, 4 * pr + 4)
                    q = slice(64 * par, 64 * par + 64)
                    yh_ready.up(dve.tensor_scalar(
                        YH[q, one(YH, pair), 4 * pr:4 * pr + 4, :].rearrange("p a b d -> p (a b) d"), yg[q, pr],
                        1.0, None, ALU.mult))

            for piece in range(4):
                prepare(0, 0, piece)
            gathered(0, 0)
            expert(0, 0, True)
            with dve.Fori(0, E // 2 - 1) as j:
                expert(2 * j + 1, 1, True, j)
                expert(2 * j + 2, 0, True, j + 1)
            expert(E - 1, 1, False, E // 2 - 1)
            def places(b, par):
                onehots_of_batch(b, par)
                gst_mm.wait(dve, b, 2)
                gt2_dve.up(dve.tensor_copy(GT[:, par, 1].rearrange("p r q -> p (r q)"), psb(2 * par + 1)))

            def finish(b, par):
                c_mm.wait(dve, b, 1)
                xb = tiles(xs, b)
                out_ready.up(dve.scalar_tensor_tensor(
                    out=xb, in0=bank(4 + par).rearrange("p (n d) -> p n d", n=NT), scalar=gates4[:, 3:4], in1=xb,
                    op0=ALU.mult, op1=ALU.add))

            places(0, 0)
            with dve.Fori(0, B // 2 - 1) as j:
                places(2 * j + 1, 1)
                finish(2 * j, 0)
                places(2 * j + 2, 0)
                finish(2 * j + 1, 1)
            places(B - 1, 1)
            finish(B - 2, 0)
            finish(B - 1, 1)

        @block.scalar
        def _(act):
            def prepare(e, par, piece):
                if piece == 0:
                    ld_w1.wait(act, e, 16)
                if piece == 2:
                    ld_w2.wait(act, e, 16)
                if piece < 2:
                    w1h_ready.up(act.activation(w1h[:, par, piece], w1r[:, piece], ACT.Copy))
                else:
                    p = piece - 2
                    w2h_ready.up(act.activation(w2h[:, par, 4 * p:4 * p + 4], w2r[:, 4 * p:4 * p + 4], ACT.Copy))

            def gathered(e, par):
                for k in range(KT):
                    g_mm2.wait(act, e, 2 * k + 1)
                    xgh_ready.up(act.activation(xgh[:, par, k, :], bank(2), ACT.Copy))

            def expert(e, par, ahead, pair=0):
                for f in range(EF):
                    m1_mm.wait(act, e, f + 1)
                    if f >= 2:
                        hl_ready.wait(act, e, f - 1)
                    gelu_ready.up(act.activation(hf[:, f % 2, :], bank(f % 2), ACT.Gelu_apprx_tanh,
                                                 bias=b1T[:, f, one(b1T, e)]))
                    if ahead and f % 2 == 0:
                        prepare(e + 1, 1 - par, f // 2)
                if ahead:
                    gathered(e + 1, 1 - par)
                for pr in range(2):
                    y_t.wait(act, e, pr + 1)
                    if not (isinstance(e, int) and e == 0):
                        yl_ready.wait(act, e - 1, pr + 1)
                    for i in range(4):
                        t, half = 2 * pr + i // 2, i % 2
                        q, o = slice(64 * half, 64 * half + 64), slice(64 * par, 64 * par + 64)
                        yg_ready.up(act.activation(yg[o, pr, i, :], yt[q, pr, i // 2, :], ACT.Copy,
                                                   scale=gt[q, par, t:t + 1]))

            for piece in range(4):
                prepare(0, 0, piece)
            gathered(0, 0)
            expert(0, 0, True)
            with act.Fori(0, E // 2 - 1) as j:
                expert(2 * j + 1, 1, True, j)
                expert(2 * j + 2, 0, True, j + 1)
            expert(E - 1, 1, False, E // 2 - 1)
            def places(b, par):
                gst_mm.wait(act, b, 1)
                gt2_act.up(act.activation(GT[:, par, 0].rearrange("p r q -> p (r q)"), psb(2 * par), ACT.Copy))

            places(0, 0)
            with act.Fori(0, B // 2 - 1) as j:
                places(2 * j + 1, 1)
                places(2 * j + 2, 0)
            places(B - 1, 1)


_INS = ["x", "ctx_1024", "mask_SxS2_fk0", "g_xattn", "g_ffn", "L0_xattn_Wq", "L0_xattn_Wkv", "L0_xattn_Wout",
        "L0_ffn_W_fc", "L0_ffn_b_fc", "L0_ffn_A_fc", "L0_ffn_B_fc", "L0_ffn_W_proj", "L0_ffn_b_proj",
        "L0_ffn_A_proj", "L0_ffn_B_proj", "L1_xattn_Wq", "L1_xattn_Wkv", "L1_ffn_gate_query", "L1_ffn_log_temp",
        "L1_ffn_w1", "L1_ffn_b1", "L1_ffn_w2", "L1_ffn_b2"]


def kernel(**inputs):
    import numpy as np
    import concourse.bacc as bacc
    from concourse.bass_utils import run_bass_kernel_spmd

    nc = bacc.Bacc("TRN2", target_bir_lowering=False, num_devices=1)
    arrays, args = {}, []
    for name in _INS:
        a = np.ascontiguousarray(inputs[name])
        a = a.reshape(a.shape or (1,))
        arrays[f"in_{name}"] = a
        args.append(nc.dram_tensor(f"in_{name}", a.shape, mybir.dt.from_np(a.dtype), kind="ExternalInput").ap())
    shape = inputs["x"].shape
    args.append(nc.dram_tensor("out_0", shape, F32, kind="ExternalOutput").ap())
    build(nc, *args)
    r = run_bass_kernel_spmd(nc, [arrays], core_ids=[0])
    return r.results[0]["out_0"]
```

```python
from contextlib import ExitStack

import concourse.bass as bass
from concourse import mybir

F32 = mybir.dt.float32
BF16 = mybir.dt.bfloat16
I32 = mybir.dt.int32
ALU = mybir.AluOpType
ACT = mybir.ActivationFunctionType
AX = mybir.AxisListType

P = 128
EPS = 1e-5
ROUND = 12582912.0


class Sig:

    def __init__(self, sem, per=0):
        self.sem, self.per, self.n = sem, per, 0

    def up(self, ins):
        self.n += 1
        ins.then_inc(self.sem, 1)

    def wait(self, eng, b, k):
        eng.wait_ge(self.sem, b * self.per + k)


def build(nc, x, ctx_1024, mask, g_xattn, g_ffn, wq0, wkv0, wout0, w_fc, b_fc, a_fc, bb_fc, w_proj, b_proj,
          a_proj, bb_proj, wq1, wkv1, gate_query, log_temp, w1, b1, w2, b2, out):
    B, S, D = x.shape
    C = ctx_1024.shape[1]
    H, A = 16, D // 16
    FF = w_fc.shape[0]
    E, _, DFF = w1.shape
    R = a_fc.shape[0]
    CAP = 64
    NT, KT, FT = S // P, D // P, FF // P
    T = B * NT
    EF = DFF // P
    ISQ = 1.0 / 16.0
    SINK = 6
    assert B * E == P and D == 256 and FF == DFF == 1024

    with ExitStack() as cx:
        def sb(name, shape, dt=F32):
            return cx.enter_context(nc.sbuf_tensor(name, shape, dt))

        def sem(name):
            return cx.enter_context(nc.semaphore(name))

        ident = sb("ident", [P, P])
        blk8 = sb("blk8", [P, B])
        blk = sb("blk", [P, P])
        iota_c = sb("iota_c", [P, CAP])
        iota_i = sb("iota_i", [P, CAP], I32)
        identb = sb("identb", [P, P], BF16)
        posB = sb("posB", [P, NT, B, E])
        affp = sb("affp", [P, NT, 3, B, E], BF16)
        G = sb("G", [P, 2, NT * B, CAP], BF16)
        gt = sb("gt", [P, 2, 4])
        rm = sb("rm", [P, 8])
        scratch = sb("scratch", [P, 1])
        mhalf = sb("mhalf", [P, NT])
        Bd = sb("Bd", [P, B])
        ra = sb("ra", [P, NT * B])
        vt = sb("vt", [P, B])
        m8 = sb("m8", [P, 8])
        xs = sb("xs", [P, T, D])
        gates4 = sb("gates4", [P, 4])
        xh = sb("xh", [P, T, D], BF16)
        xl = sb("xl", [P, T, D], BF16)
        tlog = sb("tlog", [P, NT, B, E])
        b1T = sb("b1T", [P, EF, E])

        ARENA = 41984
        arena = sb("arena", [P, ARENA])
        at = [0]

        def carve(shape, dt=F32):
            n = 1
            for s in shape:
                n *= s
            words = n if dt != BF16 else (n + 1) // 2
            v = arena[:, at[0]:at[0] + words]
            at[0] += words
            assert at[0] <= ARENA, at[0]
            if dt != F32:
                v = v.bitcast(dt)
            names = "abcdef"[:len(shape)]
            if len(shape) == 1:
                return v
            return v.rearrange(f"p ({' '.join(names)}) -> p {' '.join(names)}",
                               **{c: s for c, s in zip(names, shape)})

        ctxn = carve([B, D])
        maskr = carve([NT, C])
        wnat = carve([2 + 4 + 2, D])
        wfn = carve([FT, D])
        wpn_at = at[0]
        wpn = carve([KT, FF])
        wq1s = carve([KT, D])
        wkv1s = carve([KT, 2 * D])
        afc = carve([D])
        apj = carve([FF])
        bfn = carve([FT, R])
        bpn = carve([KT, R])
        gqn = carve([D])
        bfT = carve([FF])
        bpT = carve([D])
        w0T = carve([KT, 8 * P])
        W1T = carve([KT, FF])
        W2T = carve([FT, D])
        gqT = carve([KT, E])
        ctxT = carve([KT, B * C])
        k0T = carve([KT, B * C])
        k1T = carve([KT, B * C])
        V0 = carve([2, B, H, A + 1], BF16)
        V1 = carve([B, D])
        bfcT = carve([FT])
        b8n = carve([P])
        b1n = carve([DFF])
        bpb = carve([D])
        ltb = carve([1])
        wmx = carve([2])
        wsc = carve([4, 2])

        LNS = ("attn0", "ffn0", "attn1", "ffn1")

        def norm_buffers():
            return carve([NT, D]), carve([KT, S]), carve([NT, 6]), carve([NT, 2]), carve([NT]), carve([NT])

        buf_a, buf_d = norm_buffers(), norm_buffers()
        qT = carve([KT, S])
        kbd = wnat.rearrange("p j d -> p (j d)")[:, 0:KT * 8 * C].rearrange("p (k h c) -> p k h c", k=KT, h=8)
        Tb = carve([2, 4, C])
        mx = carve([2, 4])
        qTb = carve([KT, S])
        rden = carve([H])
        att = carve([NT, D])
        Es = carve([2, 2, 4, C], BF16)
        PT = carve([2, 2, 4, P], BF16)
        attT = w0T[:, :, D:2 * D]
        hT = wfn
        nm1 = carve([NT])
        sm1 = carve([NT])
        ri1 = carve([NT])
        here, at[0] = at[0], wpn_at
        buf_b = norm_buffers()
        assert at[0] <= wpn_at + KT * FF
        at[0] = wpn_at + KT * (FF + D)
        Eb = carve([2, 4, C])
        assert at[0] <= wpn_at + KT * (FF + 3 * D)
        at[0] = 0
        E1 = carve([NT, C])
        PT1 = carve([NT, P])
        buf_c = norm_buffers()
        assert at[0] <= B * D
        at[0] = here
        assert at[0] <= ARENA - 4608, at[0]
        bufs = [buf_a, buf_b, buf_d, buf_c]
        T_BANK = [0, 5, 0, 5]

        ps = cx.enter_context(nc.psum_tensor("ps", [P, 8, 512], F32))


        def bank(n, words=512):
            return ps[:, n, 0:words]

        ld_misc, ld_ffn, ld_x = sem("ld_misc"), sem("ld_ffn"), sem("ld_x")
        ld_w0, ld_ctx, ld_w1s = sem("ld_w0"), sem("ld_ctx"), sem("ld_w1s")
        consts_made = sem("consts_made")
        absmax_ready, allmax_ready, quant_step = sem("absmax_ready"), sem("allmax_ready"), sem("quant_step")
        fc_quantised, proj_quantised, prep_hi = sem("fc_quantised"), sem("proj_quantised"), sem("prep_hi")
        prep_mm, prep_ev = sem("prep_mm"), sem("prep_ev")
        wt_mm, wt_ready = sem("wt_mm"), sem("wt_ready")
        gate_act = sem("gate_act")

        def sig(name, per):
            return Sig(sem(name), per)

        ln_dve = [sig(f"ln_dve_{n}", 7) for n in LNS]
        rstd_ready = [sig(f"rstd_{n}", 1) for n in LNS]
        xT_mm = [sig(f"xT_mm_{n}", 1) for n in LNS]
        xT_ready = [sig(f"xT_ready_{n}", 1) for n in LNS]
        kbd_ready = sig("kbd_ready", 2)
        q_mm, q_ready = sig("q_mm", 1), sig("q_ready", 1)
        s_mm, s_masked, s_max, s_sub, s_exp = (sig(n, 8) for n in ("s_mm", "s_masked", "s_max", "s_sub", "s_exp"))
        pT_mm, pT_ready, av_mm = sig("pT_mm", 8), sig("pT_ready", 8), sig("av_mm", 8)
        att_ready = sig("att_ready", 4)
        attT_mm, attT_ready, wo_mm, x_attn0 = sig("attT_mm", 1), sig("attT_ready", 1), sig("wo_mm", 1), sig("x_attn0", 1)
        es_hi, es_lo = sig("es_hi", 8), sig("es_lo", 8)
        xs_ready = sig("xs_ready", 2)
        h_mm, h_ready, f_mm, x_ffn0 = sig("h_mm", 4), sig("h_ready", 8), sig("f_mm", 1), sig("x_ffn0", 2)
        q1_mm, q1_ready, s1_mm, m1_ready, e1_ready = (sig(n, p) for n, p in (
            ("q1_mm", 1), ("q1_ready", 1), ("s1_mm", 1), ("m1_ready", 2), ("e1_ready", 2)))
        p1T_mm, p1T_ready, av1_mm, r1_ready, x_attn1 = (sig(n, p) for n, p in (
            ("p1T_mm", 1), ("p1T_ready", 1), ("av1_mm", 1), ("r1_ready", 2), ("x_attn1", 2)))
        g_mm, t_ready = sig("g_mm", 1), sig("t_ready", 1)

        N_MISC, N_FFN, N_X = 7, 6, 5
        CONSTS = 12
        PREP = 28
        EV_K0 = 13

        route_dve, route_act, route_pe = Sig(sem("route_dve")), sem("route_act"), sem("route_pe")
        ROUTED = 53
        stored = sem("stored")
        ld_w1, ld_w2, ld_b2 = sig("ld_w1", 16), sig("ld_w2", 16), sig("ld_b2", 16)
        w1h_ready, w1l_ready, w2h_ready, w2l_ready = (sig(n, 2) for n in ("w1h_ready", "w1l_ready", "w2h_ready", "w2l_ready"))
        g_ready, g_mm2, xgh_ready, xgl_ready, gt_ready = (sig(n, p) for n, p in (
            ("g_ready", 1), ("g_mm2", 5), ("xgh_ready", 2), ("xgl_ready", 2), ("gt_ready", 2)))
        m1_mm, gelu_ready, hh_ready, hl_ready = (sig(n, EF) for n in ("m1_mm", "gelu_ready", "hh_ready", "hl_ready"))
        m2_mm, y_t, yh_ready, yl_ready = sig("m2_mm", 2), sig("y_t", 2), sig("yh_ready", 2), sig("yl_ready", 2)
        yg_ready = sig("yg_ready", 8)
        gs_ready, gst_mm = (sig(n, NT) for n in ("gs_ready", "gst_mm"))
        gt2_act, gt2_dve = (sig(n, 1) for n in ("gt2_act", "gt2_dve"))
        c_mm, out_ready = sig("c_mm", 1), sig("out_ready", 1)

        at[0] = 0
        YH, YL = [carve([E // 2, B, D], BF16) for _ in range(2)]
        w1h_at = at[0]
        w1h, w1l = [carve([2, KT, DFF], BF16) for _ in range(2)]
        w2h, w2l = [carve([2, EF, D], BF16) for _ in range(2)]
        xgh, xgl = [carve([2, KT, B * CAP], BF16) for _ in range(2)]
        hh, hl = [carve([EF, B * CAP], BF16) for _ in range(2)]
        hf = carve([3, B * CAP])
        yt = carve([2, 2, D])
        yg = carve([2, 4, D])
        experts_end = at[0]
        at[0] = 0
        ls = carve([NT * B])
        mxe = carve([NT * B])
        tn = carve([NT, B * E])
        ex = carve([NT, B * E])
        KA = carve([S])
        KB = carve([NT, P])
        lnU = carve([S])
        t6 = carve([S])
        aff = carve([S])
        wk = carve([S])
        posn = carve([S])
        blkB = carve([P])
        assert at[0] <= w1h_at and experts_end <= ARENA - 4096 - 512, (at[0], experts_end)
        w1r, w2r, b2b = (arena[:, ARENA - o:ARENA - o + w] for o, w in ((4608, 2048), (2560, 2048), (512, 512)))
        Gs = w1r.bitcast(BF16).rearrange("p (i n e c) -> p i n e c", i=2, n=NT, e=E)
        GT = w2r.bitcast(BF16).rearrange("p (i n r q) -> p i n r q", i=2, n=NT, r=E // 2)
        w1r = w1r.rearrange("p (k f) -> p k f", k=KT)
        w2r = w2r.rearrange("p (f d) -> p f d", f=EF)
        b2b = b2b.rearrange("p (a d) -> p a d", a=2)

        block = cx.enter_context(nc.Block())

        @block.sync
        def _(sp):
            def ld(dst, src, s):
                sp.dma_start(dst, src).then_inc(s, 16)

            xv = x.rearrange("b (n p) d -> p (b n) d", p=P)
            ld(wnat[:, 0:2], wq0.rearrange("(j p) d -> p j d", p=P), ld_w0)
            ld(wnat[:, 2:6], wkv0.rearrange("(j p) d -> p j d", p=P), ld_w0)
            ld(wnat[:, 6:8], wout0.rearrange("(j p) d -> p j d", p=P), ld_w0)
            ld(ctxn[0:C], ctx_1024.rearrange("b c d -> c b d"), ld_ctx)
            ld(wkv1s, wkv1.rearrange("(k p) n -> p k n", p=P), ld_w1s)
            ld(wq1s, wq1.rearrange("(k p) n -> p k n", p=P), ld_w1s)
            ld(gates4[:, 0:2], g_xattn.rearrange("(a d) -> a d", a=1).broadcast_to([P, 2]), ld_misc)
            ld(gates4[:, 2:4], g_ffn.rearrange("(a d) -> a d", a=1).broadcast_to([P, 2]), ld_misc)
            ld(ltb, log_temp.rearrange("(a d) -> a d", a=1).broadcast_to([P, 1]), ld_misc)
            ld(gqn[0:E], gate_query, ld_misc)
            ld(b8n[0:FT], b_fc.rearrange("(j p) -> j p", p=P), ld_misc)
            ld(b1n[0:E], b1, ld_misc)
            ld(bpb, b_proj.rearrange("(a d) -> a d", a=1).broadcast_to([P, D]), ld_misc)
            ld(wfn, w_fc.rearrange("(j p) d -> p j d", p=P), ld_ffn)
            ld(wpn, w_proj.rearrange("(j p) d -> p j d", p=P), ld_ffn)
            ld(bfn, bb_fc.rearrange("(j p) r -> p j r", p=P), ld_ffn)
            ld(bpn, bb_proj.rearrange("(j p) r -> p j r", p=P), ld_ffn)
            ld(afc[0:R], a_fc, ld_ffn)
            ld(apj[0:R], a_proj, ld_ffn)
            ld(xs[:, 0:4, :], xv[:, 0:4, :], ld_x)
            ld(maskr, mask.rearrange("(n p) c -> p n c", p=P), ld_x)
            for q in range(1, 4):
                ld(xs[:, 4 * q:4 * q + 4, :], xv[:, 4 * q:4 * q + 4, :], ld_x)

        def run(eng, iteration):
            iteration(eng, 0, first=True, ahead=True, weights=True)
            iteration(eng, 1, first=True, ffn=True, ahead=True)
            iteration(eng, 2, first=True, ffn=True, second=True, ahead=True)
            with eng.Fori(3, B - 1) as i:
                iteration(eng, i, first=True, ffn=True, second=True, tail=True, ahead=True)
            iteration(eng, B - 1, first=True, ffn=True, second=True, tail=True)
            iteration(eng, B, ffn=True, second=True, tail=True)
            iteration(eng, B + 1, second=True, tail=True)
            iteration(eng, B + 2, tail=True)

        def pool_rstd(pool, L, b):
            vpe, y0 = bufs[L][4:6]
            ln_dve[L].wait(pool, b, 5)
            rstd_ready[L].up(pool.tensor_tensor(y0, vpe, mhalf[:, :], ALU.pow))

        def pool_keys(pool, b, halves=range(2)):
            for m in halves:
                kb = k0T[:, m, bass.ds(b * C, C)] if not isinstance(b, int) else k0T[:, m, b * C:b * C + C]
                kbd_ready.up(pool.tensor_tensor(kbd[:, m], kb.unsqueeze(1).broadcast_to([P, 8, C]),
                                                blk8[:, :].unsqueeze(2).broadcast_to([P, 8, C]), ALU.mult))

        def pool_sub(pool, b, s):
            s_max.wait(pool, b, s + 1)
            s_sub.up(pool.tensor_tensor(Tb[:, s % 2], Tb[:, s % 2],
                                        mx[:, s % 2].unsqueeze(2).broadcast_to([P, 4, C]), ALU.subtract))

        def pool_low(pool, b, s):
            es_hi.wait(pool, b, s + 1)
            es_lo.up(pool.tensor_tensor(Es[:, s % 2, 1], Eb[:, s % 2], Es[:, s % 2, 0], ALU.subtract))

        def pool_iteration(pool, i, first=False, ffn=False, second=False, tail=False, ahead=False, weights=False):
            def sub(s):
                if first:
                    pool_sub(pool, i, s)

            def low(s):
                if first:
                    pool_low(pool, i, s)

            if ffn:
                pool_rstd(pool, 1, i - 1)
            low(1)
            sub(2)
            sub(3)
            low(2)
            if tail:
                pool_rstd(pool, 3, i - 3)
            low(3)
            sub(4)
            sub(5)
            low(4)
            if ahead:
                pool_keys(pool, i + 1, [0])
            low(5)
            sub(6)
            if ahead:
                pool_rstd(pool, 0, i + 1)
            low(6)
            sub(7)
            if ahead:
                pool_keys(pool, i + 1, [1])
            low(7)
            if ffn:
                pool_rstd(pool, 2, i - 1)
            if ahead:
                pool_sub(pool, i + 1, 0)
                pool_sub(pool, i + 1, 1)
                pool_low(pool, i + 1, 0)

        def tiles(t, b):
            return t[:, bass.ds(b * NT, NT), :] if not isinstance(b, int) else t[:, b * NT:b * NT + NT, :]

        @block.gpsimd
        def _(pool):
            pool.memset(ident[:, :], 0.0).then_inc(consts_made, 1)
            pool.memset(blk8[:, :], 1.0).then_inc(consts_made, 1)
            pool.memset(blk[:, :], 1.0).then_inc(consts_made, 1)
            pool.iota(iota_i[:, :], [[1, CAP]], base=0, channel_multiplier=0).then_inc(consts_made, 1)
            pool.memset(mhalf[:, :], -0.5).then_inc(consts_made, 1)
            pool.wait_ge(consts_made, 5)
            pool.affine_select(out=ident[:, :], in_=ident[:, :], compare_op=ALU.not_equal, fill=1.0,
                               base=0, pattern=[[-1, P]], channel_multiplier=1).then_inc(consts_made, 1)
            pool.affine_select(out=blk8[:, :], in_=blk8[:, :], compare_op=ALU.is_ge, fill=0.0,
                               base=0, pattern=[[-E, B]], channel_multiplier=1).then_inc(consts_made, 1)
            pool.affine_select(out=blk[:, :], in_=blk[:, :], compare_op=ALU.is_ge, fill=0.0,
                               base=0, pattern=[[-E, B], [0, E]], channel_multiplier=1).then_inc(consts_made, 1)
            pool.tensor_copy(iota_c[:, :], iota_i[:, :]).then_inc(consts_made, 1)
            pool.wait_ge(consts_made, 6)
            pool.tensor_copy(identb[:, :], ident[:, :]).then_inc(consts_made, 1)
            pool.wait_ge(consts_made, 10)
            pool.affine_select(out=blk8[:, :], in_=blk8[:, :], compare_op=ALU.is_ge, fill=0.0,
                               base=E - 1, pattern=[[E, B]], channel_multiplier=-1).then_inc(consts_made, 1)
            pool.affine_select(out=blk[:, :], in_=blk[:, :], compare_op=ALU.is_ge, fill=0.0,
                               base=E - 1, pattern=[[E, B], [0, E]], channel_multiplier=-1).then_inc(consts_made, 1)
            pool.wait_ge(consts_made, CONSTS)
            pool.wait_ge(absmax_ready, 2)
            pool.partition_all_reduce(wsc[:, 0], wmx[:, :], P, bass.bass_isa.ReduceOp.max).then_inc(allmax_ready, 1)
            pool.wait_ge(prep_ev, EV_K0)
            pool_keys(pool, 0)
            pool_rstd(pool, 0, 0)
            pool_sub(pool, 0, 0)
            pool_sub(pool, 0, 1)
            pool_low(pool, 0, 0)
            run(pool, pool_iteration)

        def transpose(pe, dst, src, parts=P):
            return pe.transpose(dst, src, ident[0:parts, 0:parts])

        def psb(n):
            return ps[:, n, :].bitcast(BF16)

        def three(a, b):
            return ((a[0], b[0]), (a[0], b[1]), (a[1], b[0]))

        def pe_transposed(pe, L, b):
            ln_dve[L].wait(pe, b, 7)
            for k in range(KT):
                for n in range(NT):
                    last = transpose(pe, bank(T_BANK[L])[:, k * S + n * P:k * S + n * P + P],
                                     bufs[L][0][:, n, k * P:k * P + P])
            xT_mm[L].up(last)

        def parts(t):
            return t[:, 0], t[:, 1]

        def project(pe, to, w, wcol, xT):
            for m in range(KT):
                for k in range(KT):
                    last = pe.matmul(bank(to)[:, m * S:m * S + S], w[:, k, wcol + m * P:wcol + m * P + P], xT[:, k, :],
                                     start=(k == 0), stop=(k == KT - 1))
            return last

        def col(t, k, b):
            return t[:, k, bass.ds(b * C, C)] if not isinstance(b, int) else t[:, k, b * C:b * C + C]

        def at_batch(t, b):
            return t[:, bass.ds(b, 1)] if not isinstance(b, int) else t[:, b:b + 1]

        def pe_queries(pe, b):
            xT_ready[0].wait(pe, b, 1)
            q_mm.up(project(pe, 0, w0T, 0, buf_a[1]))

        def pe_scores(pe, b, s):
            n, g = s // 4, s % 4
            s_mm.up(pe.matmul(bank(1 + s % 2, 4 * C), qT[:, g // 2, n * P:n * P + P],
                              kbd[:, g // 2, 4 * (g % 2):4 * (g % 2) + 4, :], start=True, stop=True))

        def pe_iteration(pe, i, first=False, ffn=False, second=False, tail=False, ahead=False, weights=False):
            b, p, q, c = i, i - 1, i - 2, i - 3
            xTb, xTd, xTc = buf_b[1], buf_d[1], buf_c[1]

            def weighted(s):
                n, g = s // 4, s % 4
                pT_ready.wait(pe, b, s + 1)
                if s == 4:
                    att_ready.wait(pe, b, 2)
                for h in range(4):
                    hh = 4 * g + h
                    for k, (pp, vp) in enumerate(three(parts(PT[0:C, s % 2]), parts(V0[0:C]))):
                        last = pe.matmul(bank(4)[:, hh * (A + 1):(hh + 1) * (A + 1)], pp[:, h, :],
                                         at_batch(vp, b)[:, :, hh, :].rearrange("p a c -> p (a c)"),
                                         start=(k == 0), stop=(k == 2))
                av_mm.up(last)

            def step(s):
                if not first:
                    return
                es_lo.wait(pe, b, s + 1)
                if s >= 1:
                    pT_ready.wait(pe, b, s)
                for i, part in enumerate(parts(Es[:, s % 2])):
                    for h in range(4):
                        last = pe.transpose(psb(3)[0:C, (4 * i + h) * P:(4 * i + h + 1) * P], part[:, h, :], identb[:, :])
                pT_mm.up(last)
                if s == 0:
                    kbd_ready.wait(pe, b, 2)
                if s + 2 < 8:
                    s_masked.wait(pe, b, s + 1)
                    pe_scores(pe, b, s + 2)
                if s >= 1:
                    weighted(s - 1)
                if weights:
                    pe_weights(pe, s)

            def hidden(j):
                if not ffn:
                    return
                if j == 0:
                    xT_ready[1].wait(pe, p, 1)
                    if isinstance(i, int) and i == 1:
                        pe.wait_ge(wt_ready, 8)
                if j >= 2:
                    h_ready.wait(pe, p, 2 * j - 2)
                for f in (2 * j, 2 * j + 1):
                    for k in range(KT):
                        last = pe.matmul(bank(6 + j % 2)[:, (f % 2) * S:(f % 2) * S + S],
                                         W1T[:, k, f * P:f * P + P], xTb[:, k, :],
                                         start=(k == 0), stop=(k == KT - 1))
                h_mm.up(last)

            def ffn_out(n, fs):
                for f in fs:
                    h_ready.wait(pe, p, f + 1)
                    last = pe.matmul(bank(5)[:, n * D:n * D + D], hT[:, f, n * P:n * P + P], W2T[:, f, :],
                                     start=(f == 0), stop=(f == FT - 1))
                return last

            step(0)
            if second:
                if ffn:
                    x_attn0.wait(pe, p, 1)
                pe_transposed(pe, 2, q)
            step(1)
            if ffn:
                pe_transposed(pe, 1, p)
            if second:
                xT_ready[2].wait(pe, q, 1)
                q1_mm.up(project(pe, 0, wq1s, 0, xTd))
            hidden(0)
            hidden(1)
            step(2)
            if tail:
                if ffn:
                    xT_ready[1].wait(pe, p, 1)
                pe_transposed(pe, 3, c)
            hidden(2)
            if second:
                q1_ready.wait(pe, q, 1)
                for n in range(NT):
                    for k in range(KT):
                        last = pe.matmul(bank(0)[:, n * C:n * C + C], qTb[:, k, n * P:n * P + P], col(k1T, k, q),
                                         start=(k == 0), stop=(k == KT - 1))
                s1_mm.up(last)
            hidden(3)
            step(3)
            if tail:
                xT_ready[3].wait(pe, c, 1)
            if ffn:
                ffn_out(0, range(6))
            if second:
                e1_ready.wait(pe, q, 2)
                for n in range(NT):
                    last = transpose(pe, bank(0)[0:C, n * P:n * P + P], E1[:, n, :])
                p1T_mm.up(last)
            if ffn:
                ffn_out(0, range(6, FT))
            if tail:
                for n in range(NT):
                    for k in range(KT):
                        last = pe.matmul(bank(6)[:, n * E:n * E + E], xTc[:, k, n * P:n * P + P], gqT[:, k, :],
                                         start=(k == 0), stop=(k == KT - 1))
                g_mm.up(last)
            step(4)
            if second:
                p1T_ready.wait(pe, q, 1)
                for n in range(NT):
                    last = pe.matmul(bank(0)[:, n * D:n * D + D], PT1[0:C, n, :],
                                     at_batch(V1, q)[0:C].rearrange("p a d -> p (a d)"), start=True, stop=True)
                av1_mm.up(last)
            if ffn:
                ffn_out(1, range(4))
            step(5)
            if ffn:
                ffn_out(1, range(4, 6))
            if second and first:
                x_attn1.wait(pe, q, 2)
            if ahead:
                pe_transposed(pe, 0, i + 1)
            step(6)
            if ffn:
                f_mm.up(ffn_out(1, range(6, FT)))
            if ahead:
                pe_queries(pe, i + 1)
            step(7)
            if ahead:
                q_ready.wait(pe, i + 1, 1)
                kbd_ready.wait(pe, i + 1, 1)
                s_masked.wait(pe, i, 7)
                pe_scores(pe, i + 1, 0)
            if first:
                weighted(7)
                att_ready.wait(pe, b, 4)
                for k in range(KT):
                    for n in range(NT):
                        last = transpose(pe, bank(0)[:, k * S + n * P:k * S + n * P + P], att[:, n, k * P:k * P + P])
                attT_mm.up(last)
            if ahead:
                s_masked.wait(pe, i, 8)
                pe_scores(pe, i + 1, 1)
            if first:
                attT_ready.wait(pe, b, 1)
                for n in range(NT):
                    for k in range(KT):
                        last = pe.matmul(bank(0)[:, n * D:n * D + D], attT[:, k, n * P:n * P + P], w0T[:, k, 6 * P:8 * P],
                                         start=(k == 0), stop=(k == KT - 1))
                wo_mm.up(last)

        def pe_prep(pe):
            n = [0]

            def group():
                if n[0] >= 8:
                    pe.wait_ge(prep_ev, n[0] - 7)
                n[0] += 1
                return (n[0] - 1) % 8

            def done(last):
                last.then_inc(prep_mm, 1)

            def put(g, c0, src, parts):
                w = src.shape[-1]
                return transpose(pe, bank(g)[0:w, c0:c0 + parts], src, parts)

            pe.wait_ge(consts_made, CONSTS)
            pe.wait_ge(ld_w0, 16 * 3)
            for k in range(KT):
                for jh in range(2):
                    g = group()
                    for j in range(4):
                        last = put(g, j * P, wnat[:, 4 * jh + j, k * P:k * P + P], P)
                    done(last)
            pe.wait_ge(ld_ctx, 16)
            for k in range(KT):
                for bh in range(2):
                    g = group()
                    for j in range(4):
                        last = put(g, j * C, ctxn[0:C, 4 * bh + j, k * P:k * P + P], C)
                    done(last)
            pe.wait_ge(ld_misc, 16 * N_MISC)
            g = group()
            put(g, 0, b8n[0:FT, :], FT)
            for k in range(KT):
                put(g, 16 + k * E, gqn[0:E, k * P:k * P + P], E)
            for j in range(EF):
                last = put(g, 64 + j * E, b1n[0:E, j * P:j * P + P], E)
            done(last)
            pe.wait_ge(prep_ev, 8)
            for m in range(KT):
                for half in range(2):
                    g = group()
                    for k in range(KT):
                        last = pe.matmul(bank(g, 4 * C), w0T[:, k, D + m * P:D + m * P + P],
                                         ctxT[:, k, half * 4 * C:(half + 1) * 4 * C], start=(k == 0), stop=(k == 1))
                    done(last)
            pe.wait_ge(ld_w1s, 16 * 2)
            for m in range(KT):
                for half in range(2):
                    g = group()
                    for k in range(KT):
                        last = pe.matmul(bank(g, 4 * C), wkv1s[:, k, m * P:m * P + P],
                                         ctxT[:, k, half * 4 * C:(half + 1) * 4 * C], start=(k == 0), stop=(k == 1))
                    done(last)
            for b in range(B):
                g = group()
                for c0, w in ((0, w0T[:, :, 2 * D:3 * D]), (D, wkv1s[:, :, D:2 * D])):
                    for k in range(KT):
                        last = pe.matmul(bank(g)[0:C, c0:c0 + D], ctxT[:, k, b * C:b * C + C], w[:, k, :],
                                         start=(k == 0), stop=(k == 1))
                done(last)
            pe.wait_ge(ld_ffn, 16 * N_FFN)
            for half in range(2):
                g = group()
                for j in range(4):
                    last = put(g, j * P, bfn[:, 4 * half + j, :], P)
                done(last)
            g = group()
            for j in range(KT):
                last = put(g, j * P, bpn[:, j, :], P)
            done(last)
        def pe_weights(pe, j):
            g = 5 + j % 3
            if j >= 3:
                pe.wait_ge(wt_ready, j - 2)
            if j < 4:
                pe.wait_ge(fc_quantised, 3)
                k, half = j // 2, j % 2
                for c in range(4):
                    f = 4 * half + c
                    pe.matmul(bank(g)[:, c * P:c * P + P], wfn[:, f, k * P:k * P + P], ident[:, :],
                              start=True, stop=False)
                    last = pe.matmul(bank(g)[:, c * P:c * P + P], afc[0:R, k * P:k * P + P],
                                     bfT[0:R, f * P:f * P + P], start=False, stop=True)
            else:
                pe.wait_ge(proj_quantised, 3)
                for f in range(2):
                    F = slice((2 * (j - 4) + f) * P, (2 * (j - 4) + f + 1) * P)
                    for c in range(KT):
                        c0 = f * D + c * P
                        pe.matmul(bank(g)[:, c0:c0 + P], wpn[:, c, F], ident[:, :], start=True, stop=False)
                        last = pe.matmul(bank(g)[:, c0:c0 + P], apj[0:R, F], bpT[0:R, c * P:c * P + P],
                                         start=False, stop=True)
            last.then_inc(wt_mm, 1)

        @block.tensor
        def _(pe):
            pe_prep(pe)
            pe.wait_ge(prep_ev, PREP)
            pe_transposed(pe, 0, 0)
            pe_queries(pe, 0)
            q_ready.wait(pe, 0, 1)
            kbd_ready.wait(pe, 0, 2)
            pe_scores(pe, 0, 0)
            pe_scores(pe, 0, 1)
            run(pe, pe_iteration)

        def dve_quantise(dve, i, step):
            w, done = (wfn, wpn)[i], (fc_quantised, proj_quantised)[i]
            if step == 0:
                ins = dve.tensor_scalar(w, w, wsc[:, 2, i:i + 1], ROUND, ALU.mult, ALU.add)
            elif step == 1:
                dve.wait_ge(done, 1)
                ins = dve.tensor_scalar(w, w, ROUND, 127.0, ALU.subtract, ALU.min)
            else:
                dve.wait_ge(done, 2)
                ins = dve.tensor_scalar(w, w, -128.0, wsc[:, 1, i:i + 1], ALU.max, ALU.mult)
            ins.then_inc(done, 1)

        def dve_prep(dve):
            n = [0]

            def evac(ins_of, *args):
                dve.wait_ge(prep_mm, n[0] + 1)
                last = ins_of(n[0] % 8)
                last.then_inc(prep_ev, 1)
                n[0] += 1

            dve.memset(V0[:, 0, :, :, A:A + 1], 1.0)
            dve.memset(V0[:, 1, :, :, A:A + 1], 0.0)
            for k in range(KT):
                for jh in range(2):
                    evac(lambda g: dve.tensor_copy(w0T[:, k, jh * 512:jh * 512 + 512], bank(g)))
            for k in range(KT):
                for bh in range(2):
                    evac(lambda g: dve.tensor_copy(ctxT[:, k, bh * 480:bh * 480 + 480], bank(g, 480)))

            def small(g):
                dve.tensor_copy(bfcT[:, :], bank(g)[:, 0:FT])
                dve.tensor_copy(gqT[:, :, :], bank(g)[:, 16:16 + KT * E].rearrange("p (k e) -> p k e", k=KT))
                return dve.tensor_copy(b1T[:, :, :], bank(g)[:, 64:64 + EF * E].rearrange("p (k e) -> p k e", k=EF))

            evac(small)
            for m in range(KT):
                for half in range(2):
                    evac(lambda g: dve.tensor_copy(k0T[:, m, half * 480:half * 480 + 480], bank(g, 480)))

            def absmax(i, w):
                dve.wait_ge(ld_ffn, 16 * N_FFN)
                dve.tensor_reduce(wmx[:, i:i + 1], w, AX.XY, ALU.max, apply_absolute_value=True).then_inc(absmax_ready, 1)

            def step_size():
                dve.wait_ge(allmax_ready, 1)
                dve.tensor_scalar(wsc[:, 1], wsc[:, 0], 1.0 / 127.0, None, ALU.mult).then_inc(quant_step, 1)
                dve.wait_ge(quant_step, 1)
                dve.reciprocal(wsc[:, 2], wsc[:, 1]).then_inc(quant_step, 1)
                dve.wait_ge(quant_step, 2)

            between = {14: lambda: absmax(0, wfn), 16: lambda: absmax(1, wpn), 18: step_size,
                       20: lambda: dve_quantise(dve, 0, 0)}
            for m in range(KT):
                for half in range(2):
                    evac(lambda g: dve.tensor_copy(k1T[:, m, half * 480:half * 480 + 480], bank(g, 480)))
                    between.get(n[0] - 1, lambda: None)()

            def values(g, b):
                dve.wait_ge(prep_hi, 1 + b)
                dve.tensor_tensor(V0[0:C, 1, b, :, 0:A], bank(g)[0:C, 0:D].rearrange("p (h a) -> p h a", h=H),
                                  V0[0:C, 0, b, :, 0:A], ALU.subtract)
                return dve.tensor_copy(V1[0:C, b, :], bank(g)[0:C, D:2 * D])

            dve.wait_ge(ld_x, 16 * N_X)
            dve_stats(dve, 0, 0)
            dve_normed(dve, 0, 0)
            for b in range(B):
                evac(lambda g: values(g, b))
                between.get(n[0] - 1, lambda: None)()
            dve.wait_ge(gate_act, 2)
            dve.tensor_scalar(bpb[:, :], bpb[:, :], gates4[:, 2:3], None, ALU.mult)
            for half in range(2):
                evac(lambda g: dve.tensor_scalar(bfT[0:R, half * 512:half * 512 + 512], bank(g)[0:R, :], 2.0, None, ALU.mult))
            evac(lambda g: dve.tensor_scalar(bpT[0:R, :], bank(g)[0:R, 0:D], 2.0, None, ALU.mult))
            dve_quantise(dve, 0, 1)
            dve_quantise(dve, 0, 2)

        def dve_stats(dve, L, b):
            st, mv, vpe = bufs[L][2:5]
            s = ln_dve[L]
            dve.memset(scratch[:, :], 0.0)
            for n in range(NT):
                s.up(dve.bn_stats(st[:, n, :], tiles(xs, b)[:, n, :]))
            s.wait(dve, b, 2)
            dve.memset(scratch[:, :], 0.0)
            for n in range(NT):
                s.up(dve.bn_aggr(mv[:, n, :], st[:, n, :]))
            s.wait(dve, b, 4)
            s.up(dve.tensor_scalar(vpe, mv[:, :, 1], EPS, None, ALU.add))

        def dve_normed(dve, L, b):
            xn, mv, y0 = bufs[L][0], bufs[L][3], bufs[L][5]
            rstd_ready[L].wait(dve, b, 1)
            for n in range(NT):
                ln_dve[L].up(dve.tensor_scalar(xn[:, n, :], tiles(xs, b)[:, n, :], mv[:, n, 0:1], y0[:, n:n + 1],
                                               ALU.subtract, ALU.mult))

        def dve_split(dve, b):
            xn, hi, lo = buf_c[0], tiles(xh, b), tiles(xl, b)
            ln_dve[3].wait(dve, b, 7)
            xs_ready.up(dve.tensor_copy(hi, xn))
            xs_ready.wait(dve, b, 1)
            xs_ready.up(dve.tensor_tensor(lo, xn, hi, ALU.subtract))

        def dve_high(dve, b, s):
            s_exp.wait(dve, b, s + 1)
            if s >= 2:
                pT_mm.wait(dve, b, s - 1)
            elif not (isinstance(b, int) and b == 0):
                pT_mm.wait(dve, b - 1, 7 + s)
            es_hi.up(dve.tensor_copy(Es[:, s % 2, 0], Eb[:, s % 2]))

        def dve_mask_max(dve, b, s):
            s_mm.wait(dve, b, s + 1)
            if s >= 2:
                s_exp.wait(dve, b, s - 1)
            elif not (isinstance(b, int) and b == 0):
                s_exp.wait(dve, b - 1, 7 + s)
            s_masked.up(dve.tensor_tensor(
                Tb[:, s % 2], bank(1 + s % 2, 4 * C).rearrange("p (h c) -> p h c", h=4),
                maskr[:, s // 4, :].unsqueeze(1).broadcast_to([P, 4, C]), ALU.add))
            s_masked.wait(dve, b, s + 1)
            s_max.up(dve.tensor_reduce(mx[:, s % 2], Tb[:, s % 2], AX.X, ALU.max))

        def dve_iteration(dve, i, first=False, ffn=False, second=False, tail=False, ahead=False, weights=False):
            b, p, q, c = i, i - 1, i - 2, i - 3

            def mask_max(s):
                if first:
                    dve_mask_max(dve, b, s)

            def normalise(n):
                if not first:
                    return
                av_mm.wait(dve, b, 4 * n + 4)
                o = bank(4)[:, 0:H * (A + 1)].rearrange("p (h a) -> p h a", h=H)
                att_ready.up(dve.reciprocal(rden[:, :], o[:, :, A]))
                att_ready.wait(dve, b, 2 * n + 1)
                att_ready.up(dve.tensor_tensor(att[:, n, :].rearrange("p (h a) -> p h a", h=H), o[:, :, 0:A],
                                               rden[:, :].unsqueeze(2).broadcast_to([P, H, A]), ALU.mult))

            def high(s):
                if first:
                    dve_high(dve, b, s)

            if ffn:
                dve_stats(dve, 1, p)
            high(1)
            if ffn:
                dve_normed(dve, 1, p)
            mask_max(2)
            if weights:
                dve_quantise(dve, 1, 0)
            high(2)
            mask_max(3)
            if tail:
                dve_stats(dve, 3, c)
            high(3)
            if tail:
                dve_normed(dve, 3, c)
            if weights:
                dve_quantise(dve, 1, 1)
            mask_max(4)
            if weights:
                dve_quantise(dve, 1, 2)
            if tail:
                dve_split(dve, c)
            if second:
                s1_mm.wait(dve, q, 1)
                m1_ready.up(dve.tensor_reduce(nm1[:, :], bank(0)[:, 0:NT * C].rearrange("p (n c) -> p n c", n=NT),
                                              AX.X, ALU.max))
                m1_ready.wait(dve, q, 1)
                m1_ready.up(dve.tensor_scalar(nm1[:, :], nm1[:, :], -ISQ, None, ALU.mult))
            mask_max(5)
            high(4)
            if second:
                e1_ready.wait(dve, q, 2)
                r1_ready.up(dve.reciprocal(ri1[:, :], sm1[:, :]))
                r1_ready.wait(dve, q, 1)
                r1_ready.up(dve.tensor_scalar(ri1[:, :], ri1[:, :], gates4[:, 1:2], None, ALU.mult))
            high(5)
            if tail:
                g_mm.wait(dve, c, 1)
                tl = tlog[:, :, bass.ds(c, 1), :] if not isinstance(c, int) else tlog[:, :, c:c + 1, :]
                t_ready.up(dve.tensor_scalar(tl.rearrange("p n a e -> p n (a e)"),
                                             bank(6)[:, 0:NT * E].rearrange("p (n e) -> p n e", n=NT),
                                             ltb[:, 0:1], None, ALU.mult))
            mask_max(6)
            if second:
                xq = tiles(xs, q)
                r1_ready.wait(dve, q, 2)
                av1_mm.wait(dve, q, 1)
                for n in range(NT):
                    x_attn1.up(dve.scalar_tensor_tensor(
                        out=xq[:, n, :], in0=bank(0)[:, n * D:n * D + D], scalar=ri1[:, n:n + 1], in1=xq[:, n, :],
                        op0=ALU.mult, op1=ALU.add))
            if ahead:
                dve_stats(dve, 0, i + 1)
            normalise(0)
            high(6)
            if ahead:
                dve_normed(dve, 0, i + 1)
            mask_max(7)
            high(7)
            if second:
                x_attn1.wait(dve, q, 2)
            if ffn:
                xp = tiles(xs, p)
                f_mm.wait(dve, p, 1)
                x_ffn0.up(dve.scalar_tensor_tensor(out=xp, in0=bank(5).rearrange("p (n d) -> p n d", n=NT),
                                                   scalar=gates4[:, 2:3], in1=xp, op0=ALU.mult, op1=ALU.add))
                x_ffn0.wait(dve, p, 1)
                x_ffn0.up(dve.tensor_tensor(xp, xp, bpb[:, :].unsqueeze(1).broadcast_to([P, NT, D]), ALU.add))
                x_ffn0.wait(dve, p, 2)
                dve_stats(dve, 2, p)
                dve_normed(dve, 2, p)
            normalise(1)
            if ahead:
                dve_mask_max(dve, i + 1, 0)
                dve_mask_max(dve, i + 1, 1)
                dve_high(dve, i + 1, 0)
            if first:
                xb = tiles(xs, b)
                wo_mm.wait(dve, b, 1)
                x_attn0.up(dve.scalar_tensor_tensor(out=xb, in0=bank(0).rearrange("p (n d) -> p n d", n=NT),
                                                    scalar=gates4[:, 0:1], in1=xb, op0=ALU.mult, op1=ALU.add))
                x_attn0.wait(dve, b, 1)

        @block.vector
        def _(dve):
            dve_prep(dve)
            dve_mask_max(dve, 0, 0)
            dve_mask_max(dve, 0, 1)
            dve_high(dve, 0, 0)
            run(dve, dve_iteration)

        def copy_512(act, dst, src):
            return act.activation(dst.rearrange("p k s -> p (k s)"), bank(src), ACT.Copy)

        def act_xT(act, L, b):
            xT_mm[L].wait(act, b, 1)
            xT_ready[L].up(copy_512(act, bufs[L][1], T_BANK[L]))

        def act_queries(act, b):
            q_mm.wait(act, b, 1)
            q_ready.up(copy_512(act, qT, 0))

        def act_exp(act, b, s):
            s_sub.wait(act, b, s + 1)
            if s >= 2:
                es_lo.wait(act, b, s - 1)
            elif not (isinstance(b, int) and b == 0):
                es_lo.wait(act, b - 1, 7 + s)
            s_exp.up(act.activation(Eb[:, s % 2], Tb[:, s % 2], ACT.Exp, scale=ISQ))

        def act_iteration(act, i, first=False, ffn=False, second=False, tail=False, ahead=False, weights=False):
            b, p, q, c = i, i - 1, i - 2, i - 3

            def transposed(s):
                if not first:
                    return
                pT_mm.wait(act, b, s + 1)
                if s >= 2:
                    av_mm.wait(act, b, s - 1)
                pT_ready.up(act.activation(PT[0:C, s % 2].rearrange("p i h q -> p (i h q)"), psb(3)[0:C], ACT.Copy))
                if weights:
                    dst = W1T[:, s // 2, s % 2 * 512:s % 2 * 512 + 512] if s < 4 else \
                        W2T[:, 2 * (s - 4):2 * (s - 4) + 2, :].rearrange("p f d -> p (f d)")
                    act.wait_ge(wt_mm, s + 1)
                    act.activation(dst, bank(5 + s % 3), ACT.Copy).then_inc(wt_ready, 1)

            def exps(s):
                if first:
                    act_exp(act, b, s)

            def gelus(fs):
                if not ffn:
                    return
                for f in fs:
                    j = f // 2
                    h_mm.wait(act, p, j + 1)
                    h_ready.up(act.activation(hT[:, f, :], bank(6 + j % 2)[:, (f % 2) * S:(f % 2) * S + S],
                                              ACT.Gelu, bias=bfcT[:, f:f + 1]))

            exps(1)
            transposed(0)
            if second:
                act_xT(act, 2, q)
            exps(2)
            if ffn:
                act_xT(act, 1, p)
            transposed(1)
            exps(3)
            if second:
                q1_mm.wait(act, q, 1)
                q1_ready.up(copy_512(act, qTb, 0))
            gelus(range(4))
            transposed(2)
            gelus(range(4, 6))
            if tail:
                act_xT(act, 3, c)
            gelus(range(6, 8))
            if second:
                m1_ready.wait(act, q, 2)
                for n in range(NT):
                    e1_ready.up(act.activation(E1[:, n, :], bank(0)[:, n * C:n * C + C], ACT.Exp,
                                               bias=nm1[:, n:n + 1], scale=ISQ, accum_out=sm1[:, n:n + 1]))
            exps(4)
            transposed(3)
            if second:
                p1T_mm.wait(act, q, 1)
                p1T_ready.up(act.activation(PT1[0:C, :, :],
                                            bank(0)[0:C, 0:NT * P].rearrange("p (n q) -> p n q", n=NT), ACT.Copy))
            exps(5)
            transposed(4)
            exps(6)
            transposed(5)
            if ahead:
                act_xT(act, 0, i + 1)
            exps(7)
            transposed(6)
            if ahead:
                act_queries(act, i + 1)
            transposed(7)
            if first:
                attT_mm.wait(act, b, 1)
                attT_ready.up(act.activation(attT, bank(0).rearrange("p (k s) -> p k s", k=KT), ACT.Copy))
            if ahead:
                act_exp(act, i + 1, 0)

        @block.scalar
        def _(act):
            act.wait_ge(ld_misc, 16 * N_MISC)
            act.activation(gates4[:, :], gates4[:, :], ACT.Tanh).then_inc(gate_act, 1)
            act.activation(ltb[:, :], ltb[:, :], ACT.Exp, scale=-1.0).then_inc(gate_act, 1)
            for b in range(B):
                act.wait_ge(prep_mm, 18 + b)
                act.activation(V0[0:C, 0, b, :, 0:A], bank((17 + b) % 8)[0:C, 0:D].rearrange("p (h a) -> p h a", h=H),
                               ACT.Copy).then_inc(prep_hi, 1)
            act_xT(act, 0, 0)
            act_queries(act, 0)
            act_exp(act, 0, 0)
            run(act, act_iteration)

        def act_prepare(act, e, par, piece):
            if piece == 0:
                ld_w1.wait(act, e, 16)
            if piece == 2:
                ld_w2.wait(act, e, 16)
            if piece < 2:
                w1h_ready.up(act.activation(w1h[:, par, piece], w1r[:, piece], ACT.Copy))
            else:
                p = piece - 2
                w2h_ready.up(act.activation(w2h[:, par, 4 * p:4 * p + 4], w2r[:, 4 * p:4 * p + 4], ACT.Copy))

        def nb(t):
            return t.rearrange("p (g e) -> p g e", e=E)

        @block.vector
        def _(dve):
            T0 = tlog[:, :, :, :].rearrange("p n b e -> p (n b) e")
            TN = tn.rearrange("p n (b e) -> p (n b) e", e=E)
            EX = ex.rearrange("p n (b e) -> p (n b) e", e=E)

            def step(ins):
                route_dve.n += 1
                ins.then_inc(route_dve.sem, 1)
                dve.wait_ge(route_dve.sem, route_dve.n)

            def bc(v, k=E):
                return v.unsqueeze(2).broadcast_to([P, NT * B, k])

            dve.wait_ge(t_ready.sem, B)
            step(dve.tensor_reduce(mxe[:, :], T0, AX.X, ALU.max))
            step(dve.tensor_tensor(TN, T0, bc(mxe), ALU.subtract))
            dve.wait_ge(route_act, 1)
            step(dve.tensor_reduce(ls[:, :], EX, AX.X, ALU.add))
            dve.wait_ge(route_act, 2)
            step(dve.tensor_tensor(TN, TN, bc(ls), ALU.subtract))
            dve.wait_ge(route_pe, 1)
            step(dve.tensor_reduce(rm[:, 0:1], bank(0)[:, 0:S], AX.X, ALU.max))
            step(dve.tensor_scalar(rm[:, 1:2], rm[:, 0:1], -1.0, None, ALU.mult))
            dve.wait_ge(route_act, 3)
            step(dve.reciprocal(rm[:, 3:4], rm[:, 2:3]))
            step(dve.tensor_scalar(Bd[:, :], blk8[:, :], rm[:, 3:4], None, ALU.mult))
            for it in range(SINK - 2):
                dve.wait_ge(route_pe, 3 + 2 * it)
                step(dve.reciprocal(ra[:, :], bank(1)[:, 0:NT * B]))
                dve.wait_ge(route_pe, 4 + 2 * it)
                step(dve.tensor_tensor_reduce(out=vt[:, :], in0=bank(2)[:, 0:B], in1=blk8[:, :], scale=1.0,
                                              scalar=0.0, op0=ALU.mult, op1=ALU.add, accum_out=rm[:, 2:3]))
                step(dve.reciprocal(rm[:, 3:4], rm[:, 2:3]))
                step(dve.tensor_scalar(Bd[:, :], blk8[:, :], rm[:, 3:4], None, ALU.mult))
            step(dve.tensor_scalar(blkB[:, :], blk[:, :], rm[:, 3:4], None, ALU.mult))
            dve.wait_ge(route_act, 5)
            step(dve.tensor_tensor(t6[:, :], bank(0)[:, 0:S], lnU[:, :], ALU.subtract))
            dve.wait_ge(route_act, 6)
            step(dve.reciprocal(rm[:, 5:6], rm[:, 4:5]))
            step(dve.tensor_scalar(aff[:, :], aff[:, :], rm[:, 5:6], None, ALU.mult))
            src = aff
            for _ in range(CAP // 8):
                step(dve.max(m8[:, :], src[:, :]))
                step(dve.match_replace(out=wk[:, :], in_to_replace=m8[:, :], in_values=src[:, :], imm_value=-1.0))
                src = wk
            step(dve.tensor_scalar(wk[:, :], wk[:, :], 0.0, None, ALU.is_lt))
            step(dve.memset(lnU[:, :], 1.0))
            step(dve.tensor_tensor_scan(posn[:, :], lnU[:, :], wk[:, :], 0.0, ALU.mult, ALU.add))
            step(dve.tensor_tensor(posn[:, :], posn[:, :], wk[:, :], ALU.mult))
            dve.wait_ge(route_pe, 3 + 2 * (SINK - 2) + 1)
            pv = posB[:, :, :, :].rearrange("p n b e -> p n (b e)")
            step(dve.tensor_scalar(pv, bank(1)[:, 0:S].rearrange("p (n j) -> p n j", n=NT), 1.0, None, ALU.subtract))
            A3 = [affp[:, :, i].rearrange("p n b e -> p n (b e)") for i in range(3)]
            AB = bank(2)[:, 0:S].rearrange("p (n j) -> p n j", n=NT)
            step(dve.tensor_copy(A3[0], AB))
            step(dve.tensor_tensor(tn, AB, A3[0], ALU.subtract))
            step(dve.tensor_copy(A3[1], tn))
            step(dve.tensor_tensor(A3[2], tn, A3[1], ALU.subtract))
            assert route_dve.n == ROUTED

        @block.scalar
        def _(act):
            act.wait_ge(route_dve.sem, 2)
            act.activation(ex.rearrange("p n j -> p (n j)"), tn.rearrange("p n j -> p (n j)"), ACT.Exp).then_inc(route_act, 1)
            act.wait_ge(route_dve.sem, 3)
            act.activation(ls[:, :], ls[:, :], ACT.Ln).then_inc(route_act, 1)
            act.wait_ge(route_dve.sem, 6)
            act.activation(KA[:, :], bank(0)[:, 0:S], ACT.Exp, bias=rm[:, 1:2], accum_out=rm[:, 2:3]).then_inc(route_act, 1)
            act.wait_ge(route_pe, 2)
            act.activation(KB.rearrange("p n j -> p (n j)"), bank(3)[:, 0:S], ACT.Copy).then_inc(route_act, 1)
            for piece in range(4):
                act_prepare(act, 0, 0, piece)
            act.wait_ge(route_pe, 3 + 2 * (SINK - 2))
            act.activation(lnU[:, :], bank(4)[:, 0:S], ACT.Ln).then_inc(route_act, 1)
            act.wait_ge(route_dve.sem, 26)
            act.activation(aff[:, :], t6[:, :], ACT.Exp, bias=rm[:, 1:2], accum_out=rm[:, 4:5]).then_inc(route_act, 1)

        @block.tensor
        def _(pe):
            pe.wait_ge(route_dve.sem, 4)
            for n in range(NT):
                last = transpose(pe, bank(0)[:, n * P:n * P + P], tn[:, n, :])
            last.then_inc(route_pe, 1)
            pe.wait_ge(route_act, 3)
            for n in range(NT):
                last = transpose(pe, bank(3)[:, n * P:n * P + P], KA[:, n * P:n * P + P])
            last.then_inc(route_pe, 1)
            for it in range(SINK - 2):
                pe.wait_ge(route_dve.sem, 8 + 4 * it)
                for n in range(NT):
                    last = pe.matmul(bank(1)[:, n * B:n * B + B], KA[:, n * P:n * P + P], Bd[:, :], start=True, stop=True)
                last.then_inc(route_pe, 1)
                if it == 0:
                    pe.wait_ge(route_act, 4)
                pe.wait_ge(route_dve.sem, 9 + 4 * it)
                for n in range(NT):
                    last = pe.matmul(bank(2)[:, 0:B], KB[:, n, :], ra[:, n * B:n * B + B], start=(n == 0), stop=(n == NT - 1))
                last.then_inc(route_pe, 1)
            pe.wait_ge(route_dve.sem, 25)
            pe.matmul(bank(4)[:, 0:S], blkB[:, :], KA[:, :], start=True, stop=True).then_inc(route_pe, 1)
            pe.wait_ge(route_dve.sem, 48)
            for k, t in ((1, posn), (2, aff)):
                for n in range(NT):
                    last = transpose(pe, bank(k)[:, n * P:n * P + P], t[:, n * P:n * P + P])
            last.then_inc(route_pe, 1)

        def one(t, i, n=1):
            return bass.ds(i, n) if not isinstance(i, int) else slice(i, i + n)

        HB = (0, 1, 7)
        w1_dram = w1.rearrange("e (k p) f -> p e k f", p=P)
        w2_dram = w2.rearrange("e (f p) d -> p e f d", p=P)

        @block.sync
        def _(sp):
            def load(e, par):
                if not (isinstance(e, int) and e == 0):
                    w1h_ready.wait(sp, e - 1, 2)
                    w1l_ready.wait(sp, e - 1, 2)
                sp.dma_start(w1r, w1_dram[:, one(w1, e)].rearrange("p a k f -> p (a k) f")).then_inc(ld_w1.sem, 16)
                if not (isinstance(e, int) and e == 0):
                    w2h_ready.wait(sp, e - 1, 2)
                    w2l_ready.wait(sp, e - 1, 2)
                sp.dma_start(w2r, w2_dram[:, one(w2, e)].rearrange("p a f d -> p (a f) d")).then_inc(ld_w2.sem, 16)
                if not (isinstance(e, int) and e < 2):
                    y_t.wait(sp, e - 2, 2)
                sp.dma_start(b2b[:, par], b2[one(b2, e)].broadcast_to([P, D])).then_inc(ld_b2.sem, 16)

            load(0, 0)
            load(1, 1)
            with sp.Fori(1, E // 2) as j:
                load(2 * j, 0)
                load(2 * j + 1, 1)
            with sp.Fori(0, B) as b:
                out_ready.wait(sp, b, 1)
                sp.dma_start(out.rearrange("b (n p) d -> p b n d", p=P)[:, one(out, b)].rearrange("p a n d -> p (a n) d"),
                             tiles(xs, b)).then_inc(stored, 16)
            sp.wait_ge(stored, 16 * B)

        @block.gpsimd
        def _(pool):
            def prepare(e, par):
                for k in range(KT):
                    w1h_ready.wait(pool, e, k + 1)
                    w1l_ready.up(pool.tensor_tensor(w1l[:, par, k], w1r[:, k], w1h[:, par, k], ALU.subtract))
                for p in range(2):
                    w2h_ready.wait(pool, e, p + 1)
                    w2l_ready.up(pool.tensor_tensor(w2l[:, par, 4 * p:4 * p + 4], w2r[:, 4 * p:4 * p + 4],
                                                    w2h[:, par, 4 * p:4 * p + 4], ALU.subtract))

            def outputs(e, par, pair):
                q = slice(64 * par, 64 * par + 64)
                if not (isinstance(e, int) and e == E - 1):
                    w2l_ready.wait(pool, e + 1, 2)
                for pr in range(2):
                    yh_ready.wait(pool, e, pr + 1)
                    yl_ready.up(pool.tensor_tensor(
                        YL[q, one(YL, pair), 4 * pr:4 * pr + 4, :].rearrange("p a b d -> p (a b) d"), yg[q, pr],
                        YH[q, one(YH, pair), 4 * pr:4 * pr + 4, :].rearrange("p a b d -> p (a b) d"), ALU.subtract))
                yl_ready.wait(pool, e, 2)

            prepare(0, 0)
            with pool.Fori(0, E // 2 - 1) as j:
                prepare(2 * j + 1, 1)
                outputs(2 * j, 0, j)
                prepare(2 * j + 2, 0)
                outputs(2 * j + 1, 1, j)
            prepare(E - 1, 1)
            outputs(E - 2, 0, E // 2 - 1)
            outputs(E - 1, 1, E // 2 - 1)

        @block.tensor
        def _(pe):
            def places(b, par):
                for n in range(NT):
                    gs_ready.wait(pe, b, n + 1)
                    for r in range(E // 2):
                        last = pe.transpose(psb(2 - 2 * par + n)[:, r * P:r * P + P],
                                            Gs[:, par, n, 2 * r:2 * r + 2, :].rearrange("p e c -> p (e c)"), identb[:, :])
                    gst_mm.up(last)

            def gather(e, par):
                def rows(k, src, to):
                    for b in range(B):
                        for n in range(NT):
                            last = pe.matmul(bank(to)[:, b * CAP:(b + 1) * CAP],
                                             src[:, b * NT + n, k * P:k * P + P], G[:, par, n * B + b, :],
                                             start=(n == 0), stop=(n == NT - 1))
                    g_mm2.up(last)

                g_ready.wait(pe, e, 1)
                rows(0, xh, 2)
                rows(0, xl, 3)
                if not (isinstance(e, int) and e == 0):
                    gelu_ready.wait(pe, e - 1, EF - 2)
                rows(1, xh, 7)
                if not (isinstance(e, int) and e == 0):
                    gt_ready.wait(pe, e - 1, 2)
                for t in range(4):
                    for n in range(NT):
                        last = pe.matmul(bank(6)[:, t * 8:t * 8 + 6],
                                         G[:, par, n * B + 2 * t:n * B + 2 * t + 2, :].rearrange("p b c -> p (b c)"),
                                         affp[:, n, :, 2 * t:2 * t + 2, one(affp, e)].rearrange("p i b a -> p i (b a)"),
                                         start=(n == 0), stop=(n == NT - 1))
                g_mm2.up(last)
                xgh_ready.wait(pe, e, 1)
                rows(1, xl, 2)

            def expert(e, par, ahead, pair=0):
                xgh_ready.wait(pe, e, 2)
                xgl_ready.wait(pe, e, 2)
                w1h_ready.wait(pe, e, 2)
                w1l_ready.wait(pe, e, 2)
                for f in range(EF):
                    if f >= 3:
                        gelu_ready.wait(pe, e, f - 2)
                    first = True
                    for wp, xp in ((w1h, xgh), (w1h, xgl), (w1l, xgh)):
                        for k in range(KT):
                            last = pe.matmul(bank(HB[f % 3]), wp[:, par, k, f * P:f * P + P], xp[:, par, k, :],
                                             start=first, stop=(wp is w1l and k == KT - 1))
                            first = False
                    m1_mm.up(last)
                if ahead:
                    gather(e + 1, 1 - par)
                else:
                    places(0, 0)
                hl_ready.wait(pe, e, EF)
                w2h_ready.wait(pe, e, 2)
                w2l_ready.wait(pe, e, 2)
                for t in range(4):
                    if t % 2 == 0 and not (isinstance(e, int) and e == 0):
                        y_t.wait(pe, e - 1, t // 2 + 1)
                    for f in range(EF):
                        for hp, wp in ((hh, w2h), (hh, w2l), (hl, w2h)):
                            last = pe.matmul(bank(4 + t // 2)[:, (t % 2) * D:(t % 2) * D + D],
                                             hp[:, f, t * P:t * P + P], wp[:, par, f, :],
                                             start=(f == 0 and wp is w2h and hp is hh),
                                             stop=(f == EF - 1 and hp is hl))
                    if t % 2:
                        m2_mm.up(last)

            gather(0, 0)
            expert(0, 0, True)
            with pe.Fori(0, E // 2 - 1) as j:
                expert(2 * j + 1, 1, True, j)
                expert(2 * j + 2, 0, True, j + 1)
            expert(E - 1, 1, False, E // 2 - 1)

            def combine(b, par):
                if not (isinstance(b, int) and b < 2):
                    out_ready.wait(pe, b - 2, 1)
                for n in range(NT):
                    (gt2_act, gt2_dve)[n].wait(pe, b, 1)
                    for r in range(E // 2):
                        for Y in (YH, YL):
                            last = pe.matmul(bank(4 + par)[:, n * D:n * D + D], GT[:, par, n, r, :],
                                             Y[:, r, one(Y, b), :].rearrange("p a d -> p (a d)"),
                                             start=(r == 0 and Y is YH), stop=(r == E // 2 - 1 and Y is YL))
                c_mm.up(last)

            yl_ready.wait(pe, E - 1, 2)
            places(1, 1)
            combine(0, 0)
            places(2, 0)
            combine(1, 1)
            with pe.Fori(1, B // 2 - 1) as j:
                places(2 * j + 1, 1)
                combine(2 * j, 0)
                places(2 * j + 2, 0)
                combine(2 * j + 1, 1)
            places(B - 1, 1)
            combine(B - 2, 0)
            combine(B - 1, 1)

        @block.vector
        def _(dve):
            def onehot(e, par):
                if not (isinstance(e, int) and e < 2):
                    g_mm2.wait(dve, e - 2, 5)
                g_ready.up(dve.tensor_tensor(
                    G[:, par], posB[:, :, :, one(posB, e)].rearrange("p n b a -> p (n b) a").broadcast_to([P, NT * B, CAP]),
                    iota_c[:, :].unsqueeze(1).broadcast_to([P, NT * B, CAP]), ALU.is_equal))

            def onehots_of_batch(b, par):
                for n in range(NT):
                    gs_ready.up(dve.tensor_tensor(
                        Gs[:, par, n], posB[:, n, one(posB, b)].rearrange("p a e -> p (a e)").unsqueeze(2).broadcast_to([P, E, CAP]),
                        iota_c[:, :].unsqueeze(1).broadcast_to([P, E, CAP]), ALU.is_equal))

            def gathered(e, par):
                g_mm2.wait(dve, e, 2)
                xgl_ready.up(dve.tensor_copy(xgl[:, par, 0, :], bank(3)))
                g_mm2.wait(dve, e, 4)
                gv = bank(6)[:, 0:32].rearrange("p (t i b) -> p t i b", t=4, b=2)
                for half in range(2):
                    q = slice(64 * half, 64 * half + 64)
                    gt_ready.up(dve.tensor_reduce(gt[q, par, :], gv[q, :, 0:3, half], AX.X, ALU.add))
                g_mm2.wait(dve, e, 5)
                xgl_ready.up(dve.tensor_copy(xgl[:, par, 1, :], bank(2)))

            def expert(e, par, ahead, pair=0):
                for f in range(EF):
                    gelu_ready.wait(dve, e, f + 1)
                    hh_ready.up(dve.tensor_copy(hh[:, f, :], hf[:, f % 3, :]))
                    hh_ready.wait(dve, e, f + 1)
                    hl_ready.up(dve.tensor_tensor(hl[:, f, :], hf[:, f % 3, :], hh[:, f, :], ALU.subtract))
                    if ahead and f == 0:
                        onehot(e + 1, 1 - par)
                if ahead:
                    gathered(e + 1, 1 - par)
                else:
                    w1l_ready.wait(dve, e, 2)
                    onehots_of_batch(0, 0)
                    onehots_of_batch(1, 1)
                ld_b2.wait(dve, e, 16)
                for pr in range(2):
                    m2_mm.wait(dve, e, pr + 1)
                    y_t.up(dve.tensor_tensor(yt[:, pr], bank(4 + pr).rearrange("p (t d) -> p t d", t=2),
                                             b2b[:, par].unsqueeze(1).broadcast_to([P, 2, D]), ALU.add))
                    yg_ready.wait(dve, e, 4 * pr + 4)
                    q = slice(64 * par, 64 * par + 64)
                    yh_ready.up(dve.tensor_scalar(
                        YH[q, one(YH, pair), 4 * pr:4 * pr + 4, :].rearrange("p a b d -> p (a b) d"), yg[q, pr],
                        1.0, None, ALU.mult))

            onehot(0, 0)
            gathered(0, 0)
            expert(0, 0, True)
            with dve.Fori(0, E // 2 - 1) as j:
                expert(2 * j + 1, 1, True, j)
                expert(2 * j + 2, 0, True, j + 1)
            expert(E - 1, 1, False, E // 2 - 1)

            def transposed(b, par):
                gst_mm.wait(dve, b, 2)
                gt2_dve.up(dve.tensor_copy(GT[:, par, 1].rearrange("p r q -> p (r q)"), psb(3 - 2 * par)))

            def finish(b, par):
                c_mm.wait(dve, b, 1)
                xb = tiles(xs, b)
                out_ready.up(dve.scalar_tensor_tensor(
                    out=xb, in0=bank(4 + par).rearrange("p (n d) -> p n d", n=NT), scalar=gates4[:, 3:4], in1=xb,
                    op0=ALU.mult, op1=ALU.add))

            transposed(0, 0)
            with dve.Fori(0, B // 2 - 1) as j:
                transposed(2 * j + 1, 1)
                onehots_of_batch(2 * j + 2, 0)
                finish(2 * j, 0)
                transposed(2 * j + 2, 0)
                onehots_of_batch(2 * j + 3, 1)
                finish(2 * j + 1, 1)
            transposed(B - 1, 1)
            finish(B - 2, 0)
            finish(B - 1, 1)

        @block.scalar
        def _(act):
            def gathered(e, par):
                for k, src in ((0, 2), (1, 7)):
                    g_mm2.wait(act, e, 2 * k + 1)
                    xgh_ready.up(act.activation(xgh[:, par, k, :], bank(src), ACT.Copy))

            def expert(e, par, ahead, pair=0):
                for f in range(EF):
                    m1_mm.wait(act, e, f + 1)
                    if f >= 3:
                        hl_ready.wait(act, e, f - 2)
                    gelu_ready.up(act.activation(hf[:, f % 3, :], bank(HB[f % 3]), ACT.Gelu_apprx_tanh,
                                                 bias=b1T[:, f, one(b1T, e)]))
                    if ahead and f % 2 == 0:
                        act_prepare(act, e + 1, 1 - par, f // 2)
                if ahead:
                    gathered(e + 1, 1 - par)
                for pr in range(2):
                    y_t.wait(act, e, pr + 1)
                    if not (isinstance(e, int) and e == 0):
                        yl_ready.wait(act, e - 1, pr + 1)
                    for i in range(4):
                        t, half = 2 * pr + i // 2, i % 2
                        q, o = slice(64 * half, 64 * half + 64), slice(64 * par, 64 * par + 64)
                        yg_ready.up(act.activation(yg[o, pr, i, :], yt[q, pr, i // 2, :], ACT.Copy,
                                                   scale=gt[q, par, t:t + 1]))

            gathered(0, 0)
            expert(0, 0, True)
            with act.Fori(0, E // 2 - 1) as j:
                expert(2 * j + 1, 1, True, j)
                expert(2 * j + 2, 0, True, j + 1)
            expert(E - 1, 1, False, E // 2 - 1)
            def places(b, par):
                gst_mm.wait(act, b, 1)
                if not (isinstance(b, int) and b < 2):
                    c_mm.wait(act, b - 2, 1)
                gt2_act.up(act.activation(GT[:, par, 0].rearrange("p r q -> p (r q)"), psb(2 - 2 * par), ACT.Copy))

            for b in range(3):
                places(b, b % 2)
            with act.Fori(1, B // 2 - 1) as j:
                places(2 * j + 1, 1)
                places(2 * j + 2, 0)
            places(B - 1, 1)


_INS = ["x", "ctx_1024", "mask_SxS2_fk0", "g_xattn", "g_ffn", "L0_xattn_Wq", "L0_xattn_Wkv", "L0_xattn_Wout",
        "L0_ffn_W_fc", "L0_ffn_b_fc", "L0_ffn_A_fc", "L0_ffn_B_fc", "L0_ffn_W_proj", "L0_ffn_b_proj",
        "L0_ffn_A_proj", "L0_ffn_B_proj", "L1_xattn_Wq", "L1_xattn_Wkv", "L1_ffn_gate_query", "L1_ffn_log_temp",
        "L1_ffn_w1", "L1_ffn_b1", "L1_ffn_w2", "L1_ffn_b2"]


def kernel(**inputs):
    import numpy as np
    import concourse.bacc as bacc
    from concourse.bass_utils import run_bass_kernel_spmd

    nc = bacc.Bacc("TRN2", target_bir_lowering=False, num_devices=1)
    arrays, args = {}, []
    for name in _INS:
        a = np.ascontiguousarray(inputs[name])
        a = a.reshape(a.shape or (1,))
        arrays[f"in_{name}"] = a
        args.append(nc.dram_tensor(f"in_{name}", a.shape, mybir.dt.from_np(a.dtype), kind="ExternalInput").ap())
    shape = inputs["x"].shape
    args.append(nc.dram_tensor("out_0", shape, F32, kind="ExternalOutput").ap())
    build(nc, *args)
    r = run_bass_kernel_spmd(nc, [arrays], core_ids=[0])
    return r.results[0]["out_0"]
```
